# Optimizing a Trainium2 kernel written in Bass

```python
import numpy as np
import jax
import jax.numpy as jnp

def _softmax(x, axis=-1):
    return jax.nn.softmax(x, axis=axis)

def _gelu(x):
    return jax.nn.gelu(x, approximate=True)

def _silu(x):
    return jax.nn.silu(x)

def _sigmoid(x):
    return jax.nn.sigmoid(x)

def _layernorm(x, axis=-1, eps=1e-05):
    m = jnp.mean(x, axis=axis, keepdims=True)
    v = jnp.var(x, axis=axis, keepdims=True)
    return (x - m) / jnp.sqrt(v + eps)

def _scatter_add(tgt, idx, src, axis=0):
    return tgt.at[idx].add(src)

def _segment_sum(src, seg, n):
    return jax.ops.segment_sum(src, seg, n)
kernel_name = 'mk_prb_d4_jaxref_r8_eeb7b3'

def setup_inputs(seed: int=0):
    np.random.seed(seed)
    _w = jnp.asarray

    def _L0_attn_setup():
        import jax, jax.numpy as jnp
        import numpy as np
        D_MODEL = 128
        KERNEL_SIZE = 128
        ORDER = 2
        B, T = (4, 256)

        def _layernorm(x, gamma, beta, eps=1e-05):
            mu = jnp.mean(x, axis=-1, keepdims=True)
            var = jnp.mean(jnp.square(x - mu), axis=-1, keepdims=True)
            return (x - mu) * jax.lax.rsqrt(var + eps) * gamma + beta

        def _fft_conv(y_bdt, kernel, T):
            K = kernel.shape[-1]
            kpad = jnp.pad(kernel, ((0, 0), (0, 0), (0, max(0, T - K))))[:, :, :T]
            n = 2 * T
            y_f = jnp.fft.rfft(y_bdt, n=n)
            k_f = jnp.fft.rfft(kpad, n=n)
            conv = jnp.fft.irfft(y_f * k_f, n=n)[:, :, :T]
            return conv
        key = jax.random.key(seed)
        ks = jax.random.split(key, 8)
        x = jax.random.normal(ks[0], (B, T, D_MODEL), dtype=jnp.float32)
        W_in = jax.random.normal(ks[1], (D_MODEL, D_MODEL * (ORDER + 1)), dtype=jnp.float32) * (1.0 / np.sqrt(D_MODEL))
        b_in = jnp.zeros((D_MODEL * (ORDER + 1),), dtype=jnp.float32)
        k0 = jax.random.normal(ks[2], (1, D_MODEL, KERNEL_SIZE), dtype=jnp.float32) * 0.02
        k1 = jax.random.normal(ks[3], (1, D_MODEL, KERNEL_SIZE), dtype=jnp.float32) * 0.02
        gamma = jnp.ones((D_MODEL,), dtype=jnp.float32)
        beta = jnp.zeros((D_MODEL,), dtype=jnp.float32)
        W_out = jax.random.normal(ks[4], (D_MODEL, D_MODEL), dtype=jnp.float32) * (1.0 / np.sqrt(D_MODEL))
        b_out = jnp.zeros((D_MODEL,), dtype=jnp.float32)
        return {'x': x, 'W_in': W_in, 'b_in': b_in, 'k0': k0, 'k1': k1, 'gamma': gamma, 'beta': beta, 'W_out': W_out, 'b_out': b_out}
    _L0_attn_in = _L0_attn_setup()

    def _L0_ffn_setup():
        import jax, jax.numpy as jnp
        import numpy as np
        H = 128
        I = 64
        E = 64
        G = 8
        TOPK_GROUP = 4
        K = 8
        I_SH = 128
        SCALE = 2.5

        def _route(x, router_w, e_bias):
            T = x.shape[0]
            scores = jax.nn.sigmoid(x.astype(jnp.float32) @ router_w.T.astype(jnp.float32))
            sfc = jax.lax.stop_gradient(scores) + e_bias[None, :]
            group_scores = jax.lax.top_k(sfc.reshape(T, G, E // G), 2)[0].sum(-1)
            _, gidx = jax.lax.top_k(group_scores, TOPK_GROUP)
            gmask = jax.nn.one_hot(gidx, G, dtype=sfc.dtype).sum(1)
            smask = jnp.repeat(gmask, E // G, axis=1)
            masked = jnp.where(smask > 0, sfc, 0.0)
            _, topk_idx = jax.lax.top_k(masked, K)
            w = jnp.take_along_axis(scores, topk_idx, axis=1)
            w = w / (w.sum(-1, keepdims=True) + 1e-20)
            return (topk_idx, w * SCALE)
        key = jax.random.key(seed)
        ks = jax.random.split(key, 9)
        s = 0.02
        return {'hidden_states': jax.random.normal(ks[0], (2, 128, H), jnp.float32), 'router_w': jax.random.normal(ks[1], (E, H), jnp.float32) * s, 'e_bias': jnp.zeros((E,), jnp.float32), 'Wg': jax.random.normal(ks[2], (E, H, I), jnp.float32) * s, 'Wu': jax.random.normal(ks[3], (E, H, I), jnp.float32) * s, 'Wd': jax.random.normal(ks[4], (E, I, H), jnp.float32) * s, 'SWg': jax.random.normal(ks[5], (H, I_SH), jnp.float32) * s, 'SWu': jax.random.normal(ks[6], (H, I_SH), jnp.float32) * s, 'SWd': jax.random.normal(ks[7], (I_SH, H), jnp.float32) * s}
    _L0_ffn_in = _L0_ffn_setup()

    def _L1_attn_setup():
        import jax, jax.numpy as jnp
        import numpy as np
        B, T, D = (2, 256, 128)
        NH, DH = (16, 64)
        SCALE_INIT = 0.02
        key = jax.random.key(seed)
        kx, kq, kk, kv, ko = jax.random.split(key, 5)
        return {'x': jax.random.normal(kx, (B, T, D), dtype=jnp.float32), 'Wq': jax.random.normal(kq, (D, NH * DH), dtype=jnp.float32) * SCALE_INIT, 'Wk': jax.random.normal(kk, (D, NH * DH), dtype=jnp.float32) * SCALE_INIT, 'Wv': jax.random.normal(kv, (D, NH * DH), dtype=jnp.float32) * SCALE_INIT, 'Wo': jax.random.normal(ko, (NH * DH, D), dtype=jnp.float32) * SCALE_INIT}
    _L1_attn_in = _L1_attn_setup()

    def _L1_ffn_setup():
        import jax, jax.numpy as jnp
        import numpy as np
        BLOCK = 16
        _GRID = jnp.array([0.0, 0.5, 1.0, 1.5, 2.0, 3.0, 4.0, 6.0], dtype=jnp.float32)
        _MID = jnp.array([0.25, 0.75, 1.25, 1.75, 2.5, 3.5, 5.0], dtype=jnp.float32)

        def fp4_quant_dequant(x):
            shape = x.shape
            xb = x.reshape(shape[:-1] + (shape[-1] // BLOCK, BLOCK))
            scale = jnp.max(jnp.abs(xb), axis=-1, keepdims=True) / 6.0
            scale = jnp.maximum(scale, jnp.float32(1e-12))
            xn = xb / scale
            idx = jnp.searchsorted(_MID, jnp.abs(xn))
            q = _GRID[idx] * jnp.sign(xn) * scale
            return q.reshape(shape)

        def fp4_linear(x, w):
            xq = fp4_quant_dequant(x)
            wq = fp4_quant_dequant(w)
            return jnp.einsum('bsk,nk->bsn', xq, wq)
        key = jax.random.key(seed)
        k1, k2, k3, k4 = jax.random.split(key, 4)
        H, I = (128, 352)
        x = jax.random.normal(k1, (4, 512, H), dtype=jnp.float32)
        w_gate = jax.random.normal(k2, (I, H), dtype=jnp.float32) * 0.02
        w_up = jax.random.normal(k3, (I, H), dtype=jnp.float32) * 0.02
        w_down = jax.random.normal(k4, (H, I), dtype=jnp.float32) * 0.02
        return {'x': x, 'w_gate': w_gate, 'w_up': w_up, 'w_down': w_down}
    _L1_ffn_in = _L1_ffn_setup()

    def _L2_attn_setup():
        import jax, jax.numpy as jnp
        import numpy as np
        B, T, D = (1, 256, 128)
        H = 16
        SEM_DIM, GEO_DIM, ATTN_DIM = (64, 64, 128)
        ROPE_BASE = 10000.0
        NEG = -1000000000.0

        def _heads(y, hd):
            b, t, _ = y.shape
            return y.reshape(b, t, H, hd).transpose(0, 2, 1, 3)

        def _rope(x, cos, sin):
            hd = x.shape[-1]
            x1, x2 = (x[..., :hd // 2], x[..., hd // 2:])
            c = cos[None, None]
            sn = sin[None, None]
            return jnp.concatenate([x1 * c - x2 * sn, x2 * c + x1 * sn], axis=-1)

        def _forward(x, wq_sem, wk_sem, wq_geo, wk_geo, wv, wo, k_sem_null, k_geo_null, v_null):
            b, t, _ = x.shape
            sem_hd = wq_sem.shape[1] // H
            geo_hd = wq_geo.shape[1] // H
            v_hd = wv.shape[1] // H
            sem_scale = 1.0 / np.sqrt(sem_hd)
            geo_scale = 1.0 / np.sqrt(geo_hd)
            qs = _heads(x @ wq_sem, sem_hd)
            ks = _heads(x @ wk_sem, sem_hd)
            qg = _heads(x @ wq_geo, geo_hd)
            kg = _heads(x @ wk_geo, geo_hd)
            v = _heads(x @ wv, v_hd)
            pos = jnp.arange(t, dtype=jnp.float32)
            inv_freq = 1.0 / ROPE_BASE ** (jnp.arange(0, geo_hd, 2, dtype=jnp.float32) / geo_hd)
            ang = pos[:, None] * inv_freq[None, :]
            cos, sin = (jnp.cos(ang), jnp.sin(ang))
            qg = _rope(qg, cos, sin)
            kg = _rope(kg, cos, sin)
            ksn = jnp.broadcast_to(k_sem_null.reshape(1, 1, H, sem_hd).transpose(0, 2, 1, 3), (b, H, 1, sem_hd))
            kgn = jnp.broadcast_to(k_geo_null.reshape(1, 1, H, geo_hd).transpose(0, 2, 1, 3), (b, H, 1, geo_hd))
            vn = jnp.broadcast_to(v_null.reshape(1, 1, H, v_hd).transpose(0, 2, 1, 3), (b, H, 1, v_hd))
            ks_full = jnp.concatenate([ksn, ks], axis=2)
            kg_full = jnp.concatenate([kgn, kg], axis=2)
            v_full = jnp.concatenate([vn, v], axis=2)
            scores = jnp.einsum('bhqd,bhkd->bhqk', qs, ks_full).astype(jnp.float32) * sem_scale + jnp.einsum('bhqd,bhkd->bhqk', qg, kg_full).astype(jnp.float32) * geo_scale
            causal = jnp.tril(jnp.ones((t, t), dtype=bool))
            mask = jnp.concatenate([jnp.ones((t, 1), dtype=bool), causal], axis=1)
            scores = jnp.where(mask[None, None], scores, NEG)
            probs = jax.nn.softmax(scores, axis=-1).astype(v.dtype)
            out = jnp.einsum('bhqk,bhkd->bhqd', probs, v_full)
            out = out.transpose(0, 2, 1, 3).reshape(b, t, H * v_hd)
            return out @ wo
        key = jax.random.key(seed)
        ks = jax.random.split(key, 10)
        s = 0.02
        return {'x': jax.random.normal(ks[0], (B, T, D), jnp.float32), 'wq_sem': jax.random.normal(ks[1], (D, SEM_DIM), jnp.float32) * s, 'wk_sem': jax.random.normal(ks[2], (D, SEM_DIM), jnp.float32) * s, 'wq_geo': jax.random.normal(ks[3], (D, GEO_DIM), jnp.float32) * s, 'wk_geo': jax.random.normal(ks[4], (D, GEO_DIM), jnp.float32) * s, 'wv': jax.random.normal(ks[5], (D, ATTN_DIM), jnp.float32) * s, 'wo': jax.random.normal(ks[6], (ATTN_DIM, D), jnp.float32) * s, 'k_sem_null': jax.random.normal(ks[7], (SEM_DIM,), jnp.float32) * s, 'k_geo_null': jax.random.normal(ks[8], (GEO_DIM,), jnp.float32) * s, 'v_null': jax.random.normal(ks[9], (ATTN_DIM,), jnp.float32) * s}
    _L2_attn_in = _L2_attn_setup()

    def _L2_ffn_setup():
        import jax, jax.numpy as jnp
        import numpy as np
        BEST_K = 2

        def _expert(xf, w1, w3, w2):
            return jax.nn.silu(xf @ w1) * (xf @ w3) @ w2
        key = jax.random.key(seed)
        ks = jax.random.split(key, 9)
        E, S_sh, D, H = (8, 2, 128, 64)
        B, S = (2, 256)
        w = lambda k, shape: jax.random.normal(k, shape, dtype=jnp.float32) * 0.02
        return {'x': jax.random.normal(ks[0], (B, S, D), dtype=jnp.float32), 'router_w': w(ks[1], (D, E)), 'router_b': jnp.zeros((E,), dtype=jnp.float32), 'routed_w1': w(ks[2], (E, D, H)), 'routed_w3': w(ks[3], (E, D, H)), 'routed_w2': w(ks[4], (E, H, D)), 'shared_w1': w(ks[5], (S_sh, D, H)), 'shared_w3': w(ks[6], (S_sh, D, H)), 'shared_w2': w(ks[7], (S_sh, H, D))}
    _L2_ffn_in = _L2_ffn_setup()

    def _L3_attn_setup():
        import jax, jax.numpy as jnp
        import numpy as np
        D_MODEL = 128
        N_HEADS = 16
        D_HEAD = D_MODEL // N_HEADS
        SEQ = 512
        BATCH = 1
        key = jax.random.key(seed)
        kx, kq, kk, kv, ko = jax.random.split(key, 5)
        scale = (1.0 / D_MODEL) ** 0.5
        return {'x': jax.random.normal(kx, (BATCH, SEQ, D_MODEL), dtype=jnp.float32), 'W_Q': jax.random.normal(kq, (D_MODEL, D_MODEL), dtype=jnp.float32) * scale, 'W_K': jax.random.normal(kk, (D_MODEL, D_MODEL), dtype=jnp.float32) * scale, 'W_V': jax.random.normal(kv, (D_MODEL, D_MODEL), dtype=jnp.float32) * scale, 'W_o': jax.random.normal(ko, (D_MODEL, D_MODEL), dtype=jnp.float32) * scale}
    _L3_attn_in = _L3_attn_setup()

    def _L3_ffn_setup():
        import jax, jax.numpy as jnp
        import numpy as np
        H = 128
        I = 256
        E = 8
        TOP_K = 2
        NUM_SHARED = 1
        key = jax.random.key(seed)
        ks = jax.random.split(key, 9)
        s = 0.02
        x = jax.random.normal(ks[0], (2, 256, H), dtype=jnp.float32)
        sg_w = jax.random.normal(ks[1], (I, H), dtype=jnp.float32) * s
        su_w = jax.random.normal(ks[2], (I, H), dtype=jnp.float32) * s
        sd_w = jax.random.normal(ks[3], (H, I), dtype=jnp.float32) * s
        router_w = jax.random.normal(ks[4], (E, H), dtype=jnp.float32) * s
        routing_bias = jnp.zeros((E,), dtype=jnp.float32)
        wg = jax.random.normal(ks[5], (E, I, H), dtype=jnp.float32) * s
        wu = jax.random.normal(ks[6], (E, I, H), dtype=jnp.float32) * s
        wd = jax.random.normal(ks[7], (E, H, I), dtype=jnp.float32) * s
        return {'x': x, 'sg_w': sg_w, 'su_w': su_w, 'sd_w': sd_w, 'router_w': router_w, 'routing_bias': routing_bias, 'wg': wg, 'wu': wu, 'wd': wd}
    _L3_ffn_in = _L3_ffn_setup()
    _d = {'L0_attn_x': _L0_attn_in['x'], 'L0_attn_W_in': _L0_attn_in['W_in'], 'L0_attn_b_in': _L0_attn_in['b_in'], 'L0_attn_k0': _L0_attn_in['k0'], 'L0_attn_k1': _L0_attn_in['k1'], 'L0_attn_gamma': _L0_attn_in['gamma'], 'L0_attn_beta': _L0_attn_in['beta'], 'L0_attn_W_out': _L0_attn_in['W_out'], 'L0_attn_b_out': _L0_attn_in['b_out'], 'L0_ffn_router_w': _L0_ffn_in['router_w'], 'L0_ffn_e_bias': _L0_ffn_in['e_bias'], 'L0_ffn_Wg': _L0_ffn_in['Wg'], 'L0_ffn_Wu': _L0_ffn_in['Wu'], 'L0_ffn_Wd': _L0_ffn_in['Wd'], 'L0_ffn_SWg': _L0_ffn_in['SWg'], 'L0_ffn_SWu': _L0_ffn_in['SWu'], 'L0_ffn_SWd': _L0_ffn_in['SWd'], 'L1_attn_Wq': _L1_attn_in['Wq'], 'L1_attn_Wk': _L1_attn_in['Wk'], 'L1_attn_Wv': _L1_attn_in['Wv'], 'L1_attn_Wo': _L1_attn_in['Wo'], 'L1_ffn_w_gate': _L1_ffn_in['w_gate'], 'L1_ffn_w_up': _L1_ffn_in['w_up'], 'L1_ffn_w_down': _L1_ffn_in['w_down'], 'L2_attn_wq_sem': _L2_attn_in['wq_sem'], 'L2_attn_wk_sem': _L2_attn_in['wk_sem'], 'L2_attn_wq_geo': _L2_attn_in['wq_geo'], 'L2_attn_wk_geo': _L2_attn_in['wk_geo'], 'L2_attn_wv': _L2_attn_in['wv'], 'L2_attn_wo': _L2_attn_in['wo'], 'L2_attn_k_sem_null': _L2_attn_in['k_sem_null'], 'L2_attn_k_geo_null': _L2_attn_in['k_geo_null'], 'L2_attn_v_null': _L2_attn_in['v_null'], 'L2_ffn_router_w': _L2_ffn_in['router_w'], 'L2_ffn_router_b': _L2_ffn_in['router_b'], 'L2_ffn_routed_w1': _L2_ffn_in['routed_w1'], 'L2_ffn_routed_w3': _L2_ffn_in['routed_w3'], 'L2_ffn_routed_w2': _L2_ffn_in['routed_w2'], 'L2_ffn_shared_w1': _L2_ffn_in['shared_w1'], 'L2_ffn_shared_w3': _L2_ffn_in['shared_w3'], 'L2_ffn_shared_w2': _L2_ffn_in['shared_w2'], 'L3_attn_W_Q': _L3_attn_in['W_Q'], 'L3_attn_W_K': _L3_attn_in['W_K'], 'L3_attn_W_V': _L3_attn_in['W_V'], 'L3_attn_W_o': _L3_attn_in['W_o'], 'L3_ffn_sg_w': _L3_ffn_in['sg_w'], 'L3_ffn_su_w': _L3_ffn_in['su_w'], 'L3_ffn_sd_w': _L3_ffn_in['sd_w'], 'L3_ffn_router_w': _L3_ffn_in['router_w'], 'L3_ffn_routing_bias': _L3_ffn_in['routing_bias'], 'L3_ffn_wg': _L3_ffn_in['wg'], 'L3_ffn_wu': _L3_ffn_in['wu'], 'L3_ffn_wd': _L3_ffn_in['wd']}
    _x0 = _d['L0_attn_x']
    _d['L0_attn_x'] = jax.random.normal(jax.random.fold_in(jax.random.key(seed), 1), (2, 1024, 128), dtype=_x0.dtype)
    del _x0
    return _d

def reference(L0_attn_x, L0_attn_W_in, L0_attn_b_in, L0_attn_k0, L0_attn_k1, L0_attn_gamma, L0_attn_beta, L0_attn_W_out, L0_attn_b_out, L0_ffn_router_w, L0_ffn_e_bias, L0_ffn_Wg, L0_ffn_Wu, L0_ffn_Wd, L0_ffn_SWg, L0_ffn_SWu, L0_ffn_SWd, L1_attn_Wq, L1_attn_Wk, L1_attn_Wv, L1_attn_Wo, L1_ffn_w_gate, L1_ffn_w_up, L1_ffn_w_down, L2_attn_wq_sem, L2_attn_wk_sem, L2_attn_wq_geo, L2_attn_wk_geo, L2_attn_wv, L2_attn_wo, L2_attn_k_sem_null, L2_attn_k_geo_null, L2_attn_v_null, L2_ffn_router_w, L2_ffn_router_b, L2_ffn_routed_w1, L2_ffn_routed_w3, L2_ffn_routed_w2, L2_ffn_shared_w1, L2_ffn_shared_w3, L2_ffn_shared_w2, L3_attn_W_Q, L3_attn_W_K, L3_attn_W_V, L3_attn_W_o, L3_ffn_sg_w, L3_ffn_su_w, L3_ffn_sd_w, L3_ffn_router_w, L3_ffn_routing_bias, L3_ffn_wg, L3_ffn_wu, L3_ffn_wd):

    def _L0_attn_ref(x, W_in, b_in, k0, k1, gamma, beta, W_out, b_out):
        import jax, jax.numpy as jnp
        import numpy as np
        D_MODEL = 128
        KERNEL_SIZE = 128
        ORDER = 2
        B, T = (4, 256)

        def _layernorm(x, gamma, beta, eps=1e-05):
            mu = jnp.mean(x, axis=-1, keepdims=True)
            var = jnp.mean(jnp.square(x - mu), axis=-1, keepdims=True)
            return (x - mu) * jax.lax.rsqrt(var + eps) * gamma + beta

        def _fft_conv(y_bdt, kernel, T):
            K = kernel.shape[-1]
            kpad = jnp.pad(kernel, ((0, 0), (0, 0), (0, max(0, T - K))))[:, :, :T]
            n = 2 * T
            y_f = jnp.fft.rfft(y_bdt, n=n)
            k_f = jnp.fft.rfft(kpad, n=n)
            conv = jnp.fft.irfft(y_f * k_f, n=n)[:, :, :T]
            return conv
        Bn, Tn, Dn = x.shape
        residual = x
        xn = _layernorm(x, gamma, beta)
        proj = (xn @ W_in + b_in).reshape(Bn, Tn, ORDER + 1, Dn)
        v = proj[:, :, 0, :]
        y = jnp.transpose(v, (0, 2, 1))
        for i, kern in enumerate((k0, k1)):
            xi = jnp.transpose(proj[:, :, i + 1, :], (0, 2, 1))
            y = _fft_conv(y, kern, Tn) * xi
        y = jnp.transpose(y, (0, 2, 1))
        y = y @ W_out + b_out
        return residual + y

    def _L0_ffn_ref(hidden_states, router_w, e_bias, Wg, Wu, Wd, SWg, SWu, SWd):
        import jax, jax.numpy as jnp
        import numpy as np
        H = 128
        I = 64
        E = 64
        G = 8
        TOPK_GROUP = 4
        K = 8
        I_SH = 128
        SCALE = 2.5

        def _route(x, router_w, e_bias):
            T = x.shape[0]
            scores = jax.nn.sigmoid(x.astype(jnp.float32) @ router_w.T.astype(jnp.float32))
            sfc = jax.lax.stop_gradient(scores) + e_bias[None, :]
            group_scores = jax.lax.top_k(sfc.reshape(T, G, E // G), 2)[0].sum(-1)
            _, gidx = jax.lax.top_k(group_scores, TOPK_GROUP)
            gmask = jax.nn.one_hot(gidx, G, dtype=sfc.dtype).sum(1)
            smask = jnp.repeat(gmask, E // G, axis=1)
            masked = jnp.where(smask > 0, sfc, 0.0)
            _, topk_idx = jax.lax.top_k(masked, K)
            w = jnp.take_along_axis(scores, topk_idx, axis=1)
            w = w / (w.sum(-1, keepdims=True) + 1e-20)
            return (topk_idx, w * SCALE)
        orig_shape = hidden_states.shape
        x = hidden_states.reshape(-1, orig_shape[-1])
        T = x.shape[0]
        topk_idx, topk_w = _route(x, router_w, e_bias)
        coef = jnp.zeros((T, E), topk_w.dtype).at[jnp.arange(T)[:, None], topk_idx].add(topk_w)
        g = jnp.einsum('th,ehi->tei', x, Wg)
        u = jnp.einsum('th,ehi->tei', x, Wu)
        h = jax.nn.silu(g) * u * coef[:, :, None]
        moe_out = jnp.einsum('tei,eih->th', h, Wd)
        shared = jax.nn.silu(x @ SWg) * (x @ SWu) @ SWd
        return (moe_out + shared).reshape(orig_shape)

    def _L1_attn_ref(x, Wq, Wk, Wv, Wo):
        import jax, jax.numpy as jnp
        import numpy as np
        B, T, D = (2, 256, 128)
        NH, DH = (16, 64)
        SCALE_INIT = 0.02
        b, t, _ = x.shape

        def split_heads(h):
            return h.reshape(b, t, NH, DH).transpose(0, 2, 1, 3)
        q = split_heads(x @ Wq)
        k = split_heads(x @ Wk)
        v = split_heads(x @ Wv)
        scale = jnp.asarray(1.0 / np.sqrt(DH), dtype=x.dtype)
        scores = jnp.einsum('bhqd,bhkd->bhqk', q, k) * scale
        causal_mask = jnp.arange(t)[None, :] > jnp.arange(t)[:, None]
        scores = jnp.where(causal_mask, -jnp.inf, scores)
        attn = jax.nn.softmax(scores, axis=-1)
        attn = jnp.nan_to_num(attn)
        o = jnp.einsum('bhqk,bhkd->bhqd', attn, v)
        o = o.transpose(0, 2, 1, 3).reshape(b, t, NH * DH)
        return o @ Wo

    def _L1_ffn_ref(x, w_gate, w_up, w_down):
        import jax, jax.numpy as jnp
        import numpy as np
        BLOCK = 16
        _GRID = jnp.array([0.0, 0.5, 1.0, 1.5, 2.0, 3.0, 4.0, 6.0], dtype=jnp.float32)
        _MID = jnp.array([0.25, 0.75, 1.25, 1.75, 2.5, 3.5, 5.0], dtype=jnp.float32)

        def fp4_quant_dequant(x):
            shape = x.shape
            xb = x.reshape(shape[:-1] + (shape[-1] // BLOCK, BLOCK))
            scale = jnp.max(jnp.abs(xb), axis=-1, keepdims=True) / 6.0
            scale = jnp.maximum(scale, jnp.float32(1e-12))
            xn = xb / scale
            idx = jnp.searchsorted(_MID, jnp.abs(xn))
            q = _GRID[idx] * jnp.sign(xn) * scale
            return q.reshape(shape)

        def fp4_linear(x, w):
            xq = fp4_quant_dequant(x)
            wq = fp4_quant_dequant(w)
            return jnp.einsum('bsk,nk->bsn', xq, wq)
        gate = fp4_linear(x, w_gate)
        y = fp4_linear(x, w_up)
        h = jax.nn.silu(gate) * y
        return fp4_linear(h, w_down)

    def _L2_attn_ref(x, wq_sem, wk_sem, wq_geo, wk_geo, wv, wo, k_sem_null, k_geo_null, v_null):
        import jax, jax.numpy as jnp
        import numpy as np
        B, T, D = (1, 256, 128)
        H = 16
        SEM_DIM, GEO_DIM, ATTN_DIM = (64, 64, 128)
        ROPE_BASE = 10000.0
        NEG = -1000000000.0

        def _heads(y, hd):
            b, t, _ = y.shape
            return y.reshape(b, t, H, hd).transpose(0, 2, 1, 3)

        def _rope(x, cos, sin):
            hd = x.shape[-1]
            x1, x2 = (x[..., :hd // 2], x[..., hd // 2:])
            c = cos[None, None]
            sn = sin[None, None]
            return jnp.concatenate([x1 * c - x2 * sn, x2 * c + x1 * sn], axis=-1)

        def _forward(x, wq_sem, wk_sem, wq_geo, wk_geo, wv, wo, k_sem_null, k_geo_null, v_null):
            b, t, _ = x.shape
            sem_hd = wq_sem.shape[1] // H
            geo_hd = wq_geo.shape[1] // H
            v_hd = wv.shape[1] // H
            sem_scale = 1.0 / np.sqrt(sem_hd)
            geo_scale = 1.0 / np.sqrt(geo_hd)
            qs = _heads(x @ wq_sem, sem_hd)
            ks = _heads(x @ wk_sem, sem_hd)
            qg = _heads(x @ wq_geo, geo_hd)
            kg = _heads(x @ wk_geo, geo_hd)
            v = _heads(x @ wv, v_hd)
            pos = jnp.arange(t, dtype=jnp.float32)
            inv_freq = 1.0 / ROPE_BASE ** (jnp.arange(0, geo_hd, 2, dtype=jnp.float32) / geo_hd)
            ang = pos[:, None] * inv_freq[None, :]
            cos, sin = (jnp.cos(ang), jnp.sin(ang))
            qg = _rope(qg, cos, sin)
            kg = _rope(kg, cos, sin)
            ksn = jnp.broadcast_to(k_sem_null.reshape(1, 1, H, sem_hd).transpose(0, 2, 1, 3), (b, H, 1, sem_hd))
            kgn = jnp.broadcast_to(k_geo_null.reshape(1, 1, H, geo_hd).transpose(0, 2, 1, 3), (b, H, 1, geo_hd))
            vn = jnp.broadcast_to(v_null.reshape(1, 1, H, v_hd).transpose(0, 2, 1, 3), (b, H, 1, v_hd))
            ks_full = jnp.concatenate([ksn, ks], axis=2)
            kg_full = jnp.concatenate([kgn, kg], axis=2)
            v_full = jnp.concatenate([vn, v], axis=2)
            scores = jnp.einsum('bhqd,bhkd->bhqk', qs, ks_full).astype(jnp.float32) * sem_scale + jnp.einsum('bhqd,bhkd->bhqk', qg, kg_full).astype(jnp.float32) * geo_scale
            causal = jnp.tril(jnp.ones((t, t), dtype=bool))
            mask = jnp.concatenate([jnp.ones((t, 1), dtype=bool), causal], axis=1)
            scores = jnp.where(mask[None, None], scores, NEG)
            probs = jax.nn.softmax(scores, axis=-1).astype(v.dtype)
            out = jnp.einsum('bhqk,bhkd->bhqd', probs, v_full)
            out = out.transpose(0, 2, 1, 3).reshape(b, t, H * v_hd)
            return out @ wo
        return _forward(x, wq_sem, wk_sem, wq_geo, wk_geo, wv, wo, k_sem_null, k_geo_null, v_null)

    def _L2_ffn_ref(x, router_w, router_b, routed_w1, routed_w3, routed_w2, shared_w1, shared_w3, shared_w2):
        import jax, jax.numpy as jnp
        import numpy as np
        BEST_K = 2

        def _expert(xf, w1, w3, w2):
            return jax.nn.silu(xf @ w1) * (xf @ w3) @ w2
        B, S, D = x.shape
        T = B * S
        xf = x.reshape(T, D)
        logits = xf @ router_w + router_b
        topk_vals, topk_idx = jax.lax.top_k(logits, BEST_K)
        sparse = jnp.full_like(logits, -jnp.inf)
        sparse = sparse.at[jnp.arange(T)[:, None], topk_idx].set(topk_vals)
        gates = jax.nn.softmax(sparse, axis=-1)
        routed = jax.vmap(_expert, in_axes=(None, 0, 0, 0))(xf, routed_w1, routed_w3, routed_w2)
        routed_out = jnp.einsum('etd,te->td', routed, gates)
        shared_out = jax.vmap(_expert, in_axes=(None, 0, 0, 0))(xf, shared_w1, shared_w3, shared_w2).sum(axis=0)
        return (routed_out + shared_out).reshape(B, S, D)

    def _L3_attn_ref(x, W_Q, W_K, W_V, W_o):
        import jax, jax.numpy as jnp
        import numpy as np
        D_MODEL = 128
        N_HEADS = 16
        D_HEAD = D_MODEL // N_HEADS
        SEQ = 512
        BATCH = 1
        B, S, _ = x.shape

        def heads(w):
            return (x @ w).reshape(B, S, N_HEADS, D_HEAD).transpose(0, 2, 1, 3)
        Q, K, V = (heads(W_Q), heads(W_K), heads(W_V))
        scores = jnp.einsum('bhqd,bhkd->bhqk', Q, K) / D_HEAD ** 0.5
        causal = jnp.triu(jnp.full((S, S), -jnp.inf, dtype=scores.dtype), k=1)
        scores = scores + causal
        probs = jax.nn.softmax(scores, axis=-1)
        out = jnp.einsum('bhqk,bhkd->bhqd', probs, V)
        out = out.transpose(0, 2, 1, 3).reshape(B, S, D_MODEL)
        return out @ W_o

    def _L3_ffn_ref(x, sg_w, su_w, sd_w, router_w, routing_bias, wg, wu, wd):
        import jax, jax.numpy as jnp
        import numpy as np
        H = 128
        I = 256
        E = 8
        TOP_K = 2
        NUM_SHARED = 1
        orig_shape = x.shape
        xt = x.reshape(-1, H)
        T = xt.shape[0]
        shared = jax.nn.silu(xt @ sg_w.T) * (xt @ su_w.T) @ sd_w.T
        shared = shared / NUM_SHARED
        logits = xt @ router_w.T + routing_bias
        probs = jax.nn.sigmoid(logits)
        topk_p, topk_idx = jax.lax.top_k(probs, TOP_K)
        topk_p = topk_p / jnp.sum(topk_p, axis=-1, keepdims=True)
        w = jnp.zeros((T, E), dtype=xt.dtype)
        w = w.at[jnp.arange(T)[:, None], topk_idx].add(topk_p)
        g = jnp.einsum('th,eih->tei', xt, wg)
        u = jnp.einsum('th,eih->tei', xt, wu)
        h = jax.nn.silu(g) * u
        y = jnp.einsum('tei,ehi->teh', h, wd)
        routed = jnp.einsum('te,teh->th', w, y)
        return (shared + routed).reshape(orig_shape)
    x = L0_attn_x
    xn = _layernorm(x, axis=-1)
    x = x + _L0_attn_ref(xn, L0_attn_W_in, L0_attn_b_in, L0_attn_k0, L0_attn_k1, L0_attn_gamma, L0_attn_beta, L0_attn_W_out, L0_attn_b_out) + _L0_ffn_ref(xn, L0_ffn_router_w, L0_ffn_e_bias, L0_ffn_Wg, L0_ffn_Wu, L0_ffn_Wd, L0_ffn_SWg, L0_ffn_SWu, L0_ffn_SWd)
    xn = _layernorm(x, axis=-1)
    x = x + _L1_attn_ref(xn, L1_attn_Wq, L1_attn_Wk, L1_attn_Wv, L1_attn_Wo) + _L1_ffn_ref(xn, L1_ffn_w_gate, L1_ffn_w_up, L1_ffn_w_down)
    xn = _layernorm(x, axis=-1)
    x = x + _L2_attn_ref(xn, L2_attn_wq_sem, L2_attn_wk_sem, L2_attn_wq_geo, L2_attn_wk_geo, L2_attn_wv, L2_attn_wo, L2_attn_k_sem_null, L2_attn_k_geo_null, L2_attn_v_null) + _L2_ffn_ref(xn, L2_ffn_router_w, L2_ffn_router_b, L2_ffn_routed_w1, L2_ffn_routed_w3, L2_ffn_routed_w2, L2_ffn_shared_w1, L2_ffn_shared_w3, L2_ffn_shared_w2)
    xn = _layernorm(x, axis=-1)
    x = x + _L3_attn_ref(xn, L3_attn_W_Q, L3_attn_W_K, L3_attn_W_V, L3_attn_W_o) + _L3_ffn_ref(xn, L3_ffn_sg_w, L3_ffn_su_w, L3_ffn_sd_w, L3_ffn_router_w, L3_ffn_routing_bias, L3_ffn_wg, L3_ffn_wu, L3_ffn_wd)
    return x

_drawn_inputs = setup_inputs


def setup_inputs(seed=0):
    import zlib

    import numpy as np

    out = dict(_drawn_inputs(seed))
    spreads = {'L0_attn_b_in': (0.0, 0.8),
     'L0_attn_gamma': (1.0, 0.6),
     'L0_attn_beta': (0.0, 0.8),
     'L0_attn_b_out': (0.0, 0.1),
     'L0_ffn_e_bias': (0.0, 0.8),
     'L2_ffn_router_b': (0.0, 0.8),
     'L3_ffn_routing_bias': (0.0, 0.8)}
    factors = {'L0_ffn_router_w': 8.0,
     'L0_ffn_Wg': 8.0,
     'L0_ffn_Wu': 8.0,
     'L0_ffn_Wd': 8.0,
     'L0_ffn_SWg': 8.0,
     'L0_ffn_SWu': 8.0,
     'L0_ffn_SWd': 8.0,
     'L1_attn_Wq': 8.0,
     'L1_attn_Wk': 8.0,
     'L1_attn_Wv': 6.724,
     'L1_attn_Wo': 7.147,
     'L1_ffn_w_gate': 8.0,
     'L1_ffn_w_up': 8.0,
     'L1_ffn_w_down': 8.0,
     'L2_attn_wq_sem': 8.0,
     'L2_attn_wk_sem': 8.0,
     'L2_attn_wq_geo': 8.0,
     'L2_attn_wk_geo': 8.0,
     'L2_attn_wv': 8.0,
     'L2_attn_wo': 8.0,
     'L2_attn_k_sem_null': 64.0,
     'L2_attn_k_geo_null': 64.0,
     'L2_attn_v_null': 64.0,
     'L2_ffn_router_w': 8.0,
     'L2_ffn_routed_w1': 8.0,
     'L2_ffn_routed_w3': 8.0,
     'L2_ffn_routed_w2': 8.0,
     'L2_ffn_shared_w1': 8.0,
     'L2_ffn_shared_w3': 8.0,
     'L2_ffn_shared_w2': 8.0,
     'L3_ffn_sg_w': 8.0,
     'L3_ffn_su_w': 8.0,
     'L3_ffn_sd_w': 8.0,
     'L3_ffn_router_w': 8.0,
     'L3_ffn_wg': 8.0,
     'L3_ffn_wu': 8.0,
     'L3_ffn_wd': 8.0,
     'L3_attn_W_Q': 5.262,
     'L3_attn_W_K': 5.063,
     'L3_attn_W_V': 3.413,
     'L3_attn_W_o': 3.387}
    for name, (base, spread) in spreads.items():
        noise = np.random.default_rng([zlib.crc32(name.encode()), seed]).standard_normal(out[name].shape)
        drawn = base * np.exp(spread * noise) if base else spread * noise
        out[name] = jnp.asarray(drawn.astype(out[name].dtype))
    for name, factor in factors.items():
        out[name] = (out[name] * factor).astype(out[name].dtype)
    return out
```

```python
from contextlib import ExitStack

import concourse.bass as bass
import numpy as np
from concourse import mybir

F32 = mybir.dt.float32
BF16 = mybir.dt.bfloat16
ALU = mybir.AluOpType
ACT = mybir.ActivationFunctionType
AX = mybir.AxisListType

P = 128
BATCH, SEQ = 2, 1024
TOK = BATCH * SEQ
TILES = TOK // P
GRP = 512
GROUPS = TOK // GRP
HEADS = 16
EPS = 1e-5
MASKED = -1e30
CBLK = 32
CWIN = 128
CPAD = CWIN - CBLK
TAPS = 128
NBLK = SEQ // CBLK


def dram_view(ap, offset, dims):
    return bass.AP(tensor=ap.tensor, offset=offset, ap=dims)


class Chip:

    def __init__(self, nc, ctx, dram):
        self.nc, self.ctx, self.dram = nc, ctx, dram
        self.taken = []

        def resident(name, shape):
            return ctx.enter_context(nc.sbuf_tensor(name, shape, F32))

        self.x = resident("x_tokens", [P, TILES, P])
        self.xn = resident("xn_tokens", [P, TILES, P])
        self.xnT = resident("xn_channels", [P, TOK])
        self.y = resident("y_channels", [P, TOK])
        self.ident = resident("identity", [P, P])

    def scope(self):
        return Scope(self)

    def semaphore(self, name):
        self.taken.append(self.nc.alloc_semaphore(name))
        return self.taken[-1]

    def clear_semaphores(self):
        self.nc.clear_and_free_semaphores(self.taken)
        self.nc.all_engine_barrier()
        self.taken = []


class Scope:

    def __init__(self, chip):
        self.chip, self.nc = chip, chip.nc

    def __enter__(self):
        self.ctx = ExitStack()
        self.ctx.__enter__()
        return self

    def __exit__(self, *exc):
        return self.ctx.__exit__(*exc)

    def sb(self, name, shape, dt=F32):
        return self.ctx.enter_context(self.nc.sbuf_tensor(f"{name}_sb", shape, dt))

    def ps(self, name, shape, dt=F32):
        return self.ctx.enter_context(self.nc.psum_tensor(name, shape, dt))

    def sem(self, name):
        return self.chip.semaphore(name)

    def block(self):
        return self.ctx.enter_context(self.nc.Block())


def over_last(ap, n):
    return ap.unsqueeze(len(ap.shape)).to_broadcast(list(ap.shape) + [n])



def stage_load(c):
    nc = c.nc
    with c.scope() as s:
        loaded = s.sem("ld_loaded")
        block = s.block()

        @block.sync
        def _(sp):
            sp.dma_start(c.x[:, :, :], c.dram["x"].rearrange("(t p) d -> p t d", p=P)).then_inc(loaded, 16)
            sp.dma_start(c.ident[:, :], c.dram["ident"]).then_inc(loaded, 16)
            sp.wait_ge(loaded, 32)


def norm_steps(nc, dve, step_done, src, dst, scratch, stat):
    count = [0]

    def link(ins):
        count[0] += 1
        ins.then_inc(step_done, 1)
        dve.wait_ge(step_done, count[0])

    def before_root():
        link(nc.vector.tensor_reduce(out=stat[:, 0, :], in_=src, op=ALU.add, axis=AX.X))
        link(nc.vector.tensor_scalar(stat[:, 1, :], stat[:, 0, :], 1.0 / P, None, ALU.mult))
        link(nc.vector.tensor_tensor(dst, src, over_last(stat[:, 1, :], P), ALU.subtract))
        link(nc.vector.tensor_tensor(scratch, dst, dst, ALU.mult))
        link(nc.vector.tensor_reduce(out=stat[:, 2, :], in_=scratch, op=ALU.add, axis=AX.X))
        return nc.vector.tensor_scalar(stat[:, 3, :], stat[:, 2, :], 1.0 / P, EPS, ALU.mult, ALU.add)

    def after_root():
        link(nc.vector.reciprocal(stat[:, 5, :], stat[:, 4, :]))
        return nc.vector.tensor_tensor(dst, dst, over_last(stat[:, 5, :], P), ALU.mult)

    return before_root, after_root


def stage_norm(c, tag):
    nc = c.nc
    with c.scope() as s:
        scratch = s.sb(f"{tag}_sq", [P, TILES, P])
        stat = s.sb(f"{tag}_stat", [P, 6, TILES])
        tp = [s.ps(f"{tag}_tp{g}", [P, GRP]) for g in range(GROUPS)]
        step_done, var_ready, root_ready = s.sem(f"{tag}_step"), s.sem(f"{tag}_var"), s.sem(f"{tag}_root")
        xn_ready, turned = s.sem(f"{tag}_xn"), s.sem(f"{tag}_turned")
        block = s.block()

        @block.vector
        def _(dve):
            before_root, after_root = norm_steps(nc, dve, step_done, c.x[:, :, :], c.xn[:, :, :], scratch[:, :, :], stat)
            before_root().then_inc(var_ready, 1)
            dve.wait_ge(root_ready, 1)
            after_root().then_inc(xn_ready, 1)
            for g in range(1, GROUPS, 2):
                dve.wait_ge(turned, g + 1)
                nc.vector.tensor_copy(c.xnT[:, g * GRP:(g + 1) * GRP], tp[g][:, :])

        @block.scalar
        def _(act):
            act.wait_ge(var_ready, 1)
            nc.scalar.activation(stat[:, 4, :], stat[:, 3, :], ACT.Sqrt).then_inc(root_ready, 1)
            for g in range(0, GROUPS, 2):
                act.wait_ge(turned, g + 1)
                nc.scalar.activation(c.xnT[:, g * GRP:(g + 1) * GRP], tp[g][:, :], ACT.Copy)

        @block.tensor
        def _(pe):
            pe.wait_ge(xn_ready, 1)
            for t in range(TILES):
                g, k = divmod(t, GRP // P)
                ins = nc.tensor.transpose(tp[g][:, k * P:(k + 1) * P], c.xn[:, t, :], c.ident[:, :])
                if k == GRP // P - 1:
                    ins.then_inc(turned, 1)


def stage_add(c, tag, also_xn):
    nc = c.nc
    with c.scope() as s:
        tp = [s.ps(f"{tag}_tp{g}", [P, GRP // P, P]) for g in range(GROUPS)]
        turned, res_added = s.sem(f"{tag}_turned"), s.sem(f"{tag}_res")
        block = s.block()

        @block.tensor
        def _(pe):
            for t in range(TILES):
                g, k = divmod(t, GRP // P)
                ins = nc.tensor.transpose(tp[g][:, k, :], c.y[:, t * P:(t + 1) * P], c.ident[:, :])
                if k == GRP // P - 1:
                    ins.then_inc(turned, 1)

        @block.vector
        def _(dve):
            if also_xn:
                nc.vector.tensor_tensor(c.x[:, :, :], c.x[:, :, :], c.xn[:, :, :], ALU.add).then_inc(res_added, 1)
                dve.wait_ge(res_added, 1)
            per = GRP // P
            for g in range(GROUPS):
                dve.wait_ge(turned, g + 1)
                nc.vector.tensor_tensor(c.x[:, g * per:(g + 1) * per, :], tp[g][:, :, :],
                                        c.x[:, g * per:(g + 1) * per, :], ALU.add)


def stage_store(c):
    nc = c.nc
    with c.scope() as s:
        stored = s.sem("st_stored")
        block = s.block()

        @block.sync
        def _(sp):
            sp.dma_start(c.dram["out"].rearrange("(t p) d -> p t d", p=P), c.x[:, :, :]).then_inc(stored, 16)
            sp.wait_ge(stored, 16)



def stage_conv_branch(c):
    nc = c.nc
    with c.scope() as s:
        ncol = NBLK + 1
        xT = s.sb("cv_xT", [P, BATCH, CPAD + SEQ])
        valid = s.sb("cv_valid", [1, CPAD + SEQ])
        w_in = s.sb("cv_w_in", [P, 3 * P])
        b_in = s.sb("cv_b_in", [1, 3 * P])
        w_out = s.sb("cv_w_out", [P, P])
        cols = s.sb("cv_cols", [P, 3])
        stat = s.sb("cv_stat", [P, 6, TILES])
        n2 = c.y[:, :].rearrange("p (t d) -> p t d", d=P)
        toep = [s.sb(f"cv_toep{i}", [P, CBLK, P]) for i in range(2)]
        tail = s.sb("cv_tail", [CBLK, CBLK, P])
        win = s.sb("cv_win", [P, P, BATCH, ncol])
        gate = s.sb("cv_gate", [P, 2 * P, BATCH, NBLK])
        x2 = gate[:, P:2 * P, :, :]
        yT = s.sb("cv_yT", [P, BATCH, SEQ])
        bank = [s.ps(f"cv_bank{i}", [P, 512]) for i in range(8)]
        loaded, zeroed = s.sem("cv_loaded"), s.sem("cv_zeroed")
        taps_in = [s.sem(f"cv_taps{i}") for i in range(2)]
        step_done, var_ready, root_ready = s.sem("cv_step"), s.sem("cv_var"), s.sem("cv_root")
        n2_ready, turned, xT_ready = s.sem("cv_n2r"), s.sem("cv_turned"), s.sem("cv_xTr")
        projected, copied = s.sem("cv_proj"), [s.sem(f"cv_copied{i}") for i in range(2)]
        conv_done, gated = [s.sem(f"cv_conv{i}") for i in range(2)], [s.sem(f"cv_gated{i}") for i in range(2)]
        shifted_act, shifted_pool = s.sem("cv_sha"), s.sem("cv_shp")
        y_turned, yT_ready, out_done = s.sem("cv_yt"), s.sem("cv_ytr"), s.sem("cv_out")
        block = s.block()
        GATES = slice(CPAD, P)
        CH = 8
        BLKS = BATCH * NBLK
        Q3 = slice(96, 128)

        @block.sync
        def _(sp):
            for i, taps in enumerate(("k0T", "k1T")):
                k = c.dram[taps]
                sp.dma_start(toep[i][:, :, :], dram_view(k, (2 * CBLK - 1) * P, [[P, P], [-P, CBLK], [1, P]])).then_inc(taps_in[i], 16)
                if i == 1:
                    sp.wait_ge(conv_done[0], P // 8)
                sp.dma_start(tail[:, :, :], dram_view(k, (CBLK - 1) * P, [[P, CBLK], [-P, CBLK], [1, P]])).then_inc(taps_in[i], 16)

        @block.gpsimd
        def _(pool):
            nc.gpsimd.memset(xT[:, :, 0:CPAD], 0.0).then_inc(zeroed, 1)
            nc.gpsimd.memset(valid[:, 0:CPAD], 0.0).then_inc(zeroed, 1)
            nc.gpsimd.memset(valid[:, CPAD:], 1.0).then_inc(zeroed, 1)
            if True:
                nc.gpsimd.memset(win[:, :, :, 0:CPAD // CBLK + 1], 0.0).then_inc(zeroed, 1)
            for n in range(P // CH):
                pool.wait_ge(gated[0], n + 1)
                ch = slice(n * CH, (n + 1) * CH)
                nc.gpsimd.tensor_copy(win[64:96, ch, :, 2:ncol], win[Q3, ch, :, 1:ncol - 1]).then_inc(shifted_pool, 1)

        @block.vector
        def _(dve):
            before_root, after_root = norm_steps(nc, dve, step_done, c.xn[:, :, :], n2,
                                                 yT[:, :, :].rearrange("p b (t d) -> p (b t) d", d=P), stat)
            before_root().then_inc(var_ready, 1)
            dve.wait_ge(root_ready, 1)
            after_root().then_inc(n2_ready, 1)
            dve.wait_ge(zeroed, 4)
            for a in range(0, BLKS, 2):
                dve.wait_ge(projected, a + 1)
                nc.vector.tensor_copy(win[:, :, a // NBLK, 1 + a % NBLK], bank[a % 8][:, 0:P])
                nc.vector.tensor_copy(gate[Q3, :, a // NBLK, a % NBLK], bank[a % 8][Q3, P:3 * P]).then_inc(copied[0], 1)
            for i in range(2):
                dve.wait_ge(copied[i], BLKS // 2)
            for i in range(2):
                for n in range(P // CH):
                    dve.wait_ge(conv_done[i], n + 1)
                    ch = slice(n * CH, (n + 1) * CH)
                    src = bank[n % 4][Q3, :].rearrange("p (d b a) -> p d b a", b=BATCH, a=NBLK)
                    dst = win[Q3, ch, :, 1:ncol] if i == 0 else x2[Q3, ch, :, :]
                    nc.vector.tensor_tensor(dst, src, gate[Q3, slice(i * P + n * CH, i * P + (n + 1) * CH), :, :],
                                            ALU.mult).then_inc(gated[i], 1)

        @block.scalar
        def _(act):
            for dst, name in ((w_in, "L0_W_in"), (b_in, "L0_b_in"), (w_out, "L0_W_out"), (cols, "L0_cols")):
                act.dma_start(dst[:, :], c.dram[name]).then_inc(loaded, 16)
            act.wait_ge(var_ready, 1)
            nc.scalar.activation(stat[:, 4, :], stat[:, 3, :], ACT.Sqrt).then_inc(root_ready, 1)
            act.wait_ge(loaded, 64)
            per = SEQ // GRP
            for g in range(GROUPS):
                act.wait_ge(turned, g + 1)
                at = CPAD + (g % per) * GRP
                nc.scalar.activation(xT[:, g // per, at:at + GRP], bank[g][:, :], ACT.Identity,
                                     bias=cols[:, 1:2], scale=cols[:, 0:1]).then_inc(xT_ready, 1)
            for a in range(1, BLKS, 2):
                act.wait_ge(projected, a + 1)
                nc.scalar.activation(win[:, :, a // NBLK, 1 + a % NBLK], bank[a % 8][:, 0:P], ACT.Copy)
                nc.scalar.activation(gate[Q3, :, a // NBLK, a % NBLK], bank[a % 8][Q3, P:3 * P], ACT.Copy).then_inc(copied[1], 1)
            for n in range(P // CH):
                act.wait_ge(gated[0], n + 1)
                ch = slice(n * CH, (n + 1) * CH)
                nc.scalar.activation(win[32:64, ch, :, 3:ncol], win[Q3, ch, :, 1:ncol - 2], ACT.Copy)
                nc.scalar.activation(win[0:32, ch, :, 4:ncol], win[Q3, ch, :, 1:ncol - 3], ACT.Copy).then_inc(shifted_act, 1)
            for g in range(GROUPS):
                act.wait_ge(y_turned, g + 1)
                nc.scalar.activation(yT[:, g // per, (g % per) * GRP:(g % per + 1) * GRP], bank[4 + g][:, :],
                                     ACT.Copy).then_inc(yT_ready, 1)
            for g in range(GROUPS):
                act.wait_ge(out_done, g + 1)
                nc.scalar.activation(c.y[:, g * GRP:(g + 1) * GRP], bank[g][:, :], ACT.Identity, bias=cols[:, 2:3])

        @block.tensor
        def _(pe):
            pe.wait_ge(n2_ready, 1)
            for t in range(TILES):
                g, k = divmod(t, GRP // P)
                ins = nc.tensor.transpose(bank[g][:, k * P:(k + 1) * P], n2[:, t, :], c.ident[:, :])
                if k == GRP // P - 1:
                    ins.then_inc(turned, 1)
            pe.wait_ge(xT_ready, GROUPS)
            pe.wait_ge(zeroed, 4)
            pe.wait_ge(loaded, 64)
            for a in range(BLKS):
                if a >= 8:
                    pe.wait_ge(copied[a % 2], (a - 8) // 2 + 1)
                b, at = a // NBLK, (a % NBLK) * CBLK
                nc.tensor.matmul(bank[a % 8][:, 0:3 * P], xT[:, b, at:at + CWIN], w_in[:, :], start=True, stop=False)
                nc.tensor.matmul(bank[a % 8][:, 0:3 * P], valid[:, at:at + CWIN], b_in[:, :],
                                 start=False, stop=True).then_inc(projected, 1)
            for k in range(2):
                pe.wait_ge(copied[k], BLKS // 2)
            for i in range(2):
                pe.wait_ge(taps_in[i], 32)
                for n in range(P // CH):
                    if n >= 4:
                        pe.wait_ge(gated[i], n - 3)
                    elif i == 1:
                        pe.wait_ge(gated[0], P // CH)
                    if i == 1:
                        pe.wait_ge(shifted_act, n + 1)
                        pe.wait_ge(shifted_pool, n + 1)
                    for k in range(CH):
                        d = n * CH + k
                        out = bank[n % 4][Q3, k * BLKS:(k + 1) * BLKS].rearrange("p (b a) -> p b a", b=BATCH)
                        nc.tensor.matmul(out, toep[i][:, :, d],
                                         win[:, d, :, 1:ncol], start=True, stop=False)
                        ins = nc.tensor.matmul(out, tail[:, :, d],
                                               win[0:CBLK, d, :, 0:ncol - 1], start=False, stop=True)
                    ins.then_inc(conv_done[i], 1)
            pe.wait_ge(gated[1], P // CH)
            for a in range(BLKS):
                g, k = divmod(a, GRP // CBLK)
                ins = nc.tensor.transpose(bank[4 + g][:, k * CBLK:(k + 1) * CBLK],
                                          x2[Q3, :, a // NBLK, a % NBLK], c.ident[Q3, Q3])
                if k == GRP // CBLK - 1:
                    ins.then_inc(y_turned, 1)
            per = SEQ // GRP
            for g in range(GROUPS):
                pe.wait_ge(yT_ready, g + 1)
                nc.tensor.matmul(bank[g][:, :], w_out[:, :], yT[:, g // per, (g % per) * GRP:(g % per + 1) * GRP],
                                 start=True, stop=True).then_inc(out_done, 1)



def rank_below(nc, link, score, lower, work, rank):
    earlier, equal = work
    shape = [P, TILES, 8, 8]
    of_j = score.unsqueeze(2).to_broadcast(shape)
    of_i = score.unsqueeze(3).to_broadcast(shape)
    link(nc.vector.tensor_tensor(equal, of_j, of_i, ALU.is_equal))
    link(nc.vector.tensor_tensor(equal, equal, lower.unsqueeze(1).to_broadcast(shape), ALU.mult))
    link(nc.vector.tensor_tensor(earlier, of_j, of_i, ALU.is_gt))
    link(nc.vector.tensor_tensor(earlier, earlier, equal, ALU.add))
    link(nc.vector.tensor_reduce(out=rank, in_=earlier, op=ALU.add, axis=AX.X))


def store_rows(sp, c, rows, shares, experts, copies, shared_rows, wait_rows, stored):
    n = 0
    for k in range(copies):
        sp.dma_start(rows.rearrange("(e k) n -> e k n", k=copies)[0:experts, k, :], shares).then_inc(stored, 16)
        n += 16
    sp.dma_start(rows[experts * copies:experts * copies + shared_rows, :], c.dram["ones"][0:shared_rows, :]).then_inc(stored, 16)
    n += 16
    sp.wait_ge(stored, n)


def stage_route_top2(c, tag, softmax, copies, rows):
    nc = c.nc
    E = 8
    with c.scope() as s:
        w = s.sb(f"{tag}_w", [P, E])
        bias = s.sb(f"{tag}_bias", [P, E])
        lower = s.sb(f"{tag}_lower", [P, E, E])
        logit = s.sb(f"{tag}_logit", [P, TILES, E])
        score = s.sb(f"{tag}_score", [P, TILES, E]) if not softmax else logit
        earlier, equal = s.sb(f"{tag}_earlier", [P, TILES, E, E]), s.sb(f"{tag}_equal", [P, TILES, E, E])
        rank = s.sb(f"{tag}_rank", [P, TILES, E])
        share = s.sb(f"{tag}_share", [P, TILES, E])
        stat = s.sb(f"{tag}_stat", [P, 3, TILES])
        shares = s.sb(f"{tag}_shares", [E, TOK])
        pl = s.ps(f"{tag}_pl", [P, TILES, E])
        pt = [s.ps(f"{tag}_pt{g}", [E, GRP]) for g in range(GROUPS)]
        loaded, logits_ready, step_done = s.sem(f"{tag}_loaded"), s.sem(f"{tag}_logits"), s.sem(f"{tag}_step")
        act_in, act_out, share_ready = s.sem(f"{tag}_actin"), s.sem(f"{tag}_actout"), s.sem(f"{tag}_share_r")
        turned, rows_ready, stored = s.sem(f"{tag}_turned"), s.sem(f"{tag}_rows"), s.sem(f"{tag}_stored")
        block = s.block()

        @block.sync
        def _(sp):
            sp.dma_start(w[:, :], c.dram[f"{tag}_w"]).then_inc(loaded, 16)
            sp.dma_start(bias[:, :], c.dram[f"{tag}_b"].to_broadcast([P, E])).then_inc(loaded, 16)
            sp.dma_start(lower[:, :, :], c.dram["lower"].to_broadcast([P, E, E])).then_inc(loaded, 16)
            sp.wait_ge(rows_ready, GROUPS)
            store_rows(sp, c, rows, shares[:, :], E, copies, 2 * copies if copies == 1 else copies, None, stored)

        @block.tensor
        def _(pe):
            pe.wait_ge(loaded, 48)
            for t in range(TILES):
                ins = nc.tensor.matmul(pl[:, t, :], c.xnT[:, t * P:(t + 1) * P], w[:, :], start=True, stop=True)
            ins.then_inc(logits_ready, 1)
            pe.wait_ge(share_ready, 1)
            for t in range(TILES):
                g, k = divmod(t, GRP // P)
                ins = nc.tensor.transpose(pt[g][:, k * P:(k + 1) * P], share[:, t, :], c.ident[:, :])
                if k == GRP // P - 1:
                    ins.then_inc(turned, 1)

        @block.vector
        def _(dve):
            count = [0]

            def link(ins):
                count[0] += 1
                ins.then_inc(step_done, 1)
                dve.wait_ge(step_done, count[0])

            dve.wait_ge(loaded, 48)
            dve.wait_ge(logits_ready, 1)
            link(nc.vector.tensor_tensor(logit[:, :, :], pl[:, :, :], bias[:, :].unsqueeze(1).to_broadcast([P, TILES, E]), ALU.add))
            if softmax:
                link(nc.vector.tensor_reduce(out=stat[:, 0, :], in_=logit[:, :, :], op=ALU.max, axis=AX.X))
                nc.vector.tensor_tensor(share[:, :, :], logit[:, :, :], over_last(stat[:, 0, :], E), ALU.subtract).then_inc(act_in, 1)
            else:
                nc.vector.memset(stat[:, 0, :], 0.0).then_inc(act_in, 1)
                dve.wait_ge(act_out, 1)
            rank_below(nc, link, score[:, :, :], lower[:, :, :], (earlier[:, :, :, :], equal[:, :, :, :]), rank[:, :, :])
            link(nc.vector.tensor_scalar(rank[:, :, :], rank[:, :, :], 1.5, None, ALU.is_lt))
            dve.wait_ge(act_out, 1)
            src = share if softmax else score
            link(nc.vector.tensor_tensor(share[:, :, :], src[:, :, :], rank[:, :, :], ALU.mult))
            link(nc.vector.tensor_reduce(out=stat[:, 1, :], in_=share[:, :, :], op=ALU.add, axis=AX.X))
            link(nc.vector.reciprocal(stat[:, 2, :], stat[:, 1, :]))
            nc.vector.tensor_tensor(share[:, :, :], share[:, :, :], over_last(stat[:, 2, :], E), ALU.mult).then_inc(share_ready, 1)
            for g in range(GROUPS):
                dve.wait_ge(turned, g + 1)
                nc.vector.tensor_copy(shares[:, g * GRP:(g + 1) * GRP], pt[g][:, :]).then_inc(rows_ready, 1)

        @block.scalar
        def _(act):
            act.wait_ge(act_in, 1)
            if softmax:
                nc.scalar.activation(share[:, :, :], share[:, :, :], ACT.Exp).then_inc(act_out, 1)
            else:
                nc.scalar.activation(score[:, :, :], logit[:, :, :], ACT.Sigmoid).then_inc(act_out, 1)


def stage_route_grouped(c, rows):
    nc = c.nc
    E, G = 64, 8
    M = E // G
    with c.scope() as s:
        w = s.sb("r0_w_sb", [P, E])
        bias = s.sb("r0_bias", [P, E])
        lower = s.sb("r0_lower", [P, G, G])
        score = s.sb("r0_score", [P, TILES, E])
        pick = s.sb("r0_pick", [P, TILES, E])
        left = s.sb("r0_left", [P, TILES, E])
        flag = s.sb("r0_flag", [P, TILES, E])
        top = s.sb("r0_top", [P, TILES, 8])
        group = s.sb("r0_group", [P, 5, TILES * G])
        earlier, equal = s.sb("r0_earlier", [P, TILES, G, G]), s.sb("r0_equal", [P, TILES, G, G])
        rank = s.sb("r0_rank", [P, TILES, G])
        stat = s.sb("r0_stat", [P, 3, TILES])
        shares = s.sb("r0_shares", [E, TOK])
        pl = [s.ps(f"r0_pl{i}", [P, TILES // 2, E]) for i in range(2)]
        pt = [s.ps(f"r0_pt{g}", [E, GRP]) for g in range(GROUPS)]
        loaded, logits_ready, step_done = s.sem("r0_loaded"), s.sem("r0_logits"), s.sem("r0_step")
        scores_ready, share_ready = s.sem("r0_scores"), s.sem("r0_share_r")
        turned, rows_ready, stored = s.sem("r0_turned"), s.sem("r0_rows"), s.sem("r0_stored")
        block = s.block()

        @block.sync
        def _(sp):
            sp.dma_start(w[:, :], c.dram["r0_w"]).then_inc(loaded, 16)
            sp.dma_start(bias[:, :], c.dram["r0_b"].to_broadcast([P, E])).then_inc(loaded, 16)
            sp.dma_start(lower[:, :, :], c.dram["lower"].to_broadcast([P, G, G])).then_inc(loaded, 16)
            sp.wait_ge(rows_ready, GROUPS)
            store_rows(sp, c, rows, shares[:, :], E, 1, 2, None, stored)

        @block.tensor
        def _(pe):
            pe.wait_ge(loaded, 48)
            for t in range(TILES):
                i, k = divmod(t, TILES // 2)
                ins = nc.tensor.matmul(pl[i][:, k, :], c.xnT[:, t * P:(t + 1) * P], w[:, :], start=True, stop=True)
                if k == TILES // 2 - 1:
                    ins.then_inc(logits_ready, 1)
            pe.wait_ge(share_ready, 1)
            for t in range(TILES):
                g, k = divmod(t, GRP // P)
                ins = nc.tensor.transpose(pt[g][:, k * P:(k + 1) * P], pick[:, t, :], c.ident[:, :])
                if k == GRP // P - 1:
                    ins.then_inc(turned, 1)

        @block.scalar
        def _(act):
            for i in range(2):
                act.wait_ge(logits_ready, i + 1)
                half = slice(i * TILES // 2, (i + 1) * TILES // 2)
                nc.scalar.activation(score[:, half, :], pl[i][:, :, :], ACT.Sigmoid).then_inc(scores_ready, 1)

        @block.vector
        def _(dve):
            count = [0]

            def link(ins):
                count[0] += 1
                ins.then_inc(step_done, 1)
                dve.wait_ge(step_done, count[0])

            v = nc.vector
            dve.wait_ge(loaded, 48)
            dve.wait_ge(scores_ready, 2)
            link(v.tensor_tensor(pick[:, :, :], score[:, :, :], bias[:, :].unsqueeze(1).to_broadcast([P, TILES, E]), ALU.add))
            grouped = pick[:, :, :].rearrange("p t (g m) -> p (t g) m", m=M)
            flags = flag[:, :, :].rearrange("p t (g m) -> p (t g) m", m=M)
            best, second, number, best_again, total = (group[:, i, :] for i in range(5))
            link(v.tensor_reduce(out=best, in_=grouped, op=ALU.max, axis=AX.X))
            link(v.tensor_tensor(flags, grouped, over_last(best, M), ALU.is_equal))
            link(v.tensor_reduce(out=number, in_=flags, op=ALU.add, axis=AX.X))
            link(v.scalar_tensor_tensor(out=flag[:, :, :], in0=flag[:, :, :], scalar=MASKED, in1=pick[:, :, :], op0=ALU.mult, op1=ALU.add))
            link(v.tensor_reduce(out=second, in_=flags, op=ALU.max, axis=AX.X))
            link(v.tensor_scalar(number, number, 1.5, None, ALU.is_gt))
            link(v.tensor_scalar(number, number, -MASKED, MASKED, ALU.mult, ALU.add))
            link(v.tensor_tensor(best_again, number, best, ALU.add))
            link(v.tensor_tensor(second, second, best_again, ALU.max))
            link(v.tensor_tensor(total, best, second, ALU.add))
            rank_below(nc, link, total.rearrange("p (t g) -> p t g", g=G), lower[:, :, :],
                       (earlier[:, :, :, :], equal[:, :, :, :]), rank[:, :, :])
            link(v.tensor_scalar(rank[:, :, :], rank[:, :, :], 3.5, None, ALU.is_lt))
            link(v.tensor_tensor(grouped, grouped, over_last(rank[:, :, :].rearrange("p t g -> p (t g)"), M), ALU.mult))
            link(v.tensor_scalar(pick[:, :, :], pick[:, :, :], 0.0, None, ALU.add))
            for t in range(TILES):
                ins = v.max(out=top[:, t, :], in_=pick[:, t, :])
            link(ins)
            for t in range(TILES):
                ins = v.match_replace(out=left[:, t, :], in_to_replace=top[:, t, :], in_values=pick[:, t, :], imm_value=3 * MASKED)
            link(ins)
            link(v.tensor_tensor(flag[:, :, :], pick[:, :, :], left[:, :, :], ALU.not_equal))
            link(v.tensor_tensor(pick[:, :, :], flag[:, :, :], score[:, :, :], ALU.mult))
            link(v.tensor_reduce(out=stat[:, 0, :], in_=pick[:, :, :], op=ALU.add, axis=AX.X))
            link(v.tensor_scalar(stat[:, 1, :], stat[:, 0, :], 1e-20, None, ALU.add))
            link(v.reciprocal(stat[:, 2, :], stat[:, 1, :]))
            link(v.tensor_scalar(stat[:, 2, :], stat[:, 2, :], 2.5, None, ALU.mult))
            v.tensor_tensor(pick[:, :, :], pick[:, :, :], over_last(stat[:, 2, :], E), ALU.mult).then_inc(share_ready, 1)
            for g in range(GROUPS):
                dve.wait_ge(turned, g + 1)
                v.tensor_copy(shares[:, g * GRP:(g + 1) * GRP], pt[g][:, :]).then_inc(rows_ready, 1)



def stage_experts(c, tag, weights, rows, chunks):
    nc = c.nc
    HB = 2
    with c.scope() as s:
        w_gu = [s.sb(f"{tag}_gu{i}", [P, 2 * P]) for i in range(HB)]
        w_dn = [s.sb(f"{tag}_dn{i}", [P, P]) for i in range(HB)]
        share = [s.sb(f"{tag}_share{i}", [P, TOK]) for i in range(HB)]
        hidden = [s.sb(f"{tag}_hidden{i}", [P, TOK]) for i in range(HB)]
        silu = [s.sb(f"{tag}_silu{i}", [P, GRP]) for i in range(2)]
        prod = [s.sb(f"{tag}_prod{i}", [P, GRP]) for i in range(2)]
        zeros = s.sb(f"{tag}_zeros", [P, GRP], BF16)
        gate = [s.ps(f"{tag}_pg{i}", [P, GRP]) for i in range(2)]
        up = [s.ps(f"{tag}_pu{i}", [P, GRP]) for i in range(2)]
        down = [s.ps(f"{tag}_pd{g}", [P, GRP]) for g in range(GROUPS)]
        gu_in, dn_in = [s.sem(f"{tag}_gu_in{i}") for i in range(HB)], [s.sem(f"{tag}_dn_in{i}") for i in range(HB)]
        share_in = [s.sem(f"{tag}_share_in{i}") for i in range(HB)]
        gu_done, silu_done, prod_done = s.sem(f"{tag}_gu_done"), s.sem(f"{tag}_silu_done"), s.sem(f"{tag}_prod_done")
        hidden_done, down_done, zeroed = s.sem(f"{tag}_hidden_done"), s.sem(f"{tag}_down_done"), s.sem(f"{tag}_zeroed")
        block = s.block()
        SET = HB * GROUPS
        half = P // 2

        def unit(k, par, g):
            return (k * HB + par) * GROUPS + g

        @block.sync
        def _(sp):
            def load(chunk, par, k):
                if k is not None:
                    sp.wait_ge(gu_done, unit(k, par, 0) - SET + GROUPS)
                sp.dma_start(w_gu[par][:, :], weights[bass.ds(chunk, 1), :, 0:2 * P].rearrange("c d n -> d (c n)")).then_inc(gu_in[par], 16)
                if k is not None:
                    sp.wait_ge(hidden_done, 2 + unit(k, par, 0) - SET + GROUPS)
                for j in range(2):
                    sp.dma_start(share[par][j * half:(j + 1) * half, :],
                                 rows[bass.ds(chunk * 2 + j, 1), :].to_broadcast([half, TOK])).then_inc(share_in[par], 16)
                if k is not None:
                    sp.wait_ge(down_done, unit(k, par, 0) + GROUPS)
                sp.dma_start(w_dn[par][:, :], weights[bass.ds(chunk, 1), :, 2 * P:3 * P].rearrange("c d n -> d (c n)")).then_inc(dn_in[par], 16)

            load(0, 0, None)
            load(1, 1, None)
            if chunks // HB > 1:
                with sp.Fori(1, chunks // HB) as k:
                    for par in range(HB):
                        load(k * HB + par, par, k)
            if chunks % HB:
                load(chunks - 1, 0, chunks // HB)

        @block.tensor
        def _(pe):
            pe.wait_ge(zeroed, 1)
            for g in range(GROUPS):
                ins = nc.tensor.matmul(down[g][:, :], zeros[:, 0:P], zeros[:, :], start=True, stop=False, skip_group_check=True)
            ins.then_inc(down_done, SET)

            def gate_up(k, par, g):
                n = unit(k, par, g)
                if g == 0:
                    pe.wait_ge(gu_in[par], 16 * (k + 1))
                pe.wait_ge(prod_done, n + 1)
                cols = c.xnT[:, g * GRP:(g + 1) * GRP]
                nc.tensor.matmul(gate[g % 2][:, :], w_gu[par][:, 0:P], cols, start=True, stop=True)
                nc.tensor.matmul(up[g % 2][:, :], w_gu[par][:, P:2 * P], cols, start=True, stop=True).then_inc(gu_done, 1)

            def project(k, par, g, last=False):
                n = unit(k, par, g)
                if g == 0:
                    pe.wait_ge(dn_in[par], 16 * (k + 1))
                pe.wait_ge(hidden_done, n + 3)
                nc.tensor.matmul(down[g][:, :], w_dn[par][:, :], hidden[par][:, g * GRP:(g + 1) * GRP],
                                 start=False, stop=last, skip_group_check=True).then_inc(down_done, 1)

            for g in range(GROUPS):
                gate_up(0, 0, g)
            pairs = (chunks - 1) // HB
            with pe.Fori(0, pairs) as k:
                for par in range(HB):
                    for g in range(GROUPS):
                        gate_up(k + par, 1 - par, g)
                        project(k, par, g)
            if chunks % HB == 0:
                for g in range(GROUPS):
                    gate_up(pairs, 1, g)
                    project(pairs, 0, g)
                for g in range(GROUPS):
                    project(pairs, 1, g, last=True)
            else:
                for g in range(GROUPS):
                    project(pairs, 0, g, last=True)

        def over_units(eng, step):
            with eng.Fori(0, chunks // HB) as k:
                for par in range(HB):
                    for g in range(GROUPS):
                        step(k, par, g)
            if chunks % HB:
                for g in range(GROUPS):
                    step(chunks // HB, 0, g)

        @block.scalar
        def _(act):
            def step(k, par, g):
                act.wait_ge(gu_done, unit(k, par, g) + 1)
                nc.scalar.activation(silu[g % 2][:, :], gate[g % 2][:, :], ACT.Silu).then_inc(silu_done, 1)
            over_units(act, step)
            act.wait_ge(down_done, SET + chunks * GROUPS)
            for g in range(0, GROUPS, 2):
                nc.scalar.activation(hidden[0][:, g * GRP:(g + 1) * GRP], down[g][:, :], ACT.Copy).then_inc(silu_done, 1)

        @block.vector
        def _(dve):
            nc.vector.memset(zeros[:, :], 0.0).then_inc(zeroed, 1)
            nc.vector.memset(prod[0][:, 0:1], 0.0).then_inc(prod_done, 2)
            def step(k, par, g):
                n = unit(k, par, g)
                dve.wait_ge(silu_done, n + 1)
                dve.wait_ge(hidden_done, n + 1)
                nc.vector.tensor_tensor(prod[g % 2][:, :], up[g % 2][:, :], silu[g % 2][:, :], ALU.mult).then_inc(prod_done, 1)
            over_units(dve, step)
            dve.wait_ge(down_done, SET + chunks * GROUPS)
            for g in range(1, GROUPS, 2):
                cols = slice(g * GRP, (g + 1) * GRP)
                nc.vector.tensor_tensor(c.y[:, cols], down[g][:, :], c.y[:, cols], ALU.add)
            for g in range(0, GROUPS, 2):
                cols = slice(g * GRP, (g + 1) * GRP)
                dve.wait_ge(silu_done, chunks * GROUPS + g // 2 + 1)
                nc.vector.tensor_tensor(c.y[:, cols], hidden[0][:, cols], c.y[:, cols], ALU.add)

        @block.gpsimd
        def _(pool):
            nc.gpsimd.memset(hidden[0][:, 0:1], 0.0).then_inc(hidden_done, 2)
            def step(k, par, g):
                n = unit(k, par, g)
                if g == 0:
                    pool.wait_ge(share_in[par], 32 * (k + 1))
                pool.wait_ge(prod_done, n + 3)
                pool.wait_ge(down_done, n + 1)
                cols = slice(g * GRP, (g + 1) * GRP)
                nc.gpsimd.tensor_tensor(hidden[par][:, cols], prod[g % 2][:, :], share[par][:, cols], ALU.mult).then_inc(hidden_done, 1)
            over_units(pool, step)



F32R = mybir.dt.float32r
HI, MID, LO = range(3)
Q_PARTS = (HI, HI, HI, MID, MID, LO)
K_PARTS = (HI, MID, LO, HI, MID, HI)


class Heads:

    def __init__(self, nc, tag, width, null):
        self.tag, self.width, self.null = tag, width, null
        self.small = width == 8
        self.together = 4 if self.small else 1
        self.out_rows = 32 if self.small else width + 1
        self.keys = SEQ + null
        self.part = BF16 if self.small else F32R
        self.rows = 6 * width if self.small else 3 * width
        self.moved = BF16 if self.small else F32
        self.q = nc.dram_tensor(f"{tag}_q_parts", (HEADS, self.rows, BATCH, SEQ), self.moved, kind="Internal").ap()
        self.k = nc.dram_tensor(f"{tag}_k_parts", (HEADS, self.rows, BATCH, self.keys), self.moved, kind="Internal").ap()
        self.v = nc.dram_tensor(f"{tag}_v_rows", (P, HEADS, TILES, self.out_rows), F32, kind="Internal").ap()
        self.o = nc.dram_tensor(f"{tag}_sums", (HEADS * self.out_rows, TOK), F32, kind="Internal").ap()
        self.inv = nc.dram_tensor(f"{tag}_inverse", (HEADS, TOK), F32, kind="Internal").ap()


def stage_project_small(c, h):
    nc, tag = c.nc, h.tag
    rope = h.null
    with c.scope() as s:
        names = ["wq", "wk", "wv"] + (["wq_turn", "wk_turn"] if rope else [])
        w = {n: s.sb(f"{tag}_{n}", [P, P]) for n in names}
        if rope:
            cos, sin = s.sb(f"{tag}_cos", [P, SEQ]), s.sb(f"{tag}_sin", [P, SEQ])
            turned = s.sb(f"{tag}_turned", [P, GRP])
        full = {n: s.sb(f"{tag}_{n}_full", [P, BATCH, SEQ if n == "q" else h.keys]) for n in "qk"}
        rest = {n: s.sb(f"{tag}_{n}_rest", list(full[n].shape)) for n in "qk"}
        part = {n: [s.sb(f"{tag}_{n}_part{i}", list(full[n].shape), BF16) for i in range(3)] for n in "qk"}
        v = s.sb(f"{tag}_v", [P, HEADS, TILES, h.out_rows])
        pq = [s.ps(f"{tag}_pq{i}", [P, GRP]) for i in range(2)]
        pt = [s.ps(f"{tag}_pt{i}", [P, GRP]) for i in range(2)]
        pv = [s.ps(f"{tag}_pv{i}", [P, P]) for i in range(4)]
        loaded, projected, copied = s.sem(f"{tag}_loaded"), s.sem(f"{tag}_projected"), s.sem(f"{tag}_copied")
        rotated, step_done = s.sem(f"{tag}_rotated"), s.sem(f"{tag}_step")
        v_done, v_copied, v_filled = s.sem(f"{tag}_v_done"), s.sem(f"{tag}_v_copied"), s.sem(f"{tag}_v_filled")
        hi_done, rest_done, mid_done, lo_done = (s.sem(f"{tag}_{n}") for n in ("hi", "rest", "mid", "lo"))
        stored = s.sem(f"{tag}_stored")
        block = s.block()
        per = SEQ // GRP
        order = [("q", g) for g in range(GROUPS)] + [("k", g) for g in range(GROUPS)]

        @block.sync
        def _(sp):
            for n in names:
                sp.dma_start(w[n][:, :], c.dram[f"{tag}_{n}"]).then_inc(loaded, 16)
            if rope:
                sp.dma_start(cos[:, :], c.dram["cos"]).then_inc(loaded, 16)
                sp.dma_start(sin[:, :], c.dram["sin"]).then_inc(loaded, 16)
                for b in range(BATCH):
                    with nc.allow_non_contiguous_dma(reason="the null key is a column"):
                        sp.dma_start(full["k"][:, b, SEQ:SEQ + 1], c.dram[f"{tag}_k_null"]).then_inc(loaded, 16)
            n = 0
            for i, (name, parts, rows) in enumerate((("q", Q_PARTS, h.q), ("k", K_PARTS, h.k))):
                for sem, p in ((hi_done, HI), (mid_done, MID), (lo_done, LO)):
                    sp.wait_ge(sem, i + 1)
                    for k in range(6):
                        if parts[k] == p:
                            for b in range(BATCH):
                                dst = rows[:, k * h.width:(k + 1) * h.width, b, :]
                                sp.dma_start(dst, part[name][p][:, b, :]).then_inc(stored, 16)
                                n += 16
            sp.wait_ge(v_copied, TILES)
            sp.wait_ge(v_filled, 2)
            sp.dma_start(h.v, v[:, :, :, :]).then_inc(stored, 16)
            sp.wait_ge(stored, n + 16)

        @block.gpsimd
        def _(pool):
            nc.gpsimd.memset(v[:, :, :, h.width + 1:], 0.0).then_inc(v_filled, 1)
            nc.gpsimd.memset(v[:, :, :, h.width:h.width + 1], 1.0).then_inc(v_filled, 1)

        @block.tensor
        def _(pe):
            pe.wait_ge(loaded, 16 * (len(names) + (4 if rope else 0)))
            for i, (name, g) in enumerate(order):
                if i >= 2:
                    pe.wait_ge(copied, i - 1)
                cols = c.xnT[:, g * GRP:(g + 1) * GRP]
                if rope:
                    nc.tensor.matmul(pt[i % 2][:, :], w[f"w{name}_turn"][:, :], cols, start=True, stop=True)
                nc.tensor.matmul(pq[i % 2][:, :], w[f"w{name}"][:, :], cols, start=True, stop=True).then_inc(projected, 1)
            for t in range(TILES):
                if t >= 4:
                    pe.wait_ge(v_copied, t - 3)
                nc.tensor.matmul(pv[t % 4][:, :], c.xnT[:, t * P:(t + 1) * P], w["wv"][:, :], start=True, stop=True).then_inc(v_done, 1)

        @block.vector
        def _(dve):
            count = [0]

            def link(ins):
                count[0] += 1
                ins.then_inc(step_done, 1)
                dve.wait_ge(step_done, count[0])

            if rope:
                dve.wait_ge(loaded, 16 * (len(names) + 4))
            for i, (name, g) in enumerate(order):
                dve.wait_ge(projected, i + 1)
                b, at = g // per, (g % per) * GRP
                dst = full[name][:, b, at:at + GRP]
                if rope:
                    if i:
                        dve.wait_ge(copied, i)
                    link(nc.vector.tensor_tensor(turned[:, :], pt[i % 2][:, :], sin[:, at:at + GRP], ALU.mult))
                    link(nc.vector.tensor_tensor(dst, pq[i % 2][:, :], cos[:, at:at + GRP], ALU.mult))
                    nc.vector.tensor_tensor(dst, dst, turned[:, :], ALU.add).then_inc(copied, 1)
                else:
                    nc.vector.tensor_copy(dst, pq[i % 2][:, :]).then_inc(copied, 1)
            for i, name in enumerate("qk"):
                dve.wait_ge(hi_done, i + 1)
                nc.vector.tensor_tensor(rest[name][:, :, :], full[name][:, :, :], part[name][HI][:, :, :], ALU.subtract).then_inc(rest_done, 1)
            for i, name in enumerate("qk"):
                dve.wait_ge(mid_done, i + 1)
                nc.vector.tensor_tensor(part[name][LO][:, :, :], rest[name][:, :, :], part[name][MID][:, :, :], ALU.subtract).then_inc(lo_done, 1)

        @block.scalar
        def _(act):
            for i, name in enumerate("qk"):
                act.wait_ge(copied, (i + 1) * GROUPS)
                nc.scalar.activation(part[name][HI][:, :, :], full[name][:, :, :], ACT.Copy).then_inc(hi_done, 1)
            for i, name in enumerate("qk"):
                act.wait_ge(rest_done, i + 1)
                nc.scalar.activation(part[name][MID][:, :, :], rest[name][:, :, :], ACT.Copy).then_inc(mid_done, 1)
            for t in range(TILES):
                act.wait_ge(v_done, t + 1)
                nc.scalar.activation(v[:, :, t, 0:h.width], pv[t % 4][:, :].rearrange("p (a d) -> p a d", d=h.width),
                                     ACT.Copy).then_inc(v_copied, 1)


def stage_project_wide(c, h, w_qk, w_v):
    nc, tag = c.nc, h.tag
    chunks = HEADS * h.width // P
    with c.scope() as s:
        w = [s.sb(f"{tag}_w{i}", [P, P]) for i in range(2)]
        wv = [s.sb(f"{tag}_wv{i}", [P, GRP]) for i in range(2)]
        hi = [s.sb(f"{tag}_hi{i}", [P, TOK], F32R) for i in range(2)]
        lo = [s.sb(f"{tag}_lo{i}", [P, TOK], F32R) for i in range(2)]
        v = s.sb(f"{tag}_v", [P, HEADS, TILES, h.out_rows])
        mark = s.sb(f"{tag}_pmark", [1, 6])
        bank = s.ps(f"{tag}_bank", [P, 2, TOK])
        w_in = [s.sem(f"{tag}_w_in{i}") for i in range(2)]
        wv_in = s.sem(f"{tag}_wv_in")
        projected, hi_done, lo_done = ([s.sem(f"{tag}_{n}{i}") for i in range(2)] for n in ("proj", "hi_done", "lo_done"))
        stored = [s.sem(f"{tag}_stored{i}") for i in range(2)]
        v_done, v_copied, v_filled, v_stored = (s.sem(f"{tag}_{n}") for n in ("v_done", "v_copied", "v_filled", "v_stored"))
        block = s.block()
        W = h.width

        def into(side, k, first, src):
            rows = (h.q, h.k)[side][bass.ds(2 * k, 2), first:first + W, :, :].rearrange("a r b n -> a r (b n)")
            return rows, src[:, :].bitcast(F32)

        @block.sync
        def _(sp):
            for i in range(2):
                sp.dma_start(wv[i][:, :], w_v[:, i * GRP:(i + 1) * GRP]).then_inc(wv_in, 16)
            with sp.Fori(0, chunks) as k:
                for side in range(2):
                    sp.wait_ge(projected[side], k + 1)
                    sp.dma_start(w[side][:, :], w_qk[bass.ds(side * chunks + k, 1), :, :].rearrange("c d n -> d (c n)")).then_inc(w_in[side], 16)
                for side in range(2):
                    sp.wait_ge(lo_done[side], k + 2)
                    for first, src in (((0, hi), (W, hi), (2 * W, lo)), ((0, hi), (W, lo), (2 * W, hi)))[side]:
                        dst, val = into(side, k, first, src[side])
                        sp.dma_start(dst, val).then_inc(stored[side], 16)
            for side in range(2):
                sp.wait_ge(stored[side], 16 + 48 * chunks)
            sp.wait_ge(v_copied, 2 * TILES)
            sp.wait_ge(v_filled, 1)
            sp.dma_start(h.v, v[:, :, :, :]).then_inc(v_stored, 16)
            sp.wait_ge(v_stored, 16)

        @block.tensor
        def _(pe):
            with pe.Fori(0, chunks) as k:
                for side in range(2):
                    pe.wait_ge(w_in[side], 16 * (k + 1))
                    pe.wait_ge(lo_done[side], k + 1)
                    for g in range(GROUPS):
                        ins = nc.tensor.matmul(bank[:, side, g * GRP:(g + 1) * GRP], w[side][:, :],
                                               c.xnT[:, g * GRP:(g + 1) * GRP], start=True, stop=True)
                    ins.then_inc(projected[side], 1)
            pe.wait_ge(wv_in, 32)
            for side in range(2):
                pe.wait_ge(lo_done[side], chunks + 1)
            for t in range(TILES):
                if t >= 2:
                    pe.wait_ge(v_copied, 2 * (t - 1))
                for i in range(2):
                    at = ((t % 2) * 2 + i) * GRP
                    nc.tensor.matmul(bank[:, 0, at:at + GRP], c.xnT[:, t * P:(t + 1) * P], wv[i][:, :],
                                     start=True, stop=True).then_inc(v_done, 1)

        @block.scalar
        def _(act):
            for side in range(2):
                for n, (sem, free) in enumerate(((projected, 1), (stored, 16), (lo_done, 1))):
                    at = 3 * side + n
                    nc.scalar.activation(mark[:, at:at + 1], c.ident[0:1, 0:1], ACT.Copy).then_inc(sem[side], free)
            with act.Fori(0, chunks) as k:
                for side in range(2):
                    act.wait_ge(projected[side], k + 2)
                    act.wait_ge(stored[side], 16 + 48 * k)
                    nc.scalar.activation(hi[side][:, :], bank[:, side, :], ACT.Copy).then_inc(hi_done[side], 1)
            for n in range(2 * TILES):
                act.wait_ge(v_done, n + 1)
                t, i = divmod(n, 2)
                at = ((t % 2) * 2 + i) * GRP
                half = HEADS // 2
                nc.scalar.activation(v[:, i * half:(i + 1) * half, t, 0:W],
                                     bank[:, 0, at:at + GRP].rearrange("p (a d) -> p a d", d=W), ACT.Copy).then_inc(v_copied, 1)

        @block.vector
        def _(dve):
            with dve.Fori(0, chunks) as k:
                for side in range(2):
                    dve.wait_ge(hi_done[side], k + 1)
                    nc.vector.tensor_tensor(lo[side][:, :], bank[:, side, :], hi[side][:, :].bitcast(F32), ALU.subtract).then_inc(lo_done[side], 1)

        @block.gpsimd
        def _(pool):
            nc.gpsimd.memset(v[:, :, :, W:W + 1], 1.0).then_inc(v_filled, 1)



def stage_attend(c, h, scale):
    nc, tag, G, W = c.nc, h.tag, h.together, h.width
    units = HEADS // G * BATCH
    KT = SEQ // P
    steps = ([KT] if h.null else []) + list(range(KT))
    NS = len(steps)
    if h.small:
        terms, max_row, max_term, lead = [97], 96, 0, 96
    else:
        terms, max_row, max_term, lead = [P, 96], W, 1, P
    NT = len(terms)
    with c.scope() as s:
        q = [s.sb(f"{tag}_q{i}", [P, NT, G, SEQ], h.part) for i in range(2)]
        k = [s.sb(f"{tag}_k{i}", [P, NT, G, h.keys], h.part) for i in range(2)]
        v = [s.sb(f"{tag}_vv{i}", [P, G, KT, h.out_rows]) for i in range(2)]
        v_null = [s.sb(f"{tag}_vn{i}", [P, G, h.out_rows]) for i in range(2)] if h.null else None
        e = [s.sb(f"{tag}_e{i}", [P, G, SEQ]) for i in range(2)]
        neg_max = s.sb(f"{tag}_neg_max", [P, G, KT])
        max_rows = s.sb(f"{tag}_max_rows", [G * KT, P], h.part)
        out_sb = s.sb(f"{tag}_out", [P, SEQ])
        mark = s.sb(f"{tag}_mark", [1, 4])
        above = s.sb(f"{tag}_above", [P, P])
        below = s.sb(f"{tag}_below", [P, P])
        above_b, below_b, ident_b = (s.sb(f"{tag}_{n}", [P, P], BF16) for n in ("above_b", "below_b", "ident_b"))
        ps = [s.ps(f"{tag}_ps{i}", [P, SEQ]) for i in range(2)]
        pm = s.ps(f"{tag}_pm", [P, SEQ])
        po = s.ps(f"{tag}_po", [P, SEQ])
        OUT = slice(0, P if h.small else W + 1)
        consts_in, filled, masks_ready = s.sem(f"{tag}_consts"), s.sem(f"{tag}_filled"), s.sem(f"{tag}_masks")
        FILLS = 6 + 4 * h.null
        loaded = [s.sem(f"{tag}_ld{i}") for i in range(2)]
        scored, exp_done, summed = s.sem(f"{tag}_scored"), s.sem(f"{tag}_exp"), s.sem(f"{tag}_summed")
        trial, reduced = s.sem(f"{tag}_trial"), s.sem(f"{tag}_reduced")
        max_turned, max_copied, max_in = s.sem(f"{tag}_mt"), s.sem(f"{tag}_mc"), s.sem(f"{tag}_mi")
        out_copied, out_stored = s.sem(f"{tag}_oc"), s.sem(f"{tag}_os")
        block = s.block()
        NR = KT * G + (1 if h.null else 0)

        def pieces(lo):
            return [(a, z) for a, z in ((max(lo, 0), GRP), (max(lo, GRP), SEQ)) if a < z]

        @block.sync
        def _(sp):
            sp.dma_start(above[:, :], c.dram["mask_above"]).then_inc(consts_in, 16)
            sp.dma_start(below[:, :], c.dram["mask_below"]).then_inc(consts_in, 16)
            sp.wait_ge(filled, FILLS)

            def load(i, b):
                heads = bass.ds(i * G, G)
                if h.small:
                    sp.dma_start(q[b][0:h.rows, 0, :, :], h.q[heads, :, b, :].rearrange("g r n -> r g n")).then_inc(loaded[b], 16)
                    sp.dma_start(k[b][0:h.rows, 0, :, :], h.k[heads, :, b, :].rearrange("g r n -> r g n")).then_inc(loaded[b], 16)
                else:
                    for dst, src in ((q, h.q), (k, h.k)):
                        sp.dma_start(dst[b][:, 0, 0, :].bitcast(F32), src[heads, 0:P, b, :].rearrange("g r n -> (g r) n")).then_inc(loaded[b], 16)
                        sp.dma_start(dst[b][0:W, 1, 0, :].bitcast(F32), src[heads, P:P + W, b, :].rearrange("g r n -> (g r) n")).then_inc(loaded[b], 16)
                for g in range(G):
                    sp.dma_start(v[b][:, g, :, :], h.v[:, bass.ds(i * G + g, 1), b * KT:(b + 1) * KT, :].rearrange("p a t r -> p (a t) r")).then_inc(loaded[b], 16)
                if h.null:
                    sp.dma_start(v_null[b][0:1, :, :], c.dram[f"{tag}_v_null"][:, heads, :]).then_inc(loaded[b], 16)

            def turn(i, b, last):
                u = 2 * i + b
                if not (last and b == 1):
                    sp.wait_ge(max_copied, u + 2)
                    sp.dma_start(q[1 - b][max_row:max_row + 1, max_term, :, :].rearrange("o g n -> o (g n)").bitcast(h.moved), max_rows[:, :].bitcast(h.moved)).then_inc(max_in, 16)
                sp.wait_ge(summed, 2 + NS * (u + 1))
                if not last:
                    load(i + 1, b)
                sp.wait_ge(out_copied, 2 * (u + 2))
                first = (i * G) * h.out_rows
                sp.dma_start(h.o[bass.ds(first, OUT.stop), b * SEQ:(b + 1) * SEQ], out_sb[OUT, :]).then_inc(out_stored, 16)

            load(0, 0)
            load(0, 1)
            sp.wait_ge(max_copied, 1)
            sp.dma_start(q[0][max_row:max_row + 1, max_term, :, :].rearrange("o g n -> o (g n)").bitcast(h.moved), max_rows[:, :].bitcast(h.moved)).then_inc(max_in, 16)
            with sp.Fori(0, units // 2 - 1) as i:
                for b in range(2):
                    turn(i, b, False)
            for b in range(2):
                turn(units // 2 - 1, b, True)
            sp.wait_ge(out_stored, 16 * (units + 1))

        LOADS = 16 * ((2 if h.small else 4) + G + h.null)

        @block.gpsimd
        def _(pool):
            n = 0
            if h.null:
                for rows in (e[0], e[1], v_null[0], v_null[1]):
                    nc.gpsimd.memset(rows[:, :, :], 0.0).then_inc(filled, 1)
                    n += 1
                    pool.wait_ge(filled, n)
            for b in range(2):
                if h.small:
                    fills = ((q[b][:, 0, :, :], 0.0), (k[b][0:96, 0, :, :], 0.0), (k[b][96:97, 0, :, :], 1.0))
                else:
                    fills = ((q[b][W:96, 1, :, :], 0.0), (k[b][W:96, 1, :, :], 0.0), (k[b][W:W + 1, 1, :, :], 1.0))
                for rows, value in fills:
                    nc.gpsimd.memset(rows if h.small else rows.bitcast(F32), value).then_inc(filled, 1)
                    n += 1
                    pool.wait_ge(filled, n)

        @block.tensor
        def _(pe):
            def try_max(i, b, n, first=False):
                g, t = divmod(n, KT)
                u = 2 * i + b
                if n == 0:
                    pe.wait_ge(loaded[b], LOADS * (i + 1))
                    if not first:
                        pe.wait_ge(max_copied, u)
                if n or not first:
                    pe.wait_ge(reduced, u * NR + n)
                lhs = q[b][0:lead, 0, g, t * P:(t + 1) * P]
                for lo in range(0, (t + 1) * P, GRP):
                    hi = min(lo + GRP, (t + 1) * P)
                    nc.tensor.matmul(pm[:, lo:hi], lhs, k[b][0:lead, 0, g, lo:hi], start=True, stop=hi != (t + 1) * P)
                nc.tensor.matmul(pm[:, t * P:(t + 1) * P], ident_b[:, :], above_b[:, :], start=False, stop=True).then_inc(trial, 1)

            def end_max(i, b):
                u = 2 * i + b
                if h.null:
                    pe.wait_ge(reduced, u * NR + NR - 1)
                    for g in range(G):
                        for t in range(KT):
                            ins = nc.tensor.matmul(pm[:, g * KT + t:g * KT + t + 1], q[b][0:lead, 0, g, t * P:(t + 1) * P],
                                                   k[b][0:lead, 0, g, SEQ:SEQ + 1], start=True, stop=True)
                    ins.then_inc(trial, 1)
                pe.wait_ge(reduced, u * NR + NR)
                nc.tensor.transpose(pm[0:G * KT, 0:P], neg_max[:, :, :].rearrange("p g t -> p (g t)"), c.ident[:, :]).then_inc(max_turned, 1)

            def score(i, b, st, g):
                u = 2 * i + b
                n = u * (NS * G) + st * G + g
                if st == 0 and g == 0:
                    pe.wait_ge(max_in, 16 * (u + 1))
                pe.wait_ge(exp_done, n + 1)
                t = steps[st]
                for lo, hi in pieces(0 if t == KT else t * P):
                    rows = slice(0, 1) if t == KT else slice(0, P)
                    keys = slice(SEQ, SEQ + 1) if t == KT else slice(t * P, (t + 1) * P)
                    diag = t != KT and lo == t * P
                    for m in range(NT):
                        ins = nc.tensor.matmul(ps[(st * G + g + b * NS * G) % 2][rows, lo:hi], k[b][0:terms[m], m, g, keys],
                                               q[b][0:terms[m], m, g, lo:hi], start=m == 0, stop=m == NT - 1 and not diag)
                    if diag:
                        ins = nc.tensor.matmul(ps[(st * G + g + b * NS * G) % 2][:, lo:lo + P], ident_b[:, :], below_b[:, :], start=False, stop=True)
                ins.then_inc(scored, 1)

            def weigh(i, b, st):
                u = 2 * i + b
                t = steps[st]
                if st == 0:
                    pe.wait_ge(out_copied, 2 * u + 2)
                pe.wait_ge(exp_done, (u * NS + st + 1) * G + 2)
                for lo, hi in pieces(0 if t == KT else t * P):
                    for g in range(G):
                        lhs = v_null[b][:, g, :] if t == KT else v[b][:, g, t, :]
                        out = po[g * h.out_rows:(g + 1) * h.out_rows, lo:hi]
                        ins = nc.tensor.matmul(out, lhs, e[(b * NS + st) % 2][:, g, lo:hi], start=st == 0,
                                               stop=st == NS - 1 or (t == KT // 2 - 1 and hi == GRP), skip_group_check=True)
                ins.then_inc(summed, 1)

            def unit(i, b, ahead):
                items = list(range(KT * G)) if ahead else []
                slots = NS * G
                ni, nb = (i, 1) if b == 0 else (i + 1, 0)
                done = 0
                for st in range(NS):
                    for g in range(G):
                        score(i, b, st, g)
                        want = min(len(items), -(-len(items) * (st * G + g + 1) * 4 // (3 * slots)))
                        while done < want:
                            try_max(ni, nb, done)
                            done += 1
                    if st:
                        weigh(i, b, st - 1)
                    if ahead and done == len(items) and st * G * 4 >= 3 * (slots - G) and not ended[0]:
                        end_max(ni, nb)
                        ended[0] = True
                if ahead and not ended[0]:
                    end_max(ni, nb)
                ended[0] = False
                weigh(i, b, NS - 1)

            ended = [False]
            pe.wait_ge(filled, FILLS)
            pe.wait_ge(masks_ready, 3)
            for n in range(KT * G):
                try_max(0, 0, n, first=True)
            end_max(0, 0)
            with pe.Fori(0, units // 2 - 1) as i:
                for b in range(2):
                    unit(i, b, True)
            for b in range(2):
                unit(units // 2 - 1, b, b == 0)

        @block.scalar
        def _(act):
            for n, (sem, free) in enumerate(((exp_done, 2), (out_copied, 2), (out_stored, 16))):
                nc.scalar.activation(mark[:, n:n + 1], c.ident[0:1, 0:1], ACT.Copy).then_inc(sem, free)
            act.wait_ge(filled, FILLS)

            def unit(i, b):
                u = 2 * i + b
                for st in range(NS):
                    act.wait_ge(summed, u * NS + st + 1)
                    for g in range(G):
                        act.wait_ge(scored, u * NS * G + st * G + g + 1)
                        t = steps[st]
                        rows = slice(0, 1) if t == KT else slice(0, P)
                        lo = 0 if t == KT else t * P
                        nc.scalar.activation(e[(b * NS + st) % 2][rows, g, lo:], ps[(st * G + g + b * NS * G) % 2][rows, lo:],
                                             ACT.Exp, scale=scale).then_inc(exp_done, 1)
                act.wait_ge(summed, 2 + NS * (u + 1))
                act.wait_ge(out_stored, 16 * (u + 1))
                nc.scalar.activation(out_sb[OUT, 0:GRP], po[OUT, 0:GRP], ACT.Copy).then_inc(out_copied, 1)

            with act.Fori(0, units // 2) as i:
                for b in range(2):
                    unit(i, b)

        @block.vector
        def _(dve):
            dve.wait_ge(consts_in, 32)
            nc.vector.tensor_copy(above_b[:, :], above[:, :]).then_inc(masks_ready, 1)
            nc.vector.tensor_copy(below_b[:, :], below[:, :]).then_inc(masks_ready, 1)
            nc.vector.tensor_copy(ident_b[:, :], c.ident[:, :]).then_inc(masks_ready, 1)
            nc.vector.memset(mark[:, 3:4], 0.0).then_inc(summed, 2)

            def reduce(i, b, first=False):
                u = 2 * i + b
                for n in range(KT * G):
                    g, t = divmod(n, KT)
                    dve.wait_ge(trial, u * NR + n + 1)
                    if n == 0 and not first:
                        dve.wait_ge(max_turned, u)
                    nc.vector.tensor_reduce(out=neg_max[:, g, t:t + 1], in_=pm[:, 0:(t + 1) * P], op=ALU.max, axis=AX.X,
                                            negate=True).then_inc(reduced, 1)
                if h.null:
                    dve.wait_ge(trial, (u + 1) * NR)
                    dve.wait_ge(reduced, (u + 1) * NR - 1)
                    nc.vector.scalar_tensor_tensor(out=neg_max[:, :, :].rearrange("p g t -> p (g t)"), in0=pm[:, 0:G * KT], scalar=-1.0,
                                                   in1=neg_max[:, :, :].rearrange("p g t -> p (g t)"),
                                                   op0=ALU.mult, op1=ALU.min).then_inc(reduced, 1)
                dve.wait_ge(max_turned, u + 1)
                if not first:
                    dve.wait_ge(max_in, 16 * u)
                nc.vector.tensor_copy(max_rows[:, :], pm[0:G * KT, 0:P]).then_inc(max_copied, 1)

            def copy_out(i, b):
                u = 2 * i + b
                dve.wait_ge(summed, 2 + NS * (u + 1))
                dve.wait_ge(out_stored, 16 * (u + 1))
                nc.vector.tensor_copy(out_sb[OUT, GRP:SEQ], po[OUT, GRP:SEQ]).then_inc(out_copied, 1)

            reduce(0, 0, first=True)
            with dve.Fori(0, units // 2 - 1) as i:
                reduce(i, 1)
                copy_out(i, 0)
                reduce(i + 1, 0)
                copy_out(i, 1)
            last = units // 2 - 1
            reduce(last, 1)
            copy_out(last, 0)
            copy_out(last, 1)


def stage_attention_out(c, h, w_out):
    nc, tag = c.nc, h.tag
    chunks = HEADS * h.width // P
    per = HEADS // chunks
    with c.scope() as s:
        den = s.sb(f"{tag}_den", [P, HEADS * TOK // P])
        w = [s.sb(f"{tag}_wo{i}", [P, P]) for i in range(2)]
        num = [s.sb(f"{tag}_num{i}", [P, TOK]) for i in range(2)]
        inv = [s.sb(f"{tag}_inv{i}", [P, TOK]) for i in range(2)]
        po = [s.ps(f"{tag}_pout{g}", [P, GRP]) for g in range(GROUPS)]
        den_in, den_done, den_stored = s.sem(f"{tag}_den_in"), s.sem(f"{tag}_den_done"), s.sem(f"{tag}_den_st")
        loaded, divided, used = [s.sem(f"{tag}_oin{i}") for i in range(2)], s.sem(f"{tag}_divided"), s.sem(f"{tag}_used")
        block = s.block()
        parts = P // HEADS
        width = TOK // parts

        @block.sync
        def _(sp):
            src = dram_view(h.o, h.width * TOK, [[h.out_rows * TOK, HEADS], [width, parts], [1, width]])
            sp.dma_start(den[:, :], src).then_inc(den_in, 16)
            sp.wait_ge(den_done, 1)
            sp.dma_start(h.inv.rearrange("a (k n) -> a k n", k=parts), den[:, :]).then_inc(den_stored, 16)
            sp.wait_ge(den_stored, 16)
            for k in range(chunks):
                if k >= 2:
                    sp.wait_ge(used, k - 1)
                sp.dma_start(w[k % 2][:, :], w_out[k * P:(k + 1) * P, :]).then_inc(loaded[k % 2], 16)
                src = dram_view(h.o, k * per * h.out_rows * TOK, [[h.out_rows * TOK, per], [TOK, h.width], [1, TOK]])
                sp.dma_start(num[k % 2][:, :], src).then_inc(loaded[k % 2], 16)
                src = dram_view(h.inv, k * per * TOK, [[TOK, per], [0, h.width], [1, TOK]])
                sp.dma_start(inv[k % 2][:, :], src).then_inc(loaded[k % 2], 16)

        @block.vector
        def _(dve):
            dve.wait_ge(den_in, 16)
            nc.vector.reciprocal(den[:, :], den[:, :]).then_inc(den_done, 1)
            for k in range(chunks):
                dve.wait_ge(loaded[k % 2], 48 * (k // 2 + 1))
                nc.vector.tensor_tensor(num[k % 2][:, :], num[k % 2][:, :], inv[k % 2][:, :], ALU.mult).then_inc(divided, 1)
            dve.wait_ge(used, chunks)
            for g in range(1, GROUPS, 2):
                nc.vector.tensor_copy(c.y[:, g * GRP:(g + 1) * GRP], po[g][:, :])

        @block.scalar
        def _(act):
            act.wait_ge(used, chunks)
            for g in range(0, GROUPS, 2):
                nc.scalar.activation(c.y[:, g * GRP:(g + 1) * GRP], po[g][:, :], ACT.Copy)

        @block.tensor
        def _(pe):
            for k in range(chunks):
                pe.wait_ge(divided, k + 1)
                for g in range(GROUPS):
                    ins = nc.tensor.matmul(po[g][:, :], w[k % 2][:, :], num[k % 2][:, g * GRP:(g + 1) * GRP],
                                           start=k == 0, stop=k == chunks - 1)
                ins.then_inc(used, 1)



BLOCK = 16
HIDDEN = 352


def fp4_round(nc, link, src, sign, wait_sign, mag, level, above, stat, dst):
    v = nc.vector
    largest, inverse, half = (stat[:, i, :] for i in range(3))
    link(v.scalar_tensor_tensor(out=mag, in0=src, scalar=-1.0, in1=src, op0=ALU.mult, op1=ALU.max))
    link(v.tensor_reduce(out=largest, in_=mag, op=ALU.max, axis=AX.X))
    link(v.tensor_scalar(largest, largest, 1.0 / 6.0, 1e-12, ALU.mult, ALU.max))
    link(v.reciprocal(inverse, largest))
    link(v.tensor_scalar(half, largest, 0.5, None, ALU.mult))
    link(v.tensor_tensor(mag, mag, over_last(inverse, BLOCK), ALU.mult))
    link(v.tensor_scalar(level, mag, 5.0, 2.0, ALU.is_gt, ALU.mult))
    for step in (3.5, 2.5):
        link(v.scalar_tensor_tensor(out=level, in0=mag, scalar=step, in1=level, op0=ALU.is_gt, op1=ALU.add))
    link(v.tensor_scalar(above, mag, 1.75, None, ALU.is_gt))
    link(v.scalar_tensor_tensor(out=level, in0=level, scalar=2.0, in1=above, op0=ALU.mult, op1=ALU.add))
    for step in (1.25, 0.75, 0.25):
        link(v.scalar_tensor_tensor(out=level, in0=mag, scalar=step, in1=level, op0=ALU.is_gt, op1=ALU.add))
    link(v.tensor_tensor(level, level, over_last(half, BLOCK), ALU.mult))
    wait_sign()
    return v.tensor_tensor(dst, level, sign, ALU.mult)


def stage_fp4_ffn(c, w_gate_up, w_down):
    nc = c.nc
    with c.scope() as s:
        BT = GRP // P
        rows = 3 * P
        xq = s.sb("f4_xq", [P, TILES, P])
        xqT = s.sb("f4_xqT", [P, TOK])
        w_rows = s.sb("f4_w_rows", [P, 6, P])
        wd_rows = s.sb("f4_wd_rows", [P, HIDDEN])
        wT = s.sb("f4_wT", [P, 2, rows])
        wdT = s.sb("f4_wdT", [P, 3, P])
        hid = [s.sb(f"f4_hid{i}", [P, BT, HIDDEN]) for i in range(2)]
        hq = [s.sb(f"f4_hq{i}", [P, BT, HIDDEN]) for i in range(2)]
        hqT = s.sb("f4_hqT", [P, 3, GRP])
        silu = [s.sb(f"f4_silu{i}", [P, HIDDEN]) for i in range(2)]
        size = TILES * P
        sign, mag, level, above = (s.sb(f"f4_{n}", [P, size]) for n in ("sign", "mag", "level", "above"))
        stat = s.sb("f4_stat", [P, 3, size // BLOCK])
        gate = [s.ps(f"f4_pg{i}", [P, HIDDEN]) for i in range(2)]
        up = [s.ps(f"f4_pu{i}", [P, HIDDEN]) for i in range(2)]
        pt = [s.ps(f"f4_pt{i}", [P, GRP]) for i in range(3)]
        po = s.ps("f4_po", [P, GRP])
        loaded, step_done, signed = s.sem("f4_loaded"), s.sem("f4_step"), s.sem("f4_signed")
        rounded, turned, placed = s.sem("f4_rounded"), s.sem("f4_turned"), s.sem("f4_placed")
        gu_done, silu_done, prod_done = s.sem("f4_gu_done"), s.sem("f4_silu_done"), s.sem("f4_prod_done")
        h_turned, h_placed, down_done, added = s.sem("f4_h_turned"), s.sem("f4_h_placed"), s.sem("f4_down"), s.sem("f4_added")
        block = s.block()
        chunk = [(0, P), (P, P), (2 * P, HIDDEN - 2 * P)]

        def blocks(ap):
            return ap.rearrange("p (k m) -> p k m", m=BLOCK)

        jobs = [(c.xn[:, :, :].rearrange("p t d -> p (t d)"), xq[:, :, :].rearrange("p t d -> p (t d)")),
                (w_rows[:, :, :].rearrange("p t d -> p (t d)"), w_rows[:, :, :].rearrange("p t d -> p (t d)")),
                (wd_rows[:, :], wd_rows[:, :])]
        jobs += [(hid[g % 2][:, :, :].rearrange("p t d -> p (t d)"), hq[g % 2][:, :, :].rearrange("p t d -> p (t d)"))
                 for g in range(GROUPS)]

        @block.sync
        def _(sp):
            sp.dma_start(w_rows[:, :, :], w_gate_up.rearrange("(t p) d -> p t d", p=P)).then_inc(loaded, 16)
            sp.dma_start(wd_rows[:, :], w_down).then_inc(loaded, 16)

        @block.vector
        def _(dve):
            count = [0]

            def link(ins):
                count[0] += 1
                ins.then_inc(step_done, 1)
                dve.wait_ge(step_done, count[0])

            def job(j):
                src, dst = jobs[j]
                n = src.shape[1]
                fp4_round(nc, link, blocks(src), blocks(sign[:, 0:n]), lambda: dve.wait_ge(signed, j + 1),
                          blocks(mag[:, 0:n]), blocks(level[:, 0:n]), blocks(above[:, 0:n]),
                          stat[:, :, 0:n // BLOCK], blocks(dst)).then_inc(rounded, 1)

            def gated(g):
                if g >= 2:
                    dve.wait_ge(rounded, 3 + g - 1)
                for t in range(g * BT, (g + 1) * BT):
                    dve.wait_ge(silu_done, t + 1)
                    nc.vector.tensor_tensor(hid[g % 2][:, t % BT, :], up[t % 2][:, :], silu[t % 2][:, :], ALU.mult).then_inc(prod_done, 1)

            job(0)
            dve.wait_ge(loaded, 32)
            job(1)
            job(2)
            gated(0)
            for g in range(GROUPS):
                dve.wait_ge(prod_done, (g + 1) * BT)
                if g >= 2:
                    dve.wait_ge(h_turned, 3 * (g - 1))
                job(3 + g)
                if g + 1 < GROUPS:
                    gated(g + 1)
                dve.wait_ge(down_done, g + 1)
                cols = slice(g * GRP, (g + 1) * GRP)
                nc.vector.tensor_tensor(c.y[:, cols], po[:, :], c.y[:, cols], ALU.add).then_inc(added, 1)

        @block.scalar
        def _(act):
            def signs(j):
                if j >= 1:
                    act.wait_ge(rounded, j)
                src, _ = jobs[j]
                if j >= 3:
                    act.wait_ge(prod_done, (j - 2) * BT)
                nc.scalar.activation(sign[:, 0:src.shape[1]], src, ACT.Sign).then_inc(signed, 1)

            signs(0)
            act.wait_ge(loaded, 32)
            signs(1)
            signs(2)
            for n in range(GROUPS):
                act.wait_ge(turned, n + 1)
                nc.scalar.activation(xqT[:, n * GRP:(n + 1) * GRP], (pt + [po])[n][:, :], ACT.Copy).then_inc(placed, 1)
            for i in range(2):
                act.wait_ge(turned, GROUPS + i + 1)
                nc.scalar.activation(wT[:, i, :], pt[i][:, 0:rows], ACT.Copy).then_inc(placed, 1)
            act.wait_ge(turned, GROUPS + 3)
            nc.scalar.activation(wdT[:, 0:2, :], pt[2][:, 0:2 * P].rearrange("p (a n) -> p a n", n=P), ACT.Copy).then_inc(placed, 1)
            nc.scalar.activation(wdT[0:HIDDEN - 2 * P, 2, :], pt[2][0:HIDDEN - 2 * P, 2 * P:rows], ACT.Copy).then_inc(placed, 1)

            def silus(g):
                for t in range(g * BT, (g + 1) * BT):
                    act.wait_ge(gu_done, t + 1)
                    nc.scalar.activation(silu[t % 2][:, :], gate[t % 2][:, :], ACT.Silu).then_inc(silu_done, 1)

            silus(0)
            for g in range(GROUPS):
                signs(3 + g)
                if g + 1 < GROUPS:
                    silus(g + 1)
                for k, (_, n) in enumerate(chunk):
                    act.wait_ge(h_turned, 3 * g + k + 1)
                    if g:
                        act.wait_ge(down_done, g)
                    nc.scalar.activation(hqT[0:n, k, :], pt[k][0:n, :], ACT.Copy).then_inc(h_placed, 1)

        @block.tensor
        def _(pe):
            pe.wait_ge(rounded, 1)
            for t in range(TILES):
                g, k = divmod(t, BT)
                ins = nc.tensor.transpose((pt + [po])[g][:, k * P:(k + 1) * P], xq[:, t, :], c.ident[:, :])
                if k == BT - 1:
                    ins.then_inc(turned, 1)
            pe.wait_ge(rounded, 2)
            for i in range(2):
                pe.wait_ge(placed, i + 1)
                for k in range(3):
                    ins = nc.tensor.transpose(pt[i][:, k * P:(k + 1) * P], w_rows[:, 3 * i + k, :], c.ident[:, :])
                ins.then_inc(turned, 1)
            pe.wait_ge(rounded, 3)
            pe.wait_ge(placed, 3)
            for k, (at, n) in enumerate(chunk):
                ins = nc.tensor.transpose(pt[2][0:n, k * P:(k + 1) * P], wd_rows[:, at:at + n], c.ident[:, :])
            ins.then_inc(turned, 1)
            pe.wait_ge(placed, GROUPS + 4)

            def gate_ups(g):
                for t in range(g * BT, (g + 1) * BT):
                    if t >= 2:
                        pe.wait_ge(prod_done, t - 1)
                    tile = xqT[:, t * P:(t + 1) * P]
                    nc.tensor.matmul(gate[t % 2][:, :], tile, wT[:, 0, 0:HIDDEN], start=True, stop=True)
                    nc.tensor.matmul(up[t % 2][:, :], tile, wT[:, 1, 0:HIDDEN], start=True, stop=True).then_inc(gu_done, 1)

            gate_ups(0)
            for g in range(GROUPS):
                if g + 1 < GROUPS:
                    gate_ups(g + 1)
                pe.wait_ge(rounded, 3 + g + 1)
                for k, (at, n) in enumerate(chunk):
                    if g:
                        pe.wait_ge(h_placed, 3 * (g - 1) + k + 1)
                    for t in range(BT):
                        ins = nc.tensor.transpose(pt[k][0:n, t * P:(t + 1) * P], hq[g % 2][:, t, at:at + n], c.ident[:, :])
                    ins.then_inc(h_turned, 1)
                pe.wait_ge(h_placed, 3 * (g + 1))
                if g:
                    pe.wait_ge(added, g)
                for k, (at, n) in enumerate(chunk):
                    ins = nc.tensor.matmul(po[:, :], wdT[0:n, k, :], hqT[0:n, k, :], start=k == 0, stop=k == 2)
                ins.then_inc(down_done, 1)



def build(nc, dram):
    with ExitStack() as ctx:
        c = Chip(nc, ctx, dram)

        def share_rows(tag, chunks):
            return nc.dram_tensor(f"{tag}_shares", (2 * chunks, TOK), F32, kind="Internal").ap()

        def experts(layer, rows):
            stage_experts(c, f"e{layer}", dram[f"e{layer}_w"], rows, dram[f"e{layer}_w"].shape[0])

        stage_load(c)

        stage_norm(c, "n0")
        rows = share_rows("e0", dram["e0_w"].shape[0])
        stage_conv_branch(c)
        stage_route_grouped(c, rows)
        experts(0, rows)
        stage_add(c, "s0", also_xn=True)
        c.clear_semaphores()

        stage_norm(c, "n1")
        h = Heads(nc, "a1", 64, 0)
        stage_project_wide(c, h, dram["a1_w_qk"], dram["a1_w_v"])
        stage_attend(c, h, 64 ** -0.5)
        stage_attention_out(c, h, dram["a1_w_out"])
        stage_fp4_ffn(c, dram["f1_w_gate_up"], dram["f1_w_down"])
        stage_add(c, "s1", also_xn=False)
        c.clear_semaphores()

        stage_norm(c, "n2")
        h = Heads(nc, "a2", 8, 1)
        stage_project_small(c, h)
        stage_attend(c, h, 4 ** -0.5)
        stage_attention_out(c, h, dram["a2_w_out"])
        rows = share_rows("e2", dram["e2_w"].shape[0])
        stage_route_top2(c, "r2", True, 1, rows)
        experts(2, rows)
        stage_add(c, "s2", also_xn=False)
        c.clear_semaphores()

        stage_norm(c, "n3")
        h = Heads(nc, "a3", 8, 0)
        stage_project_small(c, h)
        stage_attend(c, h, 8 ** -0.5)
        stage_attention_out(c, h, dram["a3_w_out"])
        rows = share_rows("e3", dram["e3_w"].shape[0])
        stage_route_top2(c, "r3", False, 4, rows)
        experts(3, rows)
        stage_add(c, "s3", also_xn=False)

        stage_store(c)


def laid_out(i):
    f = np.float32
    a = {"x": i["L0_attn_x"].reshape(TOK, P)}

    a["ident"] = np.eye(P, dtype=f)
    a["ones"] = np.ones((4, TOK), f)
    a["lower"] = np.tril(np.ones((8, 8), f), -1)[None]
    a["mask_above"] = np.triu(np.full((P, P), MASKED, f), 1)
    a["mask_below"] = np.tril(np.full((P, P), MASKED, f), -1)
    pos = np.arange(SEQ, dtype=f)
    freq = (1.0 / 10000.0 ** (np.arange(0, 4, 2, dtype=f) / 4)).astype(f)
    angle = pos[None, :] * freq[:, None]
    cos, sin = np.ones((HEADS, 8, SEQ), f), np.zeros((HEADS, 8, SEQ), f)
    cos[:, 4:6] = cos[:, 6:8] = np.cos(angle)
    sin[:, 4:6], sin[:, 6:8] = -np.sin(angle), np.sin(angle)
    a["cos"], a["sin"] = cos.reshape(P, SEQ), sin.reshape(P, SEQ)

    for n in range(2):
        taps = i[f"L0_attn_k{n}"][0].T[::-1]
        a[f"k{n}T"] = np.concatenate([np.zeros((CBLK, P), f), taps, np.zeros((CBLK - 1, P), f)])
    a["L0_W_in"], a["L0_W_out"] = i["L0_attn_W_in"], i["L0_attn_W_out"]
    a["L0_b_in"] = i["L0_attn_b_in"][None]
    a["L0_cols"] = np.stack([i["L0_attn_gamma"], i["L0_attn_beta"], i["L0_attn_b_out"]], 1)
    a["r0_w"], a["r0_b"] = i["L0_ffn_router_w"].T, i["L0_ffn_e_bias"][None]

    def pairs(w):
        return w.reshape(-1, 2, P, P // 2).transpose(0, 2, 1, 3).reshape(-1, P, P)

    def joined(gate, up, down):
        return np.concatenate([gate, up, down], 2)

    a["e0_w"] = np.concatenate([
        joined(pairs(i["L0_ffn_Wg"]), pairs(i["L0_ffn_Wu"]), i["L0_ffn_Wd"].reshape(-1, P, P)),
        joined(i["L0_ffn_SWg"][None], i["L0_ffn_SWu"][None], i["L0_ffn_SWd"][None])])

    def columns(w):
        return w.reshape(P, -1, P).transpose(1, 0, 2)

    a["a1_w_qk"] = np.concatenate([columns(i["L1_attn_Wq"]), columns(i["L1_attn_Wk"])])
    a["a1_w_v"], a["a1_w_out"] = i["L1_attn_Wv"], i["L1_attn_Wo"]
    pad = np.zeros((3 * P - HIDDEN, P), f)
    a["f1_w_gate_up"] = np.concatenate([i["L1_ffn_w_gate"], pad, i["L1_ffn_w_up"], pad])
    a["f1_w_down"] = i["L1_ffn_w_down"]

    def heads(sem, geo):
        return np.concatenate([sem.reshape(-1, HEADS, 4), geo.reshape(-1, HEADS, 4)], 2).reshape(-1, P)

    def partner(geo):
        return geo.reshape(-1, HEADS, 2, 2)[:, :, ::-1].reshape(-1, HEADS * 4)

    g = {n: i[f"L2_attn_{n}"] for n in ("wq_sem", "wk_sem", "wq_geo", "wk_geo", "k_sem_null", "k_geo_null")}
    for n in ("wq", "wk"):
        a[f"a2_{n}"] = heads(g[f"{n}_sem"], g[f"{n}_geo"])
        a[f"a2_{n}_turn"] = heads(g[f"{n}_sem"], partner(g[f"{n}_geo"]))
    a["a2_wv"], a["a2_w_out"] = i["L2_attn_wv"], i["L2_attn_wo"]
    a["a2_k_null"] = heads(g["k_sem_null"][None], g["k_geo_null"][None]).T
    v_null = np.zeros((1, HEADS, 32), f)
    v_null[0, :, 0:8] = i["L2_attn_v_null"].reshape(HEADS, 8)
    v_null[0, :, 8] = 1.0
    a["a2_v_null"] = v_null
    a["r2_w"], a["r2_b"] = i["L2_ffn_router_w"], i["L2_ffn_router_b"][None]
    a["e2_w"] = np.concatenate([
        joined(pairs(i[f"L2_ffn_{n}_w1"]), pairs(i[f"L2_ffn_{n}_w3"]), i[f"L2_ffn_{n}_w2"].reshape(-1, P, P))
        for n in ("routed", "shared")])

    for n in "qkv":
        a[f"a3_w{n}"] = i[f"L3_attn_W_{n.upper()}"]
    a["a3_w_out"] = i["L3_attn_W_o"]
    a["r3_w"], a["r3_b"] = i["L3_ffn_router_w"].T, i["L3_ffn_routing_bias"][None]

    def hidden_rows(w):
        return w.reshape(-1, P, P).transpose(0, 2, 1)

    def down_columns(w):
        return w.reshape(-1, P, 2, P).transpose(0, 2, 3, 1).reshape(-1, P, P)

    a["e3_w"] = np.concatenate([
        joined(hidden_rows(i["L3_ffn_wg"]), hidden_rows(i["L3_ffn_wu"]), down_columns(i["L3_ffn_wd"])),
        joined(hidden_rows(i["L3_ffn_sg_w"]), hidden_rows(i["L3_ffn_su_w"]), down_columns(i["L3_ffn_sd_w"]))])
    return {n: np.ascontiguousarray(v) for n, v in a.items()}


def kernel(**inputs):
    import concourse.bacc as bacc
    from concourse.bass_utils import run_bass_kernel_spmd

    nc = bacc.Bacc("TRN2", target_bir_lowering=False, num_devices=1)
    arrays = laid_out({n: np.asarray(v) for n, v in inputs.items()})
    dram = {n: nc.dram_tensor(f"in_{n}", v.shape, mybir.dt.from_np(v.dtype), kind="ExternalInput").ap()
            for n, v in arrays.items()}
    dram["out"] = nc.dram_tensor("out", (TOK, P), F32, kind="ExternalOutput").ap()
    build(nc, dram)
    result = run_bass_kernel_spmd(nc, [{f"in_{n}": v for n, v in arrays.items()}], core_ids=[0])
    return result.results[0]["out"].reshape(BATCH, SEQ, P)
```

```python
from contextlib import ExitStack

import concourse.bass as bass
import numpy as np
from concourse import mybir

F32 = mybir.dt.float32
BF16 = mybir.dt.bfloat16
ALU = mybir.AluOpType
ACT = mybir.ActivationFunctionType
AX = mybir.AxisListType

P = 128
BATCH, SEQ = 2, 1024
TOK = BATCH * SEQ
TILES = TOK // P
GRP = 512
GROUPS = TOK // GRP
HEADS = 16
EPS = 1e-5
MASKED = -1e30
CBLK = 32
CWIN = 128
CPAD = CWIN - CBLK
TAPS = 128
NBLK = SEQ // CBLK


def dram_view(ap, offset, dims):
    return bass.AP(tensor=ap.tensor, offset=offset, ap=dims)


class Chip:

    def __init__(self, nc, ctx, dram):
        self.nc, self.ctx, self.dram = nc, ctx, dram
        self.taken = []

        def resident(name, shape):
            return ctx.enter_context(nc.sbuf_tensor(name, shape, F32))

        self.x = resident("x_tokens", [P, TILES, P])
        self.xn = resident("xn_tokens", [P, TILES, P])
        self.xnT = resident("xn_channels", [P, TOK])
        self.y = resident("y_channels", [P, TOK])
        self.ident = resident("identity", [P, P])

    def scope(self):
        return Scope(self)

    def semaphore(self, name):
        self.taken.append(self.nc.alloc_semaphore(name))
        return self.taken[-1]

    def clear_semaphores(self):
        self.nc.clear_and_free_semaphores(self.taken)
        self.nc.all_engine_barrier()
        self.taken = []


class Scope:

    def __init__(self, chip):
        self.chip, self.nc = chip, chip.nc

    def __enter__(self):
        self.ctx = ExitStack()
        self.ctx.__enter__()
        return self

    def __exit__(self, *exc):
        return self.ctx.__exit__(*exc)

    def sb(self, name, shape, dt=F32):
        return self.ctx.enter_context(self.nc.sbuf_tensor(f"{name}_sb", shape, dt))

    def ps(self, name, shape, dt=F32):
        return self.ctx.enter_context(self.nc.psum_tensor(name, shape, dt))

    def sem(self, name):
        return self.chip.semaphore(name)

    def block(self):
        return self.ctx.enter_context(self.nc.Block())


def over_last(ap, n):
    return ap.unsqueeze(len(ap.shape)).to_broadcast(list(ap.shape) + [n])



def stage_load(c):
    nc = c.nc
    with c.scope() as s:
        loaded = s.sem("ld_loaded")
        block = s.block()

        @block.sync
        def _(sp):
            sp.dma_start(c.x[:, :, :], c.dram["x"].rearrange("(t p) d -> p t d", p=P)).then_inc(loaded, 16)
            sp.dma_start(c.ident[:, :], c.dram["ident"]).then_inc(loaded, 16)
            sp.wait_ge(loaded, 32)


def norm_steps(nc, dve, step_done, src, dst, scratch, stat):
    count = [0]

    def link(ins):
        count[0] += 1
        ins.then_inc(step_done, 1)
        dve.wait_ge(step_done, count[0])

    def before_root():
        link(nc.vector.tensor_reduce(out=stat[:, 0, :], in_=src, op=ALU.add, axis=AX.X))
        link(nc.vector.tensor_scalar(stat[:, 1, :], stat[:, 0, :], 1.0 / P, None, ALU.mult))
        link(nc.vector.tensor_tensor(dst, src, over_last(stat[:, 1, :], P), ALU.subtract))
        link(nc.vector.tensor_tensor(scratch, dst, dst, ALU.mult))
        link(nc.vector.tensor_reduce(out=stat[:, 2, :], in_=scratch, op=ALU.add, axis=AX.X))
        return nc.vector.tensor_scalar(stat[:, 3, :], stat[:, 2, :], 1.0 / P, EPS, ALU.mult, ALU.add)

    def after_root():
        link(nc.vector.reciprocal(stat[:, 5, :], stat[:, 4, :]))
        return nc.vector.tensor_tensor(dst, dst, over_last(stat[:, 5, :], P), ALU.mult)

    return before_root, after_root


def stage_norm(c, tag):
    nc = c.nc
    with c.scope() as s:
        scratch = s.sb(f"{tag}_sq", [P, TILES, P])
        stat = s.sb(f"{tag}_stat", [P, 6, TILES])
        tp = [s.ps(f"{tag}_tp{g}", [P, GRP]) for g in range(GROUPS)]
        step_done, var_ready, root_ready = s.sem(f"{tag}_step"), s.sem(f"{tag}_var"), s.sem(f"{tag}_root")
        xn_ready, turned = s.sem(f"{tag}_xn"), s.sem(f"{tag}_turned")
        block = s.block()

        @block.vector
        def _(dve):
            before_root, after_root = norm_steps(nc, dve, step_done, c.x[:, :, :], c.xn[:, :, :], scratch[:, :, :], stat)
            before_root().then_inc(var_ready, 1)
            dve.wait_ge(root_ready, 1)
            after_root().then_inc(xn_ready, 1)
            for g in range(1, GROUPS, 2):
                dve.wait_ge(turned, g + 1)
                nc.vector.tensor_copy(c.xnT[:, g * GRP:(g + 1) * GRP], tp[g][:, :])

        @block.scalar
        def _(act):
            act.wait_ge(var_ready, 1)
            nc.scalar.activation(stat[:, 4, :], stat[:, 3, :], ACT.Sqrt).then_inc(root_ready, 1)
            for g in range(0, GROUPS, 2):
                act.wait_ge(turned, g + 1)
                nc.scalar.activation(c.xnT[:, g * GRP:(g + 1) * GRP], tp[g][:, :], ACT.Copy)

        @block.tensor
        def _(pe):
            pe.wait_ge(xn_ready, 1)
            for t in range(TILES):
                g, k = divmod(t, GRP // P)
                ins = nc.tensor.transpose(tp[g][:, k * P:(k + 1) * P], c.xn[:, t, :], c.ident[:, :])
                if k == GRP // P - 1:
                    ins.then_inc(turned, 1)


def stage_add(c, tag, also_xn):
    nc = c.nc
    with c.scope() as s:
        tp = [s.ps(f"{tag}_tp{g}", [P, GRP // P, P]) for g in range(GROUPS)]
        turned, res_added = s.sem(f"{tag}_turned"), s.sem(f"{tag}_res")
        block = s.block()

        @block.tensor
        def _(pe):
            for t in range(TILES):
                g, k = divmod(t, GRP // P)
                ins = nc.tensor.transpose(tp[g][:, k, :], c.y[:, t * P:(t + 1) * P], c.ident[:, :])
                if k == GRP // P - 1:
                    ins.then_inc(turned, 1)

        @block.vector
        def _(dve):
            if also_xn:
                nc.vector.tensor_tensor(c.x[:, :, :], c.x[:, :, :], c.xn[:, :, :], ALU.add).then_inc(res_added, 1)
                dve.wait_ge(res_added, 1)
            per = GRP // P
            for g in range(GROUPS):
                dve.wait_ge(turned, g + 1)
                nc.vector.tensor_tensor(c.x[:, g * per:(g + 1) * per, :], tp[g][:, :, :],
                                        c.x[:, g * per:(g + 1) * per, :], ALU.add)


def stage_store(c):
    nc = c.nc
    with c.scope() as s:
        stored = s.sem("st_stored")
        block = s.block()

        @block.sync
        def _(sp):
            sp.dma_start(c.dram["out"].rearrange("(t p) d -> p t d", p=P), c.x[:, :, :]).then_inc(stored, 16)
            sp.wait_ge(stored, 16)



def stage_conv_branch(c):
    nc = c.nc
    with c.scope() as s:
        ncol = NBLK + 1
        xT = s.sb("cv_xT", [P, BATCH, CPAD + SEQ])
        valid = s.sb("cv_valid", [1, CPAD + SEQ])
        w_in = s.sb("cv_w_in", [P, 3 * P])
        b_in = s.sb("cv_b_in", [1, 3 * P])
        w_out = s.sb("cv_w_out", [P, P])
        cols = s.sb("cv_cols", [P, 3])
        stat = s.sb("cv_stat", [P, 6, TILES])
        n2 = c.y[:, :].rearrange("p (t d) -> p t d", d=P)
        toep = [s.sb(f"cv_toep{i}", [P, CBLK, P]) for i in range(2)]
        tail = s.sb("cv_tail", [CBLK, CBLK, P])
        win = s.sb("cv_win", [P, P, BATCH, ncol])
        gate = s.sb("cv_gate", [P, 2 * P, BATCH, NBLK])
        x2 = gate[:, P:2 * P, :, :]
        yT = s.sb("cv_yT", [P, BATCH, SEQ])
        bank = [s.ps(f"cv_bank{i}", [P, 512]) for i in range(8)]
        loaded, zeroed = s.sem("cv_loaded"), s.sem("cv_zeroed")
        taps_in = [s.sem(f"cv_taps{i}") for i in range(2)]
        step_done, var_ready, root_ready = s.sem("cv_step"), s.sem("cv_var"), s.sem("cv_root")
        n2_ready, turned, xT_ready = s.sem("cv_n2r"), s.sem("cv_turned"), s.sem("cv_xTr")
        projected, copied = s.sem("cv_proj"), [s.sem(f"cv_copied{i}") for i in range(2)]
        conv_done, gated = [s.sem(f"cv_conv{i}") for i in range(2)], [s.sem(f"cv_gated{i}") for i in range(2)]
        shifted_act, shifted_pool = s.sem("cv_sha"), s.sem("cv_shp")
        y_turned, yT_ready, out_done = s.sem("cv_yt"), s.sem("cv_ytr"), s.sem("cv_out")
        block = s.block()
        GATES = slice(CPAD, P)
        CH = 8
        BLKS = BATCH * NBLK
        Q3 = slice(96, 128)

        @block.sync
        def _(sp):
            for i, taps in enumerate(("k0T", "k1T")):
                k = c.dram[taps]
                sp.dma_start(toep[i][:, :, :], dram_view(k, (2 * CBLK - 1) * P, [[P, P], [-P, CBLK], [1, P]])).then_inc(taps_in[i], 16)
                if i == 1:
                    sp.wait_ge(conv_done[0], P // 8)
                sp.dma_start(tail[:, :, :], dram_view(k, (CBLK - 1) * P, [[P, CBLK], [-P, CBLK], [1, P]])).then_inc(taps_in[i], 16)

        @block.gpsimd
        def _(pool):
            nc.gpsimd.memset(xT[:, :, 0:CPAD], 0.0).then_inc(zeroed, 1)
            nc.gpsimd.memset(valid[:, 0:CPAD], 0.0).then_inc(zeroed, 1)
            nc.gpsimd.memset(valid[:, CPAD:], 1.0).then_inc(zeroed, 1)
            if True:
                nc.gpsimd.memset(win[:, :, :, 0:CPAD // CBLK + 1], 0.0).then_inc(zeroed, 1)
            for n in range(P // CH):
                pool.wait_ge(gated[0], n + 1)
                ch = slice(n * CH, (n + 1) * CH)
                nc.gpsimd.tensor_copy(win[64:96, ch, :, 2:ncol], win[Q3, ch, :, 1:ncol - 1]).then_inc(shifted_pool, 1)

        @block.vector
        def _(dve):
            before_root, after_root = norm_steps(nc, dve, step_done, c.xn[:, :, :], n2,
                                                 yT[:, :, :].rearrange("p b (t d) -> p (b t) d", d=P), stat)
            before_root().then_inc(var_ready, 1)
            dve.wait_ge(root_ready, 1)
            after_root().then_inc(n2_ready, 1)
            dve.wait_ge(zeroed, 4)
            for a in range(0, BLKS, 2):
                dve.wait_ge(projected, a + 1)
                nc.vector.tensor_copy(win[:, :, a // NBLK, 1 + a % NBLK], bank[a % 8][:, 0:P])
                nc.vector.tensor_copy(gate[Q3, :, a // NBLK, a % NBLK], bank[a % 8][Q3, P:3 * P]).then_inc(copied[0], 1)
            for i in range(2):
                dve.wait_ge(copied[i], BLKS // 2)
            for i in range(2):
                for n in range(P // CH):
                    dve.wait_ge(conv_done[i], n + 1)
                    ch = slice(n * CH, (n + 1) * CH)
                    src = bank[n % 4][Q3, :].rearrange("p (d b a) -> p d b a", b=BATCH, a=NBLK)
                    dst = win[Q3, ch, :, 1:ncol] if i == 0 else x2[Q3, ch, :, :]
                    nc.vector.tensor_tensor(dst, src, gate[Q3, slice(i * P + n * CH, i * P + (n + 1) * CH), :, :],
                                            ALU.mult).then_inc(gated[i], 1)

        @block.scalar
        def _(act):
            for dst, name in ((w_in, "L0_W_in"), (b_in, "L0_b_in"), (w_out, "L0_W_out"), (cols, "L0_cols")):
                act.dma_start(dst[:, :], c.dram[name]).then_inc(loaded, 16)
            act.wait_ge(var_ready, 1)
            nc.scalar.activation(stat[:, 4, :], stat[:, 3, :], ACT.Sqrt).then_inc(root_ready, 1)
            act.wait_ge(loaded, 64)
            per = SEQ // GRP
            for g in range(GROUPS):
                act.wait_ge(turned, g + 1)
                at = CPAD + (g % per) * GRP
                nc.scalar.activation(xT[:, g // per, at:at + GRP], bank[g][:, :], ACT.Identity,
                                     bias=cols[:, 1:2], scale=cols[:, 0:1]).then_inc(xT_ready, 1)
            for a in range(1, BLKS, 2):
                act.wait_ge(projected, a + 1)
                nc.scalar.activation(win[:, :, a // NBLK, 1 + a % NBLK], bank[a % 8][:, 0:P], ACT.Copy)
                nc.scalar.activation(gate[Q3, :, a // NBLK, a % NBLK], bank[a % 8][Q3, P:3 * P], ACT.Copy).then_inc(copied[1], 1)
            for n in range(P // CH):
                act.wait_ge(gated[0], n + 1)
                ch = slice(n * CH, (n + 1) * CH)
                nc.scalar.activation(win[32:64, ch, :, 3:ncol], win[Q3, ch, :, 1:ncol - 2], ACT.Copy)
                nc.scalar.activation(win[0:32, ch, :, 4:ncol], win[Q3, ch, :, 1:ncol - 3], ACT.Copy).then_inc(shifted_act, 1)
            for g in range(GROUPS):
                act.wait_ge(y_turned, g + 1)
                nc.scalar.activation(yT[:, g // per, (g % per) * GRP:(g % per + 1) * GRP], bank[4 + g][:, :],
                                     ACT.Copy).then_inc(yT_ready, 1)
            for g in range(GROUPS):
                act.wait_ge(out_done, g + 1)
                nc.scalar.activation(c.y[:, g * GRP:(g + 1) * GRP], bank[g][:, :], ACT.Identity, bias=cols[:, 2:3])

        @block.tensor
        def _(pe):
            pe.wait_ge(n2_ready, 1)
            for t in range(TILES):
                g, k = divmod(t, GRP // P)
                ins = nc.tensor.transpose(bank[g][:, k * P:(k + 1) * P], n2[:, t, :], c.ident[:, :])
                if k == GRP // P - 1:
                    ins.then_inc(turned, 1)
            pe.wait_ge(xT_ready, GROUPS)
            pe.wait_ge(zeroed, 4)
            pe.wait_ge(loaded, 64)
            for a in range(BLKS):
                if a >= 8:
                    pe.wait_ge(copied[a % 2], (a - 8) // 2 + 1)
                b, at = a // NBLK, (a % NBLK) * CBLK
                nc.tensor.matmul(bank[a % 8][:, 0:3 * P], xT[:, b, at:at + CWIN], w_in[:, :], start=True, stop=False)
                nc.tensor.matmul(bank[a % 8][:, 0:3 * P], valid[:, at:at + CWIN], b_in[:, :],
                                 start=False, stop=True).then_inc(projected, 1)
            for k in range(2):
                pe.wait_ge(copied[k], BLKS // 2)
            for i in range(2):
                pe.wait_ge(taps_in[i], 32)
                for n in range(P // CH):
                    if n >= 4:
                        pe.wait_ge(gated[i], n - 3)
                    elif i == 1:
                        pe.wait_ge(gated[0], P // CH)
                    if i == 1:
                        pe.wait_ge(shifted_act, n + 1)
                        pe.wait_ge(shifted_pool, n + 1)
                    for k in range(CH):
                        d = n * CH + k
                        out = bank[n % 4][Q3, k * BLKS:(k + 1) * BLKS].rearrange("p (b a) -> p b a", b=BATCH)
                        nc.tensor.matmul(out, toep[i][:, :, d],
                                         win[:, d, :, 1:ncol], start=True, stop=False)
                        ins = nc.tensor.matmul(out, tail[:, :, d],
                                               win[0:CBLK, d, :, 0:ncol - 1], start=False, stop=True)
                    ins.then_inc(conv_done[i], 1)
            pe.wait_ge(gated[1], P // CH)
            for a in range(BLKS):
                g, k = divmod(a, GRP // CBLK)
                ins = nc.tensor.transpose(bank[4 + g][:, k * CBLK:(k + 1) * CBLK],
                                          x2[Q3, :, a // NBLK, a % NBLK], c.ident[Q3, Q3])
                if k == GRP // CBLK - 1:
                    ins.then_inc(y_turned, 1)
            per = SEQ // GRP
            for g in range(GROUPS):
                pe.wait_ge(yT_ready, g + 1)
                nc.tensor.matmul(bank[g][:, :], w_out[:, :], yT[:, g // per, (g % per) * GRP:(g % per + 1) * GRP],
                                 start=True, stop=True).then_inc(out_done, 1)



def rank_below(nc, link, score, lower, work, rank):
    earlier, equal = work
    shape = [P, TILES, 8, 8]
    of_j = score.unsqueeze(2).to_broadcast(shape)
    of_i = score.unsqueeze(3).to_broadcast(shape)
    link(nc.vector.tensor_tensor(equal, of_j, of_i, ALU.is_equal))
    link(nc.vector.tensor_tensor(equal, equal, lower.unsqueeze(1).to_broadcast(shape), ALU.mult))
    link(nc.vector.tensor_tensor(earlier, of_j, of_i, ALU.is_gt))
    link(nc.vector.tensor_tensor(earlier, earlier, equal, ALU.add))
    link(nc.vector.tensor_reduce(out=rank, in_=earlier, op=ALU.add, axis=AX.X))


def store_rows(sp, c, rows, shares, experts, copies, shared_rows, wait_rows, stored):
    n = 0
    for k in range(copies):
        sp.dma_start(rows.rearrange("(e k) n -> e k n", k=copies)[0:experts, k, :], shares).then_inc(stored, 16)
        n += 16
    sp.dma_start(rows[experts * copies:experts * copies + shared_rows, :], c.dram["ones"][0:shared_rows, :]).then_inc(stored, 16)
    n += 16
    sp.wait_ge(stored, n)


def stage_route_top2(c, tag, softmax, copies, rows):
    nc = c.nc
    E = 8
    with c.scope() as s:
        w = s.sb(f"{tag}_w", [P, E])
        bias = s.sb(f"{tag}_bias", [P, E])
        lower = s.sb(f"{tag}_lower", [P, E, E])
        logit = s.sb(f"{tag}_logit", [P, TILES, E])
        score = s.sb(f"{tag}_score", [P, TILES, E]) if not softmax else logit
        earlier, equal = s.sb(f"{tag}_earlier", [P, TILES, E, E]), s.sb(f"{tag}_equal", [P, TILES, E, E])
        rank = s.sb(f"{tag}_rank", [P, TILES, E])
        share = s.sb(f"{tag}_share", [P, TILES, E])
        stat = s.sb(f"{tag}_stat", [P, 3, TILES])
        shares = s.sb(f"{tag}_shares", [E, TOK])
        pl = s.ps(f"{tag}_pl", [P, TILES, E])
        pt = [s.ps(f"{tag}_pt{g}", [E, GRP]) for g in range(GROUPS)]
        loaded, logits_ready, step_done = s.sem(f"{tag}_loaded"), s.sem(f"{tag}_logits"), s.sem(f"{tag}_step")
        act_in, act_out, share_ready = s.sem(f"{tag}_actin"), s.sem(f"{tag}_actout"), s.sem(f"{tag}_share_r")
        turned, rows_ready, stored = s.sem(f"{tag}_turned"), s.sem(f"{tag}_rows"), s.sem(f"{tag}_stored")
        block = s.block()

        @block.sync
        def _(sp):
            sp.dma_start(w[:, :], c.dram[f"{tag}_w"]).then_inc(loaded, 16)
            sp.dma_start(bias[:, :], c.dram[f"{tag}_b"].to_broadcast([P, E])).then_inc(loaded, 16)
            sp.dma_start(lower[:, :, :], c.dram["lower"].to_broadcast([P, E, E])).then_inc(loaded, 16)
            sp.wait_ge(rows_ready, GROUPS)
            store_rows(sp, c, rows, shares[:, :], E, copies, 2 * copies if copies == 1 else copies, None, stored)

        @block.tensor
        def _(pe):
            pe.wait_ge(loaded, 48)
            for t in range(TILES):
                ins = nc.tensor.matmul(pl[:, t, :], c.xnT[:, t * P:(t + 1) * P], w[:, :], start=True, stop=True)
            ins.then_inc(logits_ready, 1)
            pe.wait_ge(share_ready, 1)
            for t in range(TILES):
                g, k = divmod(t, GRP // P)
                ins = nc.tensor.transpose(pt[g][:, k * P:(k + 1) * P], share[:, t, :], c.ident[:, :])
                if k == GRP // P - 1:
                    ins.then_inc(turned, 1)

        @block.vector
        def _(dve):
            count = [0]

            def link(ins):
                count[0] += 1
                ins.then_inc(step_done, 1)
                dve.wait_ge(step_done, count[0])

            dve.wait_ge(loaded, 48)
            dve.wait_ge(logits_ready, 1)
            link(nc.vector.tensor_tensor(logit[:, :, :], pl[:, :, :], bias[:, :].unsqueeze(1).to_broadcast([P, TILES, E]), ALU.add))
            if softmax:
                link(nc.vector.tensor_reduce(out=stat[:, 0, :], in_=logit[:, :, :], op=ALU.max, axis=AX.X))
                nc.vector.tensor_tensor(share[:, :, :], logit[:, :, :], over_last(stat[:, 0, :], E), ALU.subtract).then_inc(act_in, 1)
            else:
                nc.vector.memset(stat[:, 0, :], 0.0).then_inc(act_in, 1)
                dve.wait_ge(act_out, 1)
            rank_below(nc, link, score[:, :, :], lower[:, :, :], (earlier[:, :, :, :], equal[:, :, :, :]), rank[:, :, :])
            link(nc.vector.tensor_scalar(rank[:, :, :], rank[:, :, :], 1.5, None, ALU.is_lt))
            dve.wait_ge(act_out, 1)
            src = share if softmax else score
            link(nc.vector.tensor_tensor(share[:, :, :], src[:, :, :], rank[:, :, :], ALU.mult))
            link(nc.vector.tensor_reduce(out=stat[:, 1, :], in_=share[:, :, :], op=ALU.add, axis=AX.X))
            link(nc.vector.reciprocal(stat[:, 2, :], stat[:, 1, :]))
            nc.vector.tensor_tensor(share[:, :, :], share[:, :, :], over_last(stat[:, 2, :], E), ALU.mult).then_inc(share_ready, 1)
            for g in range(GROUPS):
                dve.wait_ge(turned, g + 1)
                nc.vector.tensor_copy(shares[:, g * GRP:(g + 1) * GRP], pt[g][:, :]).then_inc(rows_ready, 1)

        @block.scalar
        def _(act):
            act.wait_ge(act_in, 1)
            if softmax:
                nc.scalar.activation(share[:, :, :], share[:, :, :], ACT.Exp).then_inc(act_out, 1)
            else:
                nc.scalar.activation(score[:, :, :], logit[:, :, :], ACT.Sigmoid).then_inc(act_out, 1)


def stage_route_grouped(c, rows):
    nc = c.nc
    E, G = 64, 8
    M = E // G
    with c.scope() as s:
        w = s.sb("r0_w_sb", [P, E])
        bias = s.sb("r0_bias", [P, E])
        lower = s.sb("r0_lower", [P, G, G])
        score = s.sb("r0_score", [P, TILES, E])
        pick = s.sb("r0_pick", [P, TILES, E])
        left = s.sb("r0_left", [P, TILES, E])
        flag = s.sb("r0_flag", [P, TILES, E])
        top = s.sb("r0_top", [P, TILES, 8])
        group = s.sb("r0_group", [P, 5, TILES * G])
        earlier, equal = s.sb("r0_earlier", [P, TILES, G, G]), s.sb("r0_equal", [P, TILES, G, G])
        rank = s.sb("r0_rank", [P, TILES, G])
        stat = s.sb("r0_stat", [P, 3, TILES])
        shares = s.sb("r0_shares", [E, TOK])
        pl = [s.ps(f"r0_pl{i}", [P, TILES // 2, E]) for i in range(2)]
        pt = [s.ps(f"r0_pt{g}", [E, GRP]) for g in range(GROUPS)]
        loaded, logits_ready, step_done = s.sem("r0_loaded"), s.sem("r0_logits"), s.sem("r0_step")
        scores_ready, share_ready = s.sem("r0_scores"), s.sem("r0_share_r")
        turned, rows_ready, stored = s.sem("r0_turned"), s.sem("r0_rows"), s.sem("r0_stored")
        block = s.block()

        @block.sync
        def _(sp):
            sp.dma_start(w[:, :], c.dram["r0_w"]).then_inc(loaded, 16)
            sp.dma_start(bias[:, :], c.dram["r0_b"].to_broadcast([P, E])).then_inc(loaded, 16)
            sp.dma_start(lower[:, :, :], c.dram["lower"].to_broadcast([P, G, G])).then_inc(loaded, 16)
            sp.wait_ge(rows_ready, GROUPS)
            store_rows(sp, c, rows, shares[:, :], E, 1, 2, None, stored)

        @block.tensor
        def _(pe):
            pe.wait_ge(loaded, 48)
            for t in range(TILES):
                i, k = divmod(t, TILES // 2)
                ins = nc.tensor.matmul(pl[i][:, k, :], c.xnT[:, t * P:(t + 1) * P], w[:, :], start=True, stop=True)
                if k == TILES // 2 - 1:
                    ins.then_inc(logits_ready, 1)
            pe.wait_ge(share_ready, 1)
            for t in range(TILES):
                g, k = divmod(t, GRP // P)
                ins = nc.tensor.transpose(pt[g][:, k * P:(k + 1) * P], pick[:, t, :], c.ident[:, :])
                if k == GRP // P - 1:
                    ins.then_inc(turned, 1)

        @block.scalar
        def _(act):
            for i in range(2):
                act.wait_ge(logits_ready, i + 1)
                half = slice(i * TILES // 2, (i + 1) * TILES // 2)
                nc.scalar.activation(score[:, half, :], pl[i][:, :, :], ACT.Sigmoid).then_inc(scores_ready, 1)

        @block.vector
        def _(dve):
            count = [0]

            def link(ins):
                count[0] += 1
                ins.then_inc(step_done, 1)
                dve.wait_ge(step_done, count[0])

            v = nc.vector
            dve.wait_ge(loaded, 48)
            dve.wait_ge(scores_ready, 2)
            link(v.tensor_tensor(pick[:, :, :], score[:, :, :], bias[:, :].unsqueeze(1).to_broadcast([P, TILES, E]), ALU.add))
            grouped = pick[:, :, :].rearrange("p t (g m) -> p (t g) m", m=M)
            flags = flag[:, :, :].rearrange("p t (g m) -> p (t g) m", m=M)
            best, second, number, best_again, total = (group[:, i, :] for i in range(5))
            link(v.tensor_reduce(out=best, in_=grouped, op=ALU.max, axis=AX.X))
            link(v.tensor_tensor(flags, grouped, over_last(best, M), ALU.is_equal))
            link(v.tensor_reduce(out=number, in_=flags, op=ALU.add, axis=AX.X))
            link(v.scalar_tensor_tensor(out=flag[:, :, :], in0=flag[:, :, :], scalar=MASKED, in1=pick[:, :, :], op0=ALU.mult, op1=ALU.add))
            link(v.tensor_reduce(out=second, in_=flags, op=ALU.max, axis=AX.X))
            link(v.tensor_scalar(number, number, 1.5, None, ALU.is_gt))
            link(v.tensor_scalar(number, number, -MASKED, MASKED, ALU.mult, ALU.add))
            link(v.tensor_tensor(best_again, number, best, ALU.add))
            link(v.tensor_tensor(second, second, best_again, ALU.max))
            link(v.tensor_tensor(total, best, second, ALU.add))
            rank_below(nc, link, total.rearrange("p (t g) -> p t g", g=G), lower[:, :, :],
                       (earlier[:, :, :, :], equal[:, :, :, :]), rank[:, :, :])
            link(v.tensor_scalar(rank[:, :, :], rank[:, :, :], 3.5, None, ALU.is_lt))
            link(v.tensor_tensor(grouped, grouped, over_last(rank[:, :, :].rearrange("p t g -> p (t g)"), M), ALU.mult))
            link(v.tensor_scalar(pick[:, :, :], pick[:, :, :], 0.0, None, ALU.add))
            for t in range(TILES):
                ins = v.max(out=top[:, t, :], in_=pick[:, t, :])
            link(ins)
            for t in range(TILES):
                ins = v.match_replace(out=left[:, t, :], in_to_replace=top[:, t, :], in_values=pick[:, t, :], imm_value=3 * MASKED)
            link(ins)
            link(v.tensor_tensor(flag[:, :, :], pick[:, :, :], left[:, :, :], ALU.not_equal))
            link(v.tensor_tensor(pick[:, :, :], flag[:, :, :], score[:, :, :], ALU.mult))
            link(v.tensor_reduce(out=stat[:, 0, :], in_=pick[:, :, :], op=ALU.add, axis=AX.X))
            link(v.tensor_scalar(stat[:, 1, :], stat[:, 0, :], 1e-20, None, ALU.add))
            link(v.reciprocal(stat[:, 2, :], stat[:, 1, :]))
            link(v.tensor_scalar(stat[:, 2, :], stat[:, 2, :], 2.5, None, ALU.mult))
            v.tensor_tensor(pick[:, :, :], pick[:, :, :], over_last(stat[:, 2, :], E), ALU.mult).then_inc(share_ready, 1)
            for g in range(GROUPS):
                dve.wait_ge(turned, g + 1)
                v.tensor_copy(shares[:, g * GRP:(g + 1) * GRP], pt[g][:, :]).then_inc(rows_ready, 1)



def stage_experts(c, tag, weights, rows, chunks):
    nc = c.nc
    HB = 2
    with c.scope() as s:
        w_gu = [s.sb(f"{tag}_gu{i}", [P, 2 * P]) for i in range(HB)]
        w_dn = [s.sb(f"{tag}_dn{i}", [P, P]) for i in range(HB)]
        share = [s.sb(f"{tag}_share{i}", [P, TOK]) for i in range(HB)]
        hidden = [s.sb(f"{tag}_hidden{i}", [P, TOK]) for i in range(HB)]
        silu = [s.sb(f"{tag}_silu{i}", [P, GRP]) for i in range(2)]
        prod = [s.sb(f"{tag}_prod{i}", [P, GRP]) for i in range(2)]
        zeros = s.sb(f"{tag}_zeros", [P, GRP], BF16)
        gate = [s.ps(f"{tag}_pg{i}", [P, GRP]) for i in range(2)]
        up = [s.ps(f"{tag}_pu{i}", [P, GRP]) for i in range(2)]
        down = [s.ps(f"{tag}_pd{g}", [P, GRP]) for g in range(GROUPS)]
        gu_in, dn_in = [s.sem(f"{tag}_gu_in{i}") for i in range(HB)], [s.sem(f"{tag}_dn_in{i}") for i in range(HB)]
        share_in = [s.sem(f"{tag}_share_in{i}") for i in range(HB)]
        gu_done, silu_done, prod_done = s.sem(f"{tag}_gu_done"), s.sem(f"{tag}_silu_done"), s.sem(f"{tag}_prod_done")
        hidden_done, down_done, zeroed = s.sem(f"{tag}_hidden_done"), s.sem(f"{tag}_down_done"), s.sem(f"{tag}_zeroed")
        block = s.block()
        SET = HB * GROUPS
        half = P // 2

        def unit(k, par, g):
            return (k * HB + par) * GROUPS + g

        @block.sync
        def _(sp):
            def load(chunk, par, k):
                if k is not None:
                    sp.wait_ge(gu_done, unit(k, par, 0) - SET + GROUPS)
                sp.dma_start(w_gu[par][:, :], weights[bass.ds(chunk, 1), :, 0:2 * P].rearrange("c d n -> d (c n)")).then_inc(gu_in[par], 16)
                if k is not None:
                    sp.wait_ge(hidden_done, 2 + unit(k, par, 0) - SET + GROUPS)
                for j in range(2):
                    sp.dma_start(share[par][j * half:(j + 1) * half, :],
                                 rows[bass.ds(chunk * 2 + j, 1), :].to_broadcast([half, TOK])).then_inc(share_in[par], 16)
                if k is not None:
                    sp.wait_ge(down_done, unit(k, par, 0) + GROUPS)
                sp.dma_start(w_dn[par][:, :], weights[bass.ds(chunk, 1), :, 2 * P:3 * P].rearrange("c d n -> d (c n)")).then_inc(dn_in[par], 16)

            load(0, 0, None)
            load(1, 1, None)
            if chunks // HB > 1:
                with sp.Fori(1, chunks // HB) as k:
                    for par in range(HB):
                        load(k * HB + par, par, k)
            if chunks % HB:
                load(chunks - 1, 0, chunks // HB)

        @block.tensor
        def _(pe):
            pe.wait_ge(zeroed, 1)
            for g in range(GROUPS):
                ins = nc.tensor.matmul(down[g][:, :], zeros[:, 0:P], zeros[:, :], start=True, stop=False, skip_group_check=True)
            ins.then_inc(down_done, SET)

            def gate_up(k, par, g):
                n = unit(k, par, g)
                if g == 0:
                    pe.wait_ge(gu_in[par], 16 * (k + 1))
                pe.wait_ge(prod_done, n + 1)
                cols = c.xnT[:, g * GRP:(g + 1) * GRP]
                nc.tensor.matmul(gate[g % 2][:, :], w_gu[par][:, 0:P], cols, start=True, stop=True)
                nc.tensor.matmul(up[g % 2][:, :], w_gu[par][:, P:2 * P], cols, start=True, stop=True).then_inc(gu_done, 1)

            def project(k, par, g, last=False):
                n = unit(k, par, g)
                if g == 0:
                    pe.wait_ge(dn_in[par], 16 * (k + 1))
                pe.wait_ge(hidden_done, n + 3)
                nc.tensor.matmul(down[g][:, :], w_dn[par][:, :], hidden[par][:, g * GRP:(g + 1) * GRP],
                                 start=False, stop=last, skip_group_check=True).then_inc(down_done, 1)

            for g in range(GROUPS):
                gate_up(0, 0, g)
            pairs = (chunks - 1) // HB
            with pe.Fori(0, pairs) as k:
                for par in range(HB):
                    for g in range(GROUPS):
                        gate_up(k + par, 1 - par, g)
                        project(k, par, g)
            if chunks % HB == 0:
                for g in range(GROUPS):
                    gate_up(pairs, 1, g)
                    project(pairs, 0, g)
                for g in range(GROUPS):
                    project(pairs, 1, g, last=True)
            else:
                for g in range(GROUPS):
                    project(pairs, 0, g, last=True)

        def over_units(eng, step):
            with eng.Fori(0, chunks // HB) as k:
                for par in range(HB):
                    for g in range(GROUPS):
                        step(k, par, g)
            if chunks % HB:
                for g in range(GROUPS):
                    step(chunks // HB, 0, g)

        @block.scalar
        def _(act):
            def step(k, par, g):
                act.wait_ge(gu_done, unit(k, par, g) + 1)
                nc.scalar.activation(silu[g % 2][:, :], gate[g % 2][:, :], ACT.Silu).then_inc(silu_done, 1)
            over_units(act, step)
            act.wait_ge(down_done, SET + chunks * GROUPS)
            for g in range(0, GROUPS, 2):
                nc.scalar.activation(hidden[0][:, g * GRP:(g + 1) * GRP], down[g][:, :], ACT.Copy).then_inc(silu_done, 1)

        @block.vector
        def _(dve):
            nc.vector.memset(zeros[:, :], 0.0).then_inc(zeroed, 1)
            nc.vector.memset(prod[0][:, 0:1], 0.0).then_inc(prod_done, 2)
            def step(k, par, g):
                n = unit(k, par, g)
                dve.wait_ge(silu_done, n + 1)
                dve.wait_ge(hidden_done, n + 1)
                nc.vector.tensor_tensor(prod[g % 2][:, :], up[g % 2][:, :], silu[g % 2][:, :], ALU.mult).then_inc(prod_done, 1)
            over_units(dve, step)
            dve.wait_ge(down_done, SET + chunks * GROUPS)
            for g in range(1, GROUPS, 2):
                cols = slice(g * GRP, (g + 1) * GRP)
                nc.vector.tensor_tensor(c.y[:, cols], down[g][:, :], c.y[:, cols], ALU.add)
            for g in range(0, GROUPS, 2):
                cols = slice(g * GRP, (g + 1) * GRP)
                dve.wait_ge(silu_done, chunks * GROUPS + g // 2 + 1)
                nc.vector.tensor_tensor(c.y[:, cols], hidden[0][:, cols], c.y[:, cols], ALU.add)

        @block.gpsimd
        def _(pool):
            nc.gpsimd.memset(hidden[0][:, 0:1], 0.0).then_inc(hidden_done, 2)
            def step(k, par, g):
                n = unit(k, par, g)
                if g == 0:
                    pool.wait_ge(share_in[par], 32 * (k + 1))
                pool.wait_ge(prod_done, n + 3)
                pool.wait_ge(down_done, n + 1)
                cols = slice(g * GRP, (g + 1) * GRP)
                nc.gpsimd.tensor_tensor(hidden[par][:, cols], prod[g % 2][:, :], share[par][:, cols], ALU.mult).then_inc(hidden_done, 1)
            over_units(pool, step)



F32R = mybir.dt.float32r
HI, MID, LO = range(3)
Q_PARTS = (HI, HI, HI, MID, MID, LO)
K_PARTS = (HI, MID, LO, HI, MID, HI)


class Heads:

    def __init__(self, nc, tag, width, null):
        self.tag, self.width, self.null = tag, width, null
        self.small = width == 8
        self.together = 4 if self.small else 1
        self.out_rows = 32 if self.small else width + 1
        self.keys = SEQ + null
        self.part = BF16 if self.small else F32R
        self.rows = 6 * width if self.small else 3 * width
        self.moved = BF16 if self.small else F32
        if self.small:
            self.q = nc.dram_tensor(f"{tag}_q_parts", (HEADS, self.rows, BATCH, SEQ), self.moved, kind="Internal").ap()
            self.k = nc.dram_tensor(f"{tag}_k_parts", (HEADS, self.rows, BATCH, self.keys), self.moved, kind="Internal").ap()
        self.v = nc.dram_tensor(f"{tag}_v_rows", (P, HEADS, TILES, self.out_rows), F32, kind="Internal").ap()
        self.o = nc.dram_tensor(f"{tag}_sums", (HEADS * self.out_rows, TOK), F32, kind="Internal").ap()
        self.inv = nc.dram_tensor(f"{tag}_inverse", (HEADS, TOK), F32, kind="Internal").ap()


def stage_project_small(c, h):
    nc, tag = c.nc, h.tag
    rope = h.null
    with c.scope() as s:
        names = ["wq", "wk", "wv"] + (["wq_turn", "wk_turn"] if rope else [])
        w = {n: s.sb(f"{tag}_{n}", [P, P]) for n in names}
        if rope:
            cos, sin = s.sb(f"{tag}_cos", [P, SEQ]), s.sb(f"{tag}_sin", [P, SEQ])
            turned = s.sb(f"{tag}_turned", [P, GRP])
        full = {n: s.sb(f"{tag}_{n}_full", [P, BATCH, SEQ if n == "q" else h.keys]) for n in "qk"}
        rest = {n: s.sb(f"{tag}_{n}_rest", list(full[n].shape)) for n in "qk"}
        part = {n: [s.sb(f"{tag}_{n}_part{i}", list(full[n].shape), BF16) for i in range(3)] for n in "qk"}
        v = s.sb(f"{tag}_v", [P, HEADS, TILES, h.out_rows])
        pq = [s.ps(f"{tag}_pq{i}", [P, GRP]) for i in range(2)]
        pt = [s.ps(f"{tag}_pt{i}", [P, GRP]) for i in range(2)]
        pv = [s.ps(f"{tag}_pv{i}", [P, P]) for i in range(4)]
        loaded, projected, copied = s.sem(f"{tag}_loaded"), s.sem(f"{tag}_projected"), s.sem(f"{tag}_copied")
        rotated, step_done = s.sem(f"{tag}_rotated"), s.sem(f"{tag}_step")
        v_done, v_copied, v_filled = s.sem(f"{tag}_v_done"), s.sem(f"{tag}_v_copied"), s.sem(f"{tag}_v_filled")
        hi_done, rest_done, mid_done, lo_done = (s.sem(f"{tag}_{n}") for n in ("hi", "rest", "mid", "lo"))
        stored = s.sem(f"{tag}_stored")
        block = s.block()
        per = SEQ // GRP
        order = [("q", g) for g in range(GROUPS)] + [("k", g) for g in range(GROUPS)]

        @block.sync
        def _(sp):
            for n in names:
                sp.dma_start(w[n][:, :], c.dram[f"{tag}_{n}"]).then_inc(loaded, 16)
            if rope:
                sp.dma_start(cos[:, :], c.dram["cos"]).then_inc(loaded, 16)
                sp.dma_start(sin[:, :], c.dram["sin"]).then_inc(loaded, 16)
                for b in range(BATCH):
                    with nc.allow_non_contiguous_dma(reason="the null key is a column"):
                        sp.dma_start(full["k"][:, b, SEQ:SEQ + 1], c.dram[f"{tag}_k_null"]).then_inc(loaded, 16)
            n = 0
            for i, (name, parts, rows) in enumerate((("q", Q_PARTS, h.q), ("k", K_PARTS, h.k))):
                for sem, p in ((hi_done, HI), (mid_done, MID), (lo_done, LO)):
                    sp.wait_ge(sem, i + 1)
                    for k in range(6):
                        if parts[k] == p:
                            for b in range(BATCH):
                                dst = rows[:, k * h.width:(k + 1) * h.width, b, :]
                                sp.dma_start(dst, part[name][p][:, b, :]).then_inc(stored, 16)
                                n += 16
            sp.wait_ge(v_copied, TILES)
            sp.wait_ge(v_filled, 2)
            sp.dma_start(h.v, v[:, :, :, :]).then_inc(stored, 16)
            sp.wait_ge(stored, n + 16)

        @block.gpsimd
        def _(pool):
            nc.gpsimd.memset(v[:, :, :, h.width + 1:], 0.0).then_inc(v_filled, 1)
            nc.gpsimd.memset(v[:, :, :, h.width:h.width + 1], 1.0).then_inc(v_filled, 1)

        @block.tensor
        def _(pe):
            pe.wait_ge(loaded, 16 * (len(names) + (4 if rope else 0)))
            for i, (name, g) in enumerate(order):
                if i >= 2:
                    pe.wait_ge(copied, i - 1)
                cols = c.xnT[:, g * GRP:(g + 1) * GRP]
                if rope:
                    nc.tensor.matmul(pt[i % 2][:, :], w[f"w{name}_turn"][:, :], cols, start=True, stop=True)
                nc.tensor.matmul(pq[i % 2][:, :], w[f"w{name}"][:, :], cols, start=True, stop=True).then_inc(projected, 1)
            for t in range(TILES):
                if t >= 4:
                    pe.wait_ge(v_copied, t - 3)
                nc.tensor.matmul(pv[t % 4][:, :], c.xnT[:, t * P:(t + 1) * P], w["wv"][:, :], start=True, stop=True).then_inc(v_done, 1)

        @block.vector
        def _(dve):
            count = [0]

            def link(ins):
                count[0] += 1
                ins.then_inc(step_done, 1)
                dve.wait_ge(step_done, count[0])

            if rope:
                dve.wait_ge(loaded, 16 * (len(names) + 4))
            for i, (name, g) in enumerate(order):
                dve.wait_ge(projected, i + 1)
                b, at = g // per, (g % per) * GRP
                dst = full[name][:, b, at:at + GRP]
                if rope:
                    if i:
                        dve.wait_ge(copied, i)
                    link(nc.vector.tensor_tensor(turned[:, :], pt[i % 2][:, :], sin[:, at:at + GRP], ALU.mult))
                    link(nc.vector.tensor_tensor(dst, pq[i % 2][:, :], cos[:, at:at + GRP], ALU.mult))
                    nc.vector.tensor_tensor(dst, dst, turned[:, :], ALU.add).then_inc(copied, 1)
                else:
                    nc.vector.tensor_copy(dst, pq[i % 2][:, :]).then_inc(copied, 1)
            for i, name in enumerate("qk"):
                dve.wait_ge(hi_done, i + 1)
                nc.vector.tensor_tensor(rest[name][:, :, :], full[name][:, :, :], part[name][HI][:, :, :], ALU.subtract).then_inc(rest_done, 1)
            for i, name in enumerate("qk"):
                dve.wait_ge(mid_done, i + 1)
                nc.vector.tensor_tensor(part[name][LO][:, :, :], rest[name][:, :, :], part[name][MID][:, :, :], ALU.subtract).then_inc(lo_done, 1)

        @block.scalar
        def _(act):
            for i, name in enumerate("qk"):
                act.wait_ge(copied, (i + 1) * GROUPS)
                nc.scalar.activation(part[name][HI][:, :, :], full[name][:, :, :], ACT.Copy).then_inc(hi_done, 1)
            for i, name in enumerate("qk"):
                act.wait_ge(rest_done, i + 1)
                nc.scalar.activation(part[name][MID][:, :, :], rest[name][:, :, :], ACT.Copy).then_inc(mid_done, 1)
            for t in range(TILES):
                act.wait_ge(v_done, t + 1)
                nc.scalar.activation(v[:, :, t, 0:h.width], pv[t % 4][:, :].rearrange("p (a d) -> p a d", d=h.width),
                                     ACT.Copy).then_inc(v_copied, 1)


def stage_project_v(c, h, w_v):
    nc, tag, W = c.nc, h.tag, h.width
    with c.scope() as s:
        wv = [s.sb(f"{tag}_wv{i}", [P, GRP]) for i in range(2)]
        v = s.sb(f"{tag}_v", [P, HEADS, TILES, h.out_rows])
        bank = [s.ps(f"{tag}_bank{i}", [P, GRP]) for i in range(4)]
        wv_in = s.sem(f"{tag}_wv_in")
        v_done, v_copied, v_filled, v_stored = (s.sem(f"{tag}_{n}") for n in ("v_done", "v_copied", "v_filled", "v_stored"))
        block = s.block()

        @block.sync
        def _(sp):
            for i in range(2):
                sp.dma_start(wv[i][:, :], w_v[:, i * GRP:(i + 1) * GRP]).then_inc(wv_in, 16)
            sp.wait_ge(v_filled, 1)
            for b in range(BATCH):
                half = slice(b * TILES // BATCH, (b + 1) * TILES // BATCH)
                sp.wait_ge(v_copied, 2 * half.stop)
                sp.dma_start(h.v[:, :, half, :], v[:, :, half, :]).then_inc(v_stored, 16)
            sp.wait_ge(v_stored, 16 * BATCH)

        @block.tensor
        def _(pe):
            pe.wait_ge(wv_in, 32)
            for n in range(2 * TILES):
                t, i = divmod(n, 2)
                if n >= 4:
                    pe.wait_ge(v_copied, n - 3)
                nc.tensor.matmul(bank[n % 4][:, :], c.xnT[:, t * P:(t + 1) * P], wv[i][:, :], start=True, stop=True).then_inc(v_done, 1)

        @block.scalar
        def _(act):
            half = HEADS // 2
            for n in range(2 * TILES):
                t, i = divmod(n, 2)
                act.wait_ge(v_done, n + 1)
                nc.scalar.activation(v[:, i * half:(i + 1) * half, t, 0:W],
                                     bank[n % 4][:, :].rearrange("p (a d) -> p a d", d=W), ACT.Copy).then_inc(v_copied, 1)

        @block.gpsimd
        def _(pool):
            nc.gpsimd.memset(v[:, :, :, W:W + 1], 1.0).then_inc(v_filled, 1)



def stage_attend(c, h, scale, w_qk=None):
    nc, tag, G, W = c.nc, h.tag, h.together, h.width
    units = HEADS // G * BATCH
    KT = SEQ // P
    HT = GRP // P
    NULL = KT
    steps = []
    for half in range(2):
        steps += [(half, NULL)] * h.null + [(half, t) for t in range((half + 1) * HT)]
    NS = len(steps)
    H0 = sum(1 for half, _ in steps if half == 0)
    slots = [(st, g) for st, (_, t) in enumerate(steps) for g in range(1 if t == NULL else G)]
    NSLOT = len(slots)
    slot_end = [max(n for n, (s_, _) in enumerate(slots) if s_ == st) + 1 for st in range(NS)]
    trials = [(g, t, part) for g in range(G) for t in range(KT) for part in range(1 + t // HT)]
    proj = [] if h.small else [(x, part) for part in range(2) for x in "qk"]
    NPR = len(proj)
    NTR = NPR + len(trials)
    NULLS = 2 * h.null
    NT_ALL = NTR + NULLS + 1
    RING = 3
    LAG = 1 if G > 1 else 2
    E_RING = LAG + 2
    if h.small:
        terms, max_row, max_term, lead = [97], 96, 0, 96
    else:
        terms, max_row, max_term, lead = [P, 96], W, 1, P
    NT = len(terms)
    PADK = 32 * h.null
    with c.scope() as s:
        w = None if h.small else s.sb(f"{tag}_w", [P, 4 * W])
        q = [s.sb(f"{tag}_q{i}", [P, NT, G, SEQ], h.part) for i in range(2)]
        k = [s.sb(f"{tag}_k{i}", [P, NT, G, SEQ + PADK], h.part) for i in range(2)]
        v = [s.sb(f"{tag}_vv{i}", [P, G, KT, h.out_rows]) for i in range(2)]
        v_null = [s.sb(f"{tag}_vn{i}", [P, G, h.out_rows]) for i in range(2)] if h.null else None
        e = [s.sb(f"{tag}_e{i}", [P, G, GRP]) for i in range(E_RING)]
        neg_max = s.sb(f"{tag}_neg_max", [P, G, KT])
        neg_max2 = s.sb(f"{tag}_neg_max2", [P, G, KT - HT])
        max_rows = s.sb(f"{tag}_max_rows", [G * KT, P], h.part)
        out_sb = s.sb(f"{tag}_out", [P, 2, GRP])
        mark = s.sb(f"{tag}_mark", [1, 8])
        above = s.sb(f"{tag}_above", [P, P])
        below = s.sb(f"{tag}_below", [P, P])
        above_b, below_b, ident_b = (s.sb(f"{tag}_{n}", [P, P], BF16) for n in ("above_b", "below_b", "ident_b"))
        ps = [s.ps(f"{tag}_ps{i}", [P, GRP]) for i in range(RING)]
        pm = [s.ps(f"{tag}_pm{i}", [P, GRP]) for i in range(RING)]
        po = [s.ps(f"{tag}_po{i}", [P, GRP]) for i in range(2)]
        OUT = slice(0, P if h.small else W + 1)
        consts_in, filled, masks_ready = s.sem(f"{tag}_consts"), s.sem(f"{tag}_filled"), s.sem(f"{tag}_masks")
        zero = s.sb(f"{tag}_zero", [P, 1])
        FILLS = 7 + 5 * h.null
        qk_in = [[s.sem(f"{tag}_qk_in{b}{g}") for g in range(G)] for b in range(2)]
        v_in = [s.sem(f"{tag}_v_in{b}") for b in range(2)]
        w_in, hi_done, k_doubled = (s.sem(f"{tag}_{n}") for n in ("w_in", "hi_done", "k_doubled"))
        scored, exp_done, weighed = s.sem(f"{tag}_scored"), s.sem(f"{tag}_exp"), s.sem(f"{tag}_weighed")
        trial, trial_read = s.sem(f"{tag}_trial"), s.sem(f"{tag}_trial_read")
        max_ready, max_in = s.sem(f"{tag}_max_ready"), s.sem(f"{tag}_max_in")
        out_copied = [s.sem(f"{tag}_out_copied{i}") for i in range(2)]
        out_stored = [s.sem(f"{tag}_out_stored{i}") for i in range(2)]
        block = s.block()
        last = units // 2 - 1

        def freed(u, n, total, ring):
            before = n - ring if n >= ring else max(m for m in range(total) if m % ring == n) - total
            return u * total + before + 1 + ring

        def trials_by(n):
            start, end = (0.08, 0.9) if h.small else (0.0, 0.8)
            return max(0, min(NT_ALL, int((n + 1 - start * NSLOT) / ((end - start) * NSLOT) * NT_ALL + 0.999)))

        @block.sync
        def _(sp):
            sp.dma_start(above[:, :], c.dram["mask_above"]).then_inc(consts_in, 16)
            sp.dma_start(below[:, :], c.dram["mask_below"]).then_inc(consts_in, 16)
            sp.wait_ge(filled, FILLS)

            def load_qk(i, b):
                for g in range(G):
                    head = bass.ds(i * G + g, 1)
                    for dst, src in ((q, h.q), (k, h.k)):
                        keys = src.shape[-1]
                        sp.dma_start(dst[b][0:h.rows, 0, g, 0:keys], src[head, :, b, :].rearrange("g r n -> (g r) n")).then_inc(qk_in[b][g], 16)

            def load_w(i):
                sp.dma_start(w[:, :], w_qk[bass.ds(i, 1), :, :].rearrange("a d n -> (a d) n")).then_inc(w_in, 16)

            def load_v(i, b):
                src = h.v[:, bass.ds(i * G, G), b * KT:(b + 1) * KT, :]
                sp.dma_start(v[b][:, :, :, :], src).then_inc(v_in[b], 16)
                if h.null:
                    for g in range(G):
                        sp.dma_start(v_null[b][32 * g:32 * g + 1, g, :],
                                     c.dram[f"{tag}_v_null"][:, bass.ds(i * G + g, 1), :].rearrange("o g r -> o (g r)")).then_inc(v_in[b], 16)

            def put_max(b):
                dst = q[b][max_row:max_row + 1, max_term, :, :].rearrange("o g n -> o (g n)")
                sp.dma_start(dst.bitcast(h.moved), max_rows[:, :].bitcast(h.moved)).then_inc(max_in, 16)

            def store(i, b, half):
                sp.wait_ge(out_copied[half], 2 * i + b + 2)
                at = b * SEQ + half * GRP
                sp.dma_start(h.o[bass.ds((i * G) * h.out_rows, OUT.stop), at:at + GRP], out_sb[OUT, half, :]).then_inc(out_stored[half], 16)

            def unit(i, b, is_last):
                u = 2 * i + b
                if not h.small and b == 0 and not is_last:
                    sp.wait_ge(trial, NT_ALL * (u + 1) + NPR)
                    load_w(i + 1)
                if not (is_last and b == 1):
                    sp.wait_ge(trial_read, RING + NT_ALL * (u + 2))
                    put_max(1 - b)
                store(i, b, 0)
                if not is_last:
                    if h.small:
                        sp.wait_ge(scored, NSLOT * (u + 1))
                        load_qk(i + 1, b)
                    sp.wait_ge(weighed, E_RING + NS * (u + 1))
                    load_v(i + 1, b)
                store(i, b, 1)

            if not h.small:
                load_w(0)
            for b in range(2):
                if h.small:
                    load_qk(0, b)
                load_v(0, b)
            sp.wait_ge(trial_read, RING + NT_ALL)
            put_max(0)
            with sp.Fori(0, last) as i:
                for b in range(2):
                    unit(i, b, False)
            for b in range(2):
                unit(last, b, True)
            for half in range(2):
                sp.wait_ge(out_stored[half], 16 * (units + 1))

        QK_LOADS, V_LOADS = 32, 16 * (1 + G * h.null)

        @block.gpsimd
        def _(pool):
            fills = [(zero[:, :], 0.0)]
            for b in range(2):
                if h.small:
                    fills += [(q[b][:, 0, :, :], 0.0), (k[b][0:96, 0, :, :], 0.0), (k[b][96:97, 0, :, 0:h.keys], 1.0)]
                else:
                    fills += [(q[b][W:96, 1, :, :], 0.0), (k[b][W:96, 1, :, :], 0.0), (k[b][W:W + 1, 1, :, :], 1.0)]
                if h.null:
                    fills += [(k[b][96:97, 0, :, h.keys:], 0.0), (v_null[b][:, :, :], 0.0)]
            if h.null:
                fills += [(mark[:, 7:8], 0.0)]
            for n, (rows, value) in enumerate(fills):
                nc.gpsimd.memset(rows if h.small or rows.dtype == F32 else rows.bitcast(F32), value).then_inc(filled, 1)
                pool.wait_ge(filled, n + 1)

            def double_k(i, b):
                pool.wait_ge(hi_done, (2 * i + b + 1) * NPR)
                hi = k[b][0:W, 0, 0, :].bitcast(F32)
                nc.gpsimd.tensor_tensor(k[b][0:W, 1, 0, :], hi, zero[0:W, :].to_broadcast([W, SEQ]), ALU.add).then_inc(k_doubled, 1)

            if not h.small:
                with pool.Fori(0, units // 2) as i:
                    for b in range(2):
                        double_k(i, b)

        @block.tensor
        def _(pe):
            def try_max(i, b, n):
                u = 2 * i + b
                bank = pm[n % RING]
                if h.small and n < NTR and trials[n][1:] == (0, 0):
                    pe.wait_ge(qk_in[b][trials[n][0]], QK_LOADS * (i + 1))
                if not h.small and n == 0 and b == 0:
                    pe.wait_ge(w_in, 16 * (i + 1))
                if not h.small and n == NPR:
                    pe.wait_ge(trial_read, RING + u * NT_ALL + NPR)
                pe.wait_ge(trial_read, freed(u, n, NT_ALL, RING))
                if n < NPR:
                    x, part = proj[n]
                    at = 0 if x == "q" else 2 * W
                    first = b * SEQ + part * GRP
                    ins = nc.tensor.matmul(bank[:, :], w[:, at:at + 2 * W], c.xnT[:, first:first + GRP], start=True, stop=True)
                elif n < NTR:
                    g, t, part = trials[n - NPR]
                    lhs = q[b][0:lead, 0, g, t * P:(t + 1) * P]
                    lo, hi = part * GRP, min((part + 1) * GRP, (t + 1) * P)
                    diag = hi == (t + 1) * P
                    ins = nc.tensor.matmul(bank[:, 0:hi - lo], lhs, k[b][0:lead, 0, g, lo:hi], start=True, stop=not diag)
                    if diag:
                        ins = nc.tensor.matmul(bank[:, t * P - lo:hi - lo], ident_b[:, :], above_b[:, :], start=False, stop=True)
                elif n < NTR + NULLS:
                    for g in range((n - NTR) * G // 2, (n - NTR + 1) * G // 2):
                        for t in range(KT):
                            ins = nc.tensor.matmul(bank[:, g * KT + t:g * KT + t + 1], q[b][0:lead, 0, g, t * P:(t + 1) * P],
                                                   k[b][0:lead, 0, g, SEQ:SEQ + 1], start=True, stop=True)
                else:
                    pe.wait_ge(max_ready, u + 1)
                    ins = nc.tensor.transpose(bank[0:G * KT, 0:P], neg_max[:, :, :].rearrange("p g t -> p (g t)"), c.ident[:, :])
                ins.then_inc(trial, 1)

            def score(i, b, n):
                u = 2 * i + b
                st, g = slots[n]
                half, t = steps[st]
                bank = ps[n % RING]
                if n == 0:
                    pe.wait_ge(max_in, 16 * (u + 1))
                    if not h.small:
                        pe.wait_ge(k_doubled, u + 1)
                pe.wait_ge(exp_done, freed(u, n, NSLOT, RING))
                first = half * GRP
                if t == NULL:
                    for a in range(G):
                        ins = nc.tensor.matmul(bank[32 * a:32 * a + 32, :], k[b][0:terms[0], 0, a, SEQ:SEQ + PADK],
                                               q[b][0:terms[0], 0, a, first:first + GRP], start=True, stop=True)
                else:
                    lo = max(first, t * P)
                    diag = lo == t * P
                    for m in range(NT):
                        ins = nc.tensor.matmul(bank[:, lo - first:], k[b][0:terms[m], m, g, t * P:(t + 1) * P],
                                               q[b][0:terms[m], m, g, lo:first + GRP], start=m == 0, stop=m == NT - 1 and not diag)
                    if diag:
                        ins = nc.tensor.matmul(bank[:, lo - first:lo - first + P], ident_b[:, :], below_b[:, :], start=False, stop=True)
                ins.then_inc(scored, 1)

            def weigh(i, b, st):
                u = 2 * i + b
                half, t = steps[st]
                if st == 0:
                    pe.wait_ge(v_in[b], V_LOADS * (i + 1))
                if st in (0, H0):
                    pe.wait_ge(out_copied[half], u + 1)
                if st + LAG >= NS or slot_end[st + LAG] - RING < slot_end[st]:
                    pe.wait_ge(exp_done, RING + u * NSLOT + slot_end[st])
                lo = 0 if t == NULL else max(0, t * P - half * GRP)
                for g in range(G):
                    lhs = v_null[b][:, g, :] if t == NULL else v[b][:, g, t, :]
                    ins = nc.tensor.matmul(po[half][g * h.out_rows:(g + 1) * h.out_rows, lo:], lhs,
                                           e[st % E_RING][:, 0 if t == NULL else g, lo:], start=st in (0, H0),
                                           stop=st in (H0 - 1, NS - 1), skip_group_check=True)
                ins.then_inc(weighed, 1)

            def unit(i, b, before, after):
                done = 0
                for n, (st, g) in enumerate(slots):
                    score(i, b, n)
                    while after and done < trials_by(n):
                        try_max(*after, done)
                        done += 1
                    if n + 1 == slot_end[st]:
                        if st >= LAG:
                            weigh(i, b, st - LAG)
                        elif before:
                            weigh(*before, NS - LAG + st)
                assert not after or done == NT_ALL

            pe.wait_ge(filled, FILLS)
            pe.wait_ge(masks_ready, 3)
            for n in range(NT_ALL):
                try_max(0, 0, n)
            unit(0, 0, None, (0, 1))
            with pe.Fori(0, last) as i:
                unit(i, 1, (i, 0), (i + 1, 0))
                unit(i + 1, 0, (i, 1), (i + 1, 1))
            unit(last, 1, (last, 0), None)
            for st in range(NS - LAG, NS):
                weigh(last, 1, st)

        @block.scalar
        def _(act):
            for n, (sem, free) in enumerate(((exp_done, RING), (weighed, E_RING), (trial_read, RING), (out_copied[0], 1),
                                             (out_stored[0], 16), (out_stored[1], 16))):
                nc.scalar.activation(mark[:, n:n + 1], c.ident[0:1, 0:1], ACT.Copy).then_inc(sem, free)

            def split(i, b, n):
                x, part = proj[n]
                act.wait_ge(trial, (2 * i + b) * NT_ALL + n + 1)
                dst = (q if x == "q" else k)[b]
                nc.scalar.activation(dst[:, 0, 0, part * GRP:(part + 1) * GRP], pm[n % RING][:, :], ACT.Copy).then_inc(hi_done, 1)

            def unit(i, b, after):
                u = 2 * i + b
                done = 0
                for n, (st, g) in enumerate(slots):
                    half, t = steps[st]
                    if n == 0 or slots[n - 1][0] != st:
                        act.wait_ge(weighed, freed(u, st, NS, E_RING))
                    act.wait_ge(scored, u * NSLOT + n + 1)
                    lo = 0 if t == NULL else max(0, t * P - half * GRP)
                    nc.scalar.activation(e[st % E_RING][:, g, lo:], ps[n % RING][:, lo:], ACT.Exp, scale=scale).then_inc(exp_done, 1)
                    while after and done < min(NPR, trials_by(n)):
                        split(*after, done)
                        done += 1
                    if n + 1 == slot_end[H0 + LAG]:
                        act.wait_ge(weighed, E_RING + u * NS + H0)
                        act.wait_ge(out_stored[0], 16 * (u + 1))
                        nc.scalar.activation(out_sb[OUT, 0, :], po[0][OUT, :], ACT.Copy).then_inc(out_copied[0], 1)

            for n in range(NPR):
                split(0, 0, n)
            with act.Fori(0, last) as i:
                unit(i, 0, (i, 1))
                unit(i, 1, (i + 1, 0))
            unit(last, 0, (last, 1))
            unit(last, 1, None)

        @block.vector
        def _(dve):
            dve.wait_ge(consts_in, 32)
            nc.vector.tensor_copy(above_b[:, :], above[:, :]).then_inc(masks_ready, 1)
            nc.vector.tensor_copy(below_b[:, :], below[:, :]).then_inc(masks_ready, 1)
            nc.vector.tensor_copy(ident_b[:, :], c.ident[:, :]).then_inc(masks_ready, 1)
            nc.vector.memset(mark[:, 6:7], 0.0).then_inc(out_copied[1], 1)

            def flat(ap):
                return ap.rearrange("p g t -> p (g t)")

            def reduce(i, b, before):
                u = 2 * i + b
                for n, (x, part) in enumerate(proj):
                    dve.wait_ge(hi_done, u * NPR + n + 1)
                    cols = slice(part * GRP, (part + 1) * GRP)
                    if x == "q":
                        nc.vector.tensor_tensor(q[b][0:W, 1, 0, cols], pm[n % RING][0:W, :], q[b][0:W, 0, 0, cols].bitcast(F32), ALU.subtract).then_inc(trial_read, 1)
                    else:
                        nc.vector.tensor_tensor(k[b][W:P, 0, 0, cols], pm[n % RING][W:P, :], k[b][W:P, 0, 0, cols].bitcast(F32), ALU.subtract).then_inc(trial_read, 1)
                for n, (g, t, part) in enumerate(trials, NPR):
                    hi = min((part + 1) * GRP, (t + 1) * P) - part * GRP
                    dst = neg_max2[:, g, t - HT:t - HT + 1] if part else neg_max[:, g, t:t + 1]
                    dve.wait_ge(trial, u * NT_ALL + n + 1)
                    nc.vector.tensor_reduce(out=dst, in_=pm[n % RING][:, 0:hi], op=ALU.max, axis=AX.X, negate=True).then_inc(trial_read, 1)
                    if before and n == NTR // 4:
                        copy_out(*before)
                for n in range(NTR, NTR + NULLS):
                    part = slice((n - NTR) * G // 2 * KT, (n - NTR + 1) * G // 2 * KT)
                    dve.wait_ge(trial, u * NT_ALL + n + 1)
                    dve.wait_ge(trial_read, RING + u * NT_ALL + NTR)
                    nc.vector.scalar_tensor_tensor(out=flat(neg_max)[:, part], in0=pm[n % RING][:, part], scalar=-1.0,
                                                   in1=flat(neg_max)[:, part], op0=ALU.mult, op1=ALU.min).then_inc(trial_read, 1)
                dve.wait_ge(trial_read, RING + (u + 1) * NT_ALL - 1)
                nc.vector.tensor_tensor(neg_max[:, :, HT:], neg_max[:, :, HT:], neg_max2[:, :, :], ALU.min).then_inc(max_ready, 1)
                dve.wait_ge(trial, (u + 1) * NT_ALL)
                if not (isinstance(u, int) and u == 0):
                    dve.wait_ge(max_in, 16 * u)
                nc.vector.tensor_copy(max_rows[:, :], pm[(NT_ALL - 1) % RING][0:G * KT, 0:P]).then_inc(trial_read, 1)

            def copy_out(i, b):
                u = 2 * i + b
                dve.wait_ge(weighed, E_RING + NS * (u + 1))
                dve.wait_ge(out_stored[1], 16 * (u + 1))
                nc.vector.tensor_copy(out_sb[OUT, 1, :], po[1][OUT, :]).then_inc(out_copied[1], 1)

            for b in range(2):
                reduce(0, b, None)
            with dve.Fori(0, last) as i:
                for b in range(2):
                    reduce(i + 1, b, (i, b))
            for b in range(2):
                copy_out(last, b)


def stage_attention_out(c, h, w_out):
    nc, tag = c.nc, h.tag
    chunks = HEADS * h.width // P
    per = HEADS // chunks
    with c.scope() as s:
        den = s.sb(f"{tag}_den", [P, HEADS * TOK // P])
        w = [s.sb(f"{tag}_wo{i}", [P, P]) for i in range(2)]
        num = [s.sb(f"{tag}_num{i}", [P, TOK]) for i in range(2)]
        inv = [s.sb(f"{tag}_inv{i}", [P, TOK]) for i in range(2)]
        po = [s.ps(f"{tag}_pout{g}", [P, GRP]) for g in range(GROUPS)]
        den_in, den_done, den_stored = s.sem(f"{tag}_den_in"), s.sem(f"{tag}_den_done"), s.sem(f"{tag}_den_st")
        loaded, divided, used = [s.sem(f"{tag}_oin{i}") for i in range(2)], s.sem(f"{tag}_divided"), s.sem(f"{tag}_used")
        block = s.block()
        parts = P // HEADS
        width = TOK // parts

        @block.sync
        def _(sp):
            src = dram_view(h.o, h.width * TOK, [[h.out_rows * TOK, HEADS], [width, parts], [1, width]])
            sp.dma_start(den[:, :], src).then_inc(den_in, 16)
            sp.wait_ge(den_done, 1)
            sp.dma_start(h.inv.rearrange("a (k n) -> a k n", k=parts), den[:, :]).then_inc(den_stored, 16)
            sp.wait_ge(den_stored, 16)
            for k in range(chunks):
                if k >= 2:
                    sp.wait_ge(used, k - 1)
                sp.dma_start(w[k % 2][:, :], w_out[k * P:(k + 1) * P, :]).then_inc(loaded[k % 2], 16)
                src = dram_view(h.o, k * per * h.out_rows * TOK, [[h.out_rows * TOK, per], [TOK, h.width], [1, TOK]])
                sp.dma_start(num[k % 2][:, :], src).then_inc(loaded[k % 2], 16)
                src = dram_view(h.inv, k * per * TOK, [[TOK, per], [0, h.width], [1, TOK]])
                sp.dma_start(inv[k % 2][:, :], src).then_inc(loaded[k % 2], 16)

        @block.vector
        def _(dve):
            dve.wait_ge(den_in, 16)
            nc.vector.reciprocal(den[:, :], den[:, :]).then_inc(den_done, 1)
            for k in range(chunks):
                dve.wait_ge(loaded[k % 2], 48 * (k // 2 + 1))
                nc.vector.tensor_tensor(num[k % 2][:, :], num[k % 2][:, :], inv[k % 2][:, :], ALU.mult).then_inc(divided, 1)
            dve.wait_ge(used, chunks)
            for g in range(1, GROUPS, 2):
                nc.vector.tensor_copy(c.y[:, g * GRP:(g + 1) * GRP], po[g][:, :])

        @block.scalar
        def _(act):
            act.wait_ge(used, chunks)
            for g in range(0, GROUPS, 2):
                nc.scalar.activation(c.y[:, g * GRP:(g + 1) * GRP], po[g][:, :], ACT.Copy)

        @block.tensor
        def _(pe):
            for k in range(chunks):
                pe.wait_ge(divided, k + 1)
                for g in range(GROUPS):
                    ins = nc.tensor.matmul(po[g][:, :], w[k % 2][:, :], num[k % 2][:, g * GRP:(g + 1) * GRP],
                                           start=k == 0, stop=k == chunks - 1)
                ins.then_inc(used, 1)



BLOCK = 16
HIDDEN = 352


def fp4_round(nc, link, src, sign, wait_sign, mag, level, above, stat, dst):
    v = nc.vector
    largest, inverse, half = (stat[:, i, :] for i in range(3))
    link(v.scalar_tensor_tensor(out=mag, in0=src, scalar=-1.0, in1=src, op0=ALU.mult, op1=ALU.max))
    link(v.tensor_reduce(out=largest, in_=mag, op=ALU.max, axis=AX.X))
    link(v.tensor_scalar(largest, largest, 1.0 / 6.0, 1e-12, ALU.mult, ALU.max))
    link(v.reciprocal(inverse, largest))
    link(v.tensor_scalar(half, largest, 0.5, None, ALU.mult))
    link(v.tensor_tensor(mag, mag, over_last(inverse, BLOCK), ALU.mult))
    link(v.tensor_scalar(level, mag, 5.0, 2.0, ALU.is_gt, ALU.mult))
    for step in (3.5, 2.5):
        link(v.scalar_tensor_tensor(out=level, in0=mag, scalar=step, in1=level, op0=ALU.is_gt, op1=ALU.add))
    link(v.tensor_scalar(above, mag, 1.75, None, ALU.is_gt))
    link(v.scalar_tensor_tensor(out=level, in0=level, scalar=2.0, in1=above, op0=ALU.mult, op1=ALU.add))
    for step in (1.25, 0.75, 0.25):
        link(v.scalar_tensor_tensor(out=level, in0=mag, scalar=step, in1=level, op0=ALU.is_gt, op1=ALU.add))
    link(v.tensor_tensor(level, level, over_last(half, BLOCK), ALU.mult))
    wait_sign()
    return v.tensor_tensor(dst, level, sign, ALU.mult)


def stage_fp4_ffn(c, w_gate_up, w_down):
    nc = c.nc
    with c.scope() as s:
        BT = GRP // P
        rows = 3 * P
        xq = s.sb("f4_xq", [P, TILES, P])
        xqT = s.sb("f4_xqT", [P, TOK])
        w_rows = s.sb("f4_w_rows", [P, 6, P])
        wd_rows = s.sb("f4_wd_rows", [P, HIDDEN])
        wT = s.sb("f4_wT", [P, 2, rows])
        wdT = s.sb("f4_wdT", [P, 3, P])
        hid = [s.sb(f"f4_hid{i}", [P, BT, HIDDEN]) for i in range(2)]
        hq = [s.sb(f"f4_hq{i}", [P, BT, HIDDEN]) for i in range(2)]
        hqT = s.sb("f4_hqT", [P, 3, GRP])
        silu = [s.sb(f"f4_silu{i}", [P, HIDDEN]) for i in range(2)]
        size = TILES * P
        sign, mag, level, above = (s.sb(f"f4_{n}", [P, size]) for n in ("sign", "mag", "level", "above"))
        stat = s.sb("f4_stat", [P, 3, size // BLOCK])
        gate = [s.ps(f"f4_pg{i}", [P, HIDDEN]) for i in range(2)]
        up = [s.ps(f"f4_pu{i}", [P, HIDDEN]) for i in range(2)]
        pt = [s.ps(f"f4_pt{i}", [P, GRP]) for i in range(3)]
        po = s.ps("f4_po", [P, GRP])
        loaded, step_done, signed = s.sem("f4_loaded"), s.sem("f4_step"), s.sem("f4_signed")
        rounded, turned, placed = s.sem("f4_rounded"), s.sem("f4_turned"), s.sem("f4_placed")
        gu_done, silu_done, prod_done = s.sem("f4_gu_done"), s.sem("f4_silu_done"), s.sem("f4_prod_done")
        h_turned, h_placed, down_done, added = s.sem("f4_h_turned"), s.sem("f4_h_placed"), s.sem("f4_down"), s.sem("f4_added")
        block = s.block()
        chunk = [(0, P), (P, P), (2 * P, HIDDEN - 2 * P)]

        def blocks(ap):
            return ap.rearrange("p (k m) -> p k m", m=BLOCK)

        jobs = [(c.xn[:, :, :].rearrange("p t d -> p (t d)"), xq[:, :, :].rearrange("p t d -> p (t d)")),
                (w_rows[:, :, :].rearrange("p t d -> p (t d)"), w_rows[:, :, :].rearrange("p t d -> p (t d)")),
                (wd_rows[:, :], wd_rows[:, :])]
        jobs += [(hid[g % 2][:, :, :].rearrange("p t d -> p (t d)"), hq[g % 2][:, :, :].rearrange("p t d -> p (t d)"))
                 for g in range(GROUPS)]

        @block.sync
        def _(sp):
            sp.dma_start(w_rows[:, :, :], w_gate_up.rearrange("(t p) d -> p t d", p=P)).then_inc(loaded, 16)
            sp.dma_start(wd_rows[:, :], w_down).then_inc(loaded, 16)

        @block.vector
        def _(dve):
            count = [0]

            def link(ins):
                count[0] += 1
                ins.then_inc(step_done, 1)
                dve.wait_ge(step_done, count[0])

            def job(j):
                src, dst = jobs[j]
                n = src.shape[1]
                fp4_round(nc, link, blocks(src), blocks(sign[:, 0:n]), lambda: dve.wait_ge(signed, j + 1),
                          blocks(mag[:, 0:n]), blocks(level[:, 0:n]), blocks(above[:, 0:n]),
                          stat[:, :, 0:n // BLOCK], blocks(dst)).then_inc(rounded, 1)

            def gated(g):
                if g >= 2:
                    dve.wait_ge(rounded, 3 + g - 1)
                for t in range(g * BT, (g + 1) * BT):
                    dve.wait_ge(silu_done, t + 1)
                    nc.vector.tensor_tensor(hid[g % 2][:, t % BT, :], up[t % 2][:, :], silu[t % 2][:, :], ALU.mult).then_inc(prod_done, 1)

            job(0)
            dve.wait_ge(loaded, 32)
            job(1)
            job(2)
            gated(0)
            for g in range(GROUPS):
                dve.wait_ge(prod_done, (g + 1) * BT)
                if g >= 2:
                    dve.wait_ge(h_turned, 3 * (g - 1))
                job(3 + g)
                if g + 1 < GROUPS:
                    gated(g + 1)
                dve.wait_ge(down_done, g + 1)
                cols = slice(g * GRP, (g + 1) * GRP)
                nc.vector.tensor_tensor(c.y[:, cols], po[:, :], c.y[:, cols], ALU.add).then_inc(added, 1)

        @block.scalar
        def _(act):
            def signs(j):
                if j >= 1:
                    act.wait_ge(rounded, j)
                src, _ = jobs[j]
                if j >= 3:
                    act.wait_ge(prod_done, (j - 2) * BT)
                nc.scalar.activation(sign[:, 0:src.shape[1]], src, ACT.Sign).then_inc(signed, 1)

            signs(0)
            act.wait_ge(loaded, 32)
            signs(1)
            signs(2)
            for n in range(GROUPS):
                act.wait_ge(turned, n + 1)
                nc.scalar.activation(xqT[:, n * GRP:(n + 1) * GRP], (pt + [po])[n][:, :], ACT.Copy).then_inc(placed, 1)
            for i in range(2):
                act.wait_ge(turned, GROUPS + i + 1)
                nc.scalar.activation(wT[:, i, :], pt[i][:, 0:rows], ACT.Copy).then_inc(placed, 1)
            act.wait_ge(turned, GROUPS + 3)
            nc.scalar.activation(wdT[:, 0:2, :], pt[2][:, 0:2 * P].rearrange("p (a n) -> p a n", n=P), ACT.Copy).then_inc(placed, 1)
            nc.scalar.activation(wdT[0:HIDDEN - 2 * P, 2, :], pt[2][0:HIDDEN - 2 * P, 2 * P:rows], ACT.Copy).then_inc(placed, 1)

            def silus(g):
                for t in range(g * BT, (g + 1) * BT):
                    act.wait_ge(gu_done, t + 1)
                    nc.scalar.activation(silu[t % 2][:, :], gate[t % 2][:, :], ACT.Silu).then_inc(silu_done, 1)

            silus(0)
            for g in range(GROUPS):
                signs(3 + g)
                if g + 1 < GROUPS:
                    silus(g + 1)
                for k, (_, n) in enumerate(chunk):
                    act.wait_ge(h_turned, 3 * g + k + 1)
                    if g:
                        act.wait_ge(down_done, g)
                    nc.scalar.activation(hqT[0:n, k, :], pt[k][0:n, :], ACT.Copy).then_inc(h_placed, 1)

        @block.tensor
        def _(pe):
            pe.wait_ge(rounded, 1)
            for t in range(TILES):
                g, k = divmod(t, BT)
                ins = nc.tensor.transpose((pt + [po])[g][:, k * P:(k + 1) * P], xq[:, t, :], c.ident[:, :])
                if k == BT - 1:
                    ins.then_inc(turned, 1)
            pe.wait_ge(rounded, 2)
            for i in range(2):
                pe.wait_ge(placed, i + 1)
                for k in range(3):
                    ins = nc.tensor.transpose(pt[i][:, k * P:(k + 1) * P], w_rows[:, 3 * i + k, :], c.ident[:, :])
                ins.then_inc(turned, 1)
            pe.wait_ge(rounded, 3)
            pe.wait_ge(placed, 3)
            for k, (at, n) in enumerate(chunk):
                ins = nc.tensor.transpose(pt[2][0:n, k * P:(k + 1) * P], wd_rows[:, at:at + n], c.ident[:, :])
            ins.then_inc(turned, 1)
            pe.wait_ge(placed, GROUPS + 4)

            def gate_ups(g):
                for t in range(g * BT, (g + 1) * BT):
                    if t >= 2:
                        pe.wait_ge(prod_done, t - 1)
                    tile = xqT[:, t * P:(t + 1) * P]
                    nc.tensor.matmul(gate[t % 2][:, :], tile, wT[:, 0, 0:HIDDEN], start=True, stop=True)
                    nc.tensor.matmul(up[t % 2][:, :], tile, wT[:, 1, 0:HIDDEN], start=True, stop=True).then_inc(gu_done, 1)

            gate_ups(0)
            for g in range(GROUPS):
                if g + 1 < GROUPS:
                    gate_ups(g + 1)
                pe.wait_ge(rounded, 3 + g + 1)
                for k, (at, n) in enumerate(chunk):
                    if g:
                        pe.wait_ge(h_placed, 3 * (g - 1) + k + 1)
                    for t in range(BT):
                        ins = nc.tensor.transpose(pt[k][0:n, t * P:(t + 1) * P], hq[g % 2][:, t, at:at + n], c.ident[:, :])
                    ins.then_inc(h_turned, 1)
                pe.wait_ge(h_placed, 3 * (g + 1))
                if g:
                    pe.wait_ge(added, g)
                for k, (at, n) in enumerate(chunk):
                    ins = nc.tensor.matmul(po[:, :], wdT[0:n, k, :], hqT[0:n, k, :], start=k == 0, stop=k == 2)
                ins.then_inc(down_done, 1)



def build(nc, dram):
    with ExitStack() as ctx:
        c = Chip(nc, ctx, dram)

        def share_rows(tag, chunks):
            return nc.dram_tensor(f"{tag}_shares", (2 * chunks, TOK), F32, kind="Internal").ap()

        def experts(layer, rows):
            stage_experts(c, f"e{layer}", dram[f"e{layer}_w"], rows, dram[f"e{layer}_w"].shape[0])

        stage_load(c)

        stage_norm(c, "n0")
        rows = share_rows("e0", dram["e0_w"].shape[0])
        stage_conv_branch(c)
        stage_route_grouped(c, rows)
        experts(0, rows)
        stage_add(c, "s0", also_xn=True)
        c.clear_semaphores()

        stage_norm(c, "n1")
        h = Heads(nc, "a1", 64, 0)
        stage_project_v(c, h, dram["a1_w_v"])
        stage_attend(c, h, 64 ** -0.5, dram["a1_w_qk"])
        stage_attention_out(c, h, dram["a1_w_out"])
        stage_fp4_ffn(c, dram["f1_w_gate_up"], dram["f1_w_down"])
        stage_add(c, "s1", also_xn=False)
        c.clear_semaphores()

        stage_norm(c, "n2")
        h = Heads(nc, "a2", 8, 1)
        stage_project_small(c, h)
        stage_attend(c, h, 4 ** -0.5)
        stage_attention_out(c, h, dram["a2_w_out"])
        rows = share_rows("e2", dram["e2_w"].shape[0])
        stage_route_top2(c, "r2", True, 1, rows)
        experts(2, rows)
        stage_add(c, "s2", also_xn=False)
        c.clear_semaphores()

        stage_norm(c, "n3")
        h = Heads(nc, "a3", 8, 0)
        stage_project_small(c, h)
        stage_attend(c, h, 8 ** -0.5)
        stage_attention_out(c, h, dram["a3_w_out"])
        rows = share_rows("e3", dram["e3_w"].shape[0])
        stage_route_top2(c, "r3", False, 4, rows)
        experts(3, rows)
        stage_add(c, "s3", also_xn=False)

        stage_store(c)


def laid_out(i):
    f = np.float32
    a = {"x": i["L0_attn_x"].reshape(TOK, P)}

    a["ident"] = np.eye(P, dtype=f)
    a["ones"] = np.ones((4, TOK), f)
    a["lower"] = np.tril(np.ones((8, 8), f), -1)[None]
    a["mask_above"] = np.triu(np.full((P, P), MASKED, f), 1)
    a["mask_below"] = np.tril(np.full((P, P), MASKED, f), -1)
    pos = np.arange(SEQ, dtype=f)
    freq = (1.0 / 10000.0 ** (np.arange(0, 4, 2, dtype=f) / 4)).astype(f)
    angle = pos[None, :] * freq[:, None]
    cos, sin = np.ones((HEADS, 8, SEQ), f), np.zeros((HEADS, 8, SEQ), f)
    cos[:, 4:6] = cos[:, 6:8] = np.cos(angle)
    sin[:, 4:6], sin[:, 6:8] = -np.sin(angle), np.sin(angle)
    a["cos"], a["sin"] = cos.reshape(P, SEQ), sin.reshape(P, SEQ)

    for n in range(2):
        taps = i[f"L0_attn_k{n}"][0].T[::-1]
        a[f"k{n}T"] = np.concatenate([np.zeros((CBLK, P), f), taps, np.zeros((CBLK - 1, P), f)])
    a["L0_W_in"], a["L0_W_out"] = i["L0_attn_W_in"], i["L0_attn_W_out"]
    a["L0_b_in"] = i["L0_attn_b_in"][None]
    a["L0_cols"] = np.stack([i["L0_attn_gamma"], i["L0_attn_beta"], i["L0_attn_b_out"]], 1)
    a["r0_w"], a["r0_b"] = i["L0_ffn_router_w"].T, i["L0_ffn_e_bias"][None]

    def pairs(w):
        return w.reshape(-1, 2, P, P // 2).transpose(0, 2, 1, 3).reshape(-1, P, P)

    def joined(gate, up, down):
        return np.concatenate([gate, up, down], 2)

    a["e0_w"] = np.concatenate([
        joined(pairs(i["L0_ffn_Wg"]), pairs(i["L0_ffn_Wu"]), i["L0_ffn_Wd"].reshape(-1, P, P)),
        joined(i["L0_ffn_SWg"][None], i["L0_ffn_SWu"][None], i["L0_ffn_SWd"][None])])

    def twice(w):
        w = w.reshape(P, HEADS, -1).transpose(1, 0, 2)
        return [w, w]

    a["a1_w_qk"] = np.concatenate(twice(i["L1_attn_Wq"]) + twice(i["L1_attn_Wk"]), 2)
    a["a1_w_v"], a["a1_w_out"] = i["L1_attn_Wv"], i["L1_attn_Wo"]
    pad = np.zeros((3 * P - HIDDEN, P), f)
    a["f1_w_gate_up"] = np.concatenate([i["L1_ffn_w_gate"], pad, i["L1_ffn_w_up"], pad])
    a["f1_w_down"] = i["L1_ffn_w_down"]

    def heads(sem, geo):
        return np.concatenate([sem.reshape(-1, HEADS, 4), geo.reshape(-1, HEADS, 4)], 2).reshape(-1, P)

    def partner(geo):
        return geo.reshape(-1, HEADS, 2, 2)[:, :, ::-1].reshape(-1, HEADS * 4)

    g = {n: i[f"L2_attn_{n}"] for n in ("wq_sem", "wk_sem", "wq_geo", "wk_geo", "k_sem_null", "k_geo_null")}
    for n in ("wq", "wk"):
        a[f"a2_{n}"] = heads(g[f"{n}_sem"], g[f"{n}_geo"])
        a[f"a2_{n}_turn"] = heads(g[f"{n}_sem"], partner(g[f"{n}_geo"]))
    a["a2_wv"], a["a2_w_out"] = i["L2_attn_wv"], i["L2_attn_wo"]
    a["a2_k_null"] = heads(g["k_sem_null"][None], g["k_geo_null"][None]).T
    v_null = np.zeros((1, HEADS, 32), f)
    v_null[0, :, 0:8] = i["L2_attn_v_null"].reshape(HEADS, 8)
    v_null[0, :, 8] = 1.0
    a["a2_v_null"] = v_null
    a["r2_w"], a["r2_b"] = i["L2_ffn_router_w"], i["L2_ffn_router_b"][None]
    a["e2_w"] = np.concatenate([
        joined(pairs(i[f"L2_ffn_{n}_w1"]), pairs(i[f"L2_ffn_{n}_w3"]), i[f"L2_ffn_{n}_w2"].reshape(-1, P, P))
        for n in ("routed", "shared")])

    for n in "qkv":
        a[f"a3_w{n}"] = i[f"L3_attn_W_{n.upper()}"]
    a["a3_w_out"] = i["L3_attn_W_o"]
    a["r3_w"], a["r3_b"] = i["L3_ffn_router_w"].T, i["L3_ffn_routing_bias"][None]

    def hidden_rows(w):
        return w.reshape(-1, P, P).transpose(0, 2, 1)

    def down_columns(w):
        return w.reshape(-1, P, 2, P).transpose(0, 2, 3, 1).reshape(-1, P, P)

    a["e3_w"] = np.concatenate([
        joined(hidden_rows(i["L3_ffn_wg"]), hidden_rows(i["L3_ffn_wu"]), down_columns(i["L3_ffn_wd"])),
        joined(hidden_rows(i["L3_ffn_sg_w"]), hidden_rows(i["L3_ffn_su_w"]), down_columns(i["L3_ffn_sd_w"]))])
    return {n: np.ascontiguousarray(v) for n, v in a.items()}


def kernel(**inputs):
    import concourse.bacc as bacc
    from concourse.bass_utils import run_bass_kernel_spmd

    nc = bacc.Bacc("TRN2", target_bir_lowering=False, num_devices=1)
    arrays = laid_out({n: np.asarray(v) for n, v in inputs.items()})
    dram = {n: nc.dram_tensor(f"in_{n}", v.shape, mybir.dt.from_np(v.dtype), kind="ExternalInput").ap()
            for n, v in arrays.items()}
    dram["out"] = nc.dram_tensor("out", (TOK, P), F32, kind="ExternalOutput").ap()
    build(nc, dram)
    result = run_bass_kernel_spmd(nc, [{f"in_{n}": v for n, v in arrays.items()}], core_ids=[0])
    return result.results[0]["out"].reshape(BATCH, SEQ, P)
```

```python
from contextlib import ExitStack

import concourse.bass as bass
import numpy as np
from concourse import mybir

F32 = mybir.dt.float32
BF16 = mybir.dt.bfloat16
ALU = mybir.AluOpType
ACT = mybir.ActivationFunctionType
AX = mybir.AxisListType

P = 128
BATCH, SEQ = 2, 1024
TOK = BATCH * SEQ
TILES = TOK // P
GRP = 512
GROUPS = TOK // GRP
HEADS = 16
EPS = 1e-5
MASKED = -1e30
CBLK = 32
CWIN = 128
CPAD = CWIN - CBLK
TAPS = 128
NBLK = SEQ // CBLK


def dram_view(ap, offset, dims):
    return bass.AP(tensor=ap.tensor, offset=offset, ap=dims)


class Chip:

    def __init__(self, nc, ctx, dram):
        self.nc, self.ctx, self.dram = nc, ctx, dram
        self.taken = []

        def resident(name, shape):
            return ctx.enter_context(nc.sbuf_tensor(name, shape, F32))

        self.x = resident("x_tokens", [P, TILES, P])
        self.xn = resident("xn_tokens", [P, TILES, P])
        self.xnT = resident("xn_channels", [P, TOK])
        self.y = resident("y_channels", [P, TOK])
        self.ident = resident("identity", [P, P])

    def scope(self):
        return Scope(self)

    def semaphore(self, name):
        self.taken.append(self.nc.alloc_semaphore(name))
        return self.taken[-1]

    def clear_semaphores(self):
        self.nc.clear_and_free_semaphores(self.taken)
        self.nc.all_engine_barrier()
        self.taken = []


class Scope:

    def __init__(self, chip):
        self.chip, self.nc = chip, chip.nc

    def __enter__(self):
        self.ctx = ExitStack()
        self.ctx.__enter__()
        return self

    def __exit__(self, *exc):
        return self.ctx.__exit__(*exc)

    def sb(self, name, shape, dt=F32):
        return self.ctx.enter_context(self.nc.sbuf_tensor(f"{name}_sb", shape, dt))

    def ps(self, name, shape, dt=F32):
        return self.ctx.enter_context(self.nc.psum_tensor(name, shape, dt))

    def sem(self, name):
        return self.chip.semaphore(name)

    def block(self):
        return self.ctx.enter_context(self.nc.Block())


def over_last(ap, n):
    return ap.unsqueeze(len(ap.shape)).to_broadcast(list(ap.shape) + [n])



def stage_load(c):
    nc = c.nc
    with c.scope() as s:
        loaded = s.sem("ld_loaded")
        block = s.block()

        @block.sync
        def _(sp):
            sp.dma_start(c.x[:, :, :], c.dram["x"].rearrange("(t p) d -> p t d", p=P)).then_inc(loaded, 16)
            sp.dma_start(c.ident[:, :], c.dram["ident"]).then_inc(loaded, 16)
            sp.wait_ge(loaded, 32)


def norm_steps(nc, dve, step_done, src, dst, scratch, stat):
    count = [0]

    def link(ins):
        count[0] += 1
        ins.then_inc(step_done, 1)
        dve.wait_ge(step_done, count[0])

    def before_root():
        link(nc.vector.tensor_reduce(out=stat[:, 0, :], in_=src, op=ALU.add, axis=AX.X))
        link(nc.vector.tensor_scalar(stat[:, 1, :], stat[:, 0, :], 1.0 / P, None, ALU.mult))
        link(nc.vector.tensor_tensor(dst, src, over_last(stat[:, 1, :], P), ALU.subtract))
        link(nc.vector.tensor_tensor(scratch, dst, dst, ALU.mult))
        link(nc.vector.tensor_reduce(out=stat[:, 2, :], in_=scratch, op=ALU.add, axis=AX.X))
        return nc.vector.tensor_scalar(stat[:, 3, :], stat[:, 2, :], 1.0 / P, EPS, ALU.mult, ALU.add)

    def after_root():
        link(nc.vector.reciprocal(stat[:, 5, :], stat[:, 4, :]))
        return nc.vector.tensor_tensor(dst, dst, over_last(stat[:, 5, :], P), ALU.mult)

    return before_root, after_root


def stage_norm(c, tag):
    nc = c.nc
    with c.scope() as s:
        scratch = s.sb(f"{tag}_sq", [P, TILES, P])
        stat = s.sb(f"{tag}_stat", [P, 6, TILES])
        tp = [s.ps(f"{tag}_tp{g}", [P, GRP]) for g in range(GROUPS)]
        step_done, var_ready, root_ready = s.sem(f"{tag}_step"), s.sem(f"{tag}_var"), s.sem(f"{tag}_root")
        xn_ready, turned = s.sem(f"{tag}_xn"), s.sem(f"{tag}_turned")
        block = s.block()

        @block.vector
        def _(dve):
            before_root, after_root = norm_steps(nc, dve, step_done, c.x[:, :, :], c.xn[:, :, :], scratch[:, :, :], stat)
            before_root().then_inc(var_ready, 1)
            dve.wait_ge(root_ready, 1)
            after_root().then_inc(xn_ready, 1)
            for g in range(1, GROUPS, 2):
                dve.wait_ge(turned, g + 1)
                nc.vector.tensor_copy(c.xnT[:, g * GRP:(g + 1) * GRP], tp[g][:, :])

        @block.scalar
        def _(act):
            act.wait_ge(var_ready, 1)
            nc.scalar.activation(stat[:, 4, :], stat[:, 3, :], ACT.Sqrt).then_inc(root_ready, 1)
            for g in range(0, GROUPS, 2):
                act.wait_ge(turned, g + 1)
                nc.scalar.activation(c.xnT[:, g * GRP:(g + 1) * GRP], tp[g][:, :], ACT.Copy)

        @block.tensor
        def _(pe):
            pe.wait_ge(xn_ready, 1)
            for t in range(TILES):
                g, k = divmod(t, GRP // P)
                ins = nc.tensor.transpose(tp[g][:, k * P:(k + 1) * P], c.xn[:, t, :], c.ident[:, :])
                if k == GRP // P - 1:
                    ins.then_inc(turned, 1)


def stage_add(c, tag, also_xn):
    nc = c.nc
    with c.scope() as s:
        tp = [s.ps(f"{tag}_tp{g}", [P, GRP // P, P]) for g in range(GROUPS)]
        turned, res_added = s.sem(f"{tag}_turned"), s.sem(f"{tag}_res")
        block = s.block()

        @block.tensor
        def _(pe):
            for t in range(TILES):
                g, k = divmod(t, GRP // P)
                ins = nc.tensor.transpose(tp[g][:, k, :], c.y[:, t * P:(t + 1) * P], c.ident[:, :])
                if k == GRP // P - 1:
                    ins.then_inc(turned, 1)

        @block.vector
        def _(dve):
            if also_xn:
                nc.vector.tensor_tensor(c.x[:, :, :], c.x[:, :, :], c.xn[:, :, :], ALU.add).then_inc(res_added, 1)
                dve.wait_ge(res_added, 1)
            per = GRP // P
            for g in range(GROUPS):
                dve.wait_ge(turned, g + 1)
                nc.vector.tensor_tensor(c.x[:, g * per:(g + 1) * per, :], tp[g][:, :, :],
                                        c.x[:, g * per:(g + 1) * per, :], ALU.add)


def stage_store(c):
    nc = c.nc
    with c.scope() as s:
        stored = s.sem("st_stored")
        block = s.block()

        @block.sync
        def _(sp):
            sp.dma_start(c.dram["out"].rearrange("(t p) d -> p t d", p=P), c.x[:, :, :]).then_inc(stored, 16)
            sp.wait_ge(stored, 16)



def stage_conv_branch(c):
    nc = c.nc
    with c.scope() as s:
        ncol = NBLK + 1
        xT = s.sb("cv_xT", [P, BATCH, CPAD + SEQ])
        valid = s.sb("cv_valid", [1, CPAD + SEQ])
        w_in = s.sb("cv_w_in", [P, 3 * P])
        b_in = s.sb("cv_b_in", [1, 3 * P])
        w_out = s.sb("cv_w_out", [P, P])
        cols = s.sb("cv_cols", [P, 3])
        stat = s.sb("cv_stat", [P, 6, TILES])
        n2 = c.y[:, :].rearrange("p (t d) -> p t d", d=P)
        toep = [s.sb(f"cv_toep{i}", [P, CBLK, P]) for i in range(2)]
        tail = s.sb("cv_tail", [CBLK, CBLK, P])
        win = s.sb("cv_win", [P, P, BATCH, ncol])
        gate = s.sb("cv_gate", [P, 2 * P, BATCH, NBLK])
        x2 = gate[:, P:2 * P, :, :]
        yT = s.sb("cv_yT", [P, BATCH, SEQ])
        bank = [s.ps(f"cv_bank{i}", [P, 512]) for i in range(8)]
        loaded, zeroed = s.sem("cv_loaded"), s.sem("cv_zeroed")
        taps_in = [s.sem(f"cv_taps{i}") for i in range(2)]
        step_done, var_ready, root_ready = s.sem("cv_step"), s.sem("cv_var"), s.sem("cv_root")
        n2_ready, turned, xT_ready = s.sem("cv_n2r"), s.sem("cv_turned"), s.sem("cv_xTr")
        projected, copied = s.sem("cv_proj"), [s.sem(f"cv_copied{i}") for i in range(2)]
        conv_done, gated = [s.sem(f"cv_conv{i}") for i in range(2)], [s.sem(f"cv_gated{i}") for i in range(2)]
        shifted_act, shifted_pool = s.sem("cv_sha"), s.sem("cv_shp")
        y_turned, yT_ready, out_done = s.sem("cv_yt"), s.sem("cv_ytr"), s.sem("cv_out")
        block = s.block()
        GATES = slice(CPAD, P)
        CH = 8
        BLKS = BATCH * NBLK
        Q3 = slice(96, 128)

        @block.sync
        def _(sp):
            for i, taps in enumerate(("k0T", "k1T")):
                k = c.dram[taps]
                sp.dma_start(toep[i][:, :, :], dram_view(k, (2 * CBLK - 1) * P, [[P, P], [-P, CBLK], [1, P]])).then_inc(taps_in[i], 16)
                if i == 1:
                    sp.wait_ge(conv_done[0], P // 8)
                sp.dma_start(tail[:, :, :], dram_view(k, (CBLK - 1) * P, [[P, CBLK], [-P, CBLK], [1, P]])).then_inc(taps_in[i], 16)

        @block.gpsimd
        def _(pool):
            nc.gpsimd.memset(xT[:, :, 0:CPAD], 0.0).then_inc(zeroed, 1)
            nc.gpsimd.memset(valid[:, 0:CPAD], 0.0).then_inc(zeroed, 1)
            nc.gpsimd.memset(valid[:, CPAD:], 1.0).then_inc(zeroed, 1)
            if True:
                nc.gpsimd.memset(win[:, :, :, 0:CPAD // CBLK + 1], 0.0).then_inc(zeroed, 1)
            for n in range(P // CH):
                pool.wait_ge(gated[0], n + 1)
                ch = slice(n * CH, (n + 1) * CH)
                nc.gpsimd.tensor_copy(win[64:96, ch, :, 2:ncol], win[Q3, ch, :, 1:ncol - 1]).then_inc(shifted_pool, 1)

        @block.vector
        def _(dve):
            before_root, after_root = norm_steps(nc, dve, step_done, c.xn[:, :, :], n2,
                                                 yT[:, :, :].rearrange("p b (t d) -> p (b t) d", d=P), stat)
            before_root().then_inc(var_ready, 1)
            dve.wait_ge(root_ready, 1)
            after_root().then_inc(n2_ready, 1)
            dve.wait_ge(zeroed, 4)
            for a in range(0, BLKS, 2):
                dve.wait_ge(projected, a + 1)
                nc.vector.tensor_copy(win[:, :, a // NBLK, 1 + a % NBLK], bank[a % 8][:, 0:P])
                nc.vector.tensor_copy(gate[Q3, :, a // NBLK, a % NBLK], bank[a % 8][Q3, P:3 * P]).then_inc(copied[0], 1)
            for i in range(2):
                dve.wait_ge(copied[i], BLKS // 2)
            for i in range(2):
                for n in range(P // CH):
                    dve.wait_ge(conv_done[i], n + 1)
                    ch = slice(n * CH, (n + 1) * CH)
                    src = bank[n % 4][Q3, :].rearrange("p (d b a) -> p d b a", b=BATCH, a=NBLK)
                    dst = win[Q3, ch, :, 1:ncol] if i == 0 else x2[Q3, ch, :, :]
                    nc.vector.tensor_tensor(dst, src, gate[Q3, slice(i * P + n * CH, i * P + (n + 1) * CH), :, :],
                                            ALU.mult).then_inc(gated[i], 1)

        @block.scalar
        def _(act):
            for dst, name in ((w_in, "L0_W_in"), (b_in, "L0_b_in"), (w_out, "L0_W_out"), (cols, "L0_cols")):
                act.dma_start(dst[:, :], c.dram[name]).then_inc(loaded, 16)
            act.wait_ge(var_ready, 1)
            nc.scalar.activation(stat[:, 4, :], stat[:, 3, :], ACT.Sqrt).then_inc(root_ready, 1)
            act.wait_ge(loaded, 64)
            per = SEQ // GRP
            for g in range(GROUPS):
                act.wait_ge(turned, g + 1)
                at = CPAD + (g % per) * GRP
                nc.scalar.activation(xT[:, g // per, at:at + GRP], bank[g][:, :], ACT.Identity,
                                     bias=cols[:, 1:2], scale=cols[:, 0:1]).then_inc(xT_ready, 1)
            for a in range(1, BLKS, 2):
                act.wait_ge(projected, a + 1)
                nc.scalar.activation(win[:, :, a // NBLK, 1 + a % NBLK], bank[a % 8][:, 0:P], ACT.Copy)
                nc.scalar.activation(gate[Q3, :, a // NBLK, a % NBLK], bank[a % 8][Q3, P:3 * P], ACT.Copy).then_inc(copied[1], 1)
            for n in range(P // CH):
                act.wait_ge(gated[0], n + 1)
                ch = slice(n * CH, (n + 1) * CH)
                nc.scalar.activation(win[32:64, ch, :, 3:ncol], win[Q3, ch, :, 1:ncol - 2], ACT.Copy)
                nc.scalar.activation(win[0:32, ch, :, 4:ncol], win[Q3, ch, :, 1:ncol - 3], ACT.Copy).then_inc(shifted_act, 1)
            for g in range(GROUPS):
                act.wait_ge(y_turned, g + 1)
                nc.scalar.activation(yT[:, g // per, (g % per) * GRP:(g % per + 1) * GRP], bank[4 + g][:, :],
                                     ACT.Copy).then_inc(yT_ready, 1)
            for g in range(GROUPS):
                act.wait_ge(out_done, g + 1)
                nc.scalar.activation(c.y[:, g * GRP:(g + 1) * GRP], bank[g][:, :], ACT.Identity, bias=cols[:, 2:3])

        @block.tensor
        def _(pe):
            pe.wait_ge(n2_ready, 1)
            for t in range(TILES):
                g, k = divmod(t, GRP // P)
                ins = nc.tensor.transpose(bank[g][:, k * P:(k + 1) * P], n2[:, t, :], c.ident[:, :])
                if k == GRP // P - 1:
                    ins.then_inc(turned, 1)
            pe.wait_ge(xT_ready, GROUPS)
            pe.wait_ge(zeroed, 4)
            pe.wait_ge(loaded, 64)
            for a in range(BLKS):
                if a >= 8:
                    pe.wait_ge(copied[a % 2], (a - 8) // 2 + 1)
                b, at = a // NBLK, (a % NBLK) * CBLK
                nc.tensor.matmul(bank[a % 8][:, 0:3 * P], xT[:, b, at:at + CWIN], w_in[:, :], start=True, stop=False)
                nc.tensor.matmul(bank[a % 8][:, 0:3 * P], valid[:, at:at + CWIN], b_in[:, :],
                                 start=False, stop=True).then_inc(projected, 1)
            for k in range(2):
                pe.wait_ge(copied[k], BLKS // 2)
            for i in range(2):
                pe.wait_ge(taps_in[i], 32)
                for n in range(P // CH):
                    if n >= 4:
                        pe.wait_ge(gated[i], n - 3)
                    elif i == 1:
                        pe.wait_ge(gated[0], P // CH)
                    if i == 1:
                        pe.wait_ge(shifted_act, n + 1)
                        pe.wait_ge(shifted_pool, n + 1)
                    for k in range(CH):
                        d = n * CH + k
                        out = bank[n % 4][Q3, k * BLKS:(k + 1) * BLKS].rearrange("p (b a) -> p b a", b=BATCH)
                        nc.tensor.matmul(out, toep[i][:, :, d],
                                         win[:, d, :, 1:ncol], start=True, stop=False)
                        ins = nc.tensor.matmul(out, tail[:, :, d],
                                               win[0:CBLK, d, :, 0:ncol - 1], start=False, stop=True)
                    ins.then_inc(conv_done[i], 1)
            pe.wait_ge(gated[1], P // CH)
            for a in range(BLKS):
                g, k = divmod(a, GRP // CBLK)
                ins = nc.tensor.transpose(bank[4 + g][:, k * CBLK:(k + 1) * CBLK],
                                          x2[Q3, :, a // NBLK, a % NBLK], c.ident[Q3, Q3])
                if k == GRP // CBLK - 1:
                    ins.then_inc(y_turned, 1)
            per = SEQ // GRP
            for g in range(GROUPS):
                pe.wait_ge(yT_ready, g + 1)
                nc.tensor.matmul(bank[g][:, :], w_out[:, :], yT[:, g // per, (g % per) * GRP:(g % per + 1) * GRP],
                                 start=True, stop=True).then_inc(out_done, 1)



def rank_below(nc, link, score, lower, work, rank):
    earlier, equal = work
    shape = [P, TILES, 8, 8]
    of_j = score.unsqueeze(2).to_broadcast(shape)
    of_i = score.unsqueeze(3).to_broadcast(shape)
    link(nc.vector.tensor_tensor(equal, of_j, of_i, ALU.is_equal))
    link(nc.vector.tensor_tensor(equal, equal, lower.unsqueeze(1).to_broadcast(shape), ALU.mult))
    link(nc.vector.tensor_tensor(earlier, of_j, of_i, ALU.is_gt))
    link(nc.vector.tensor_tensor(earlier, earlier, equal, ALU.add))
    link(nc.vector.tensor_reduce(out=rank, in_=earlier, op=ALU.add, axis=AX.X))


def store_rows(sp, c, rows, shares, experts, copies, shared_rows, wait_rows, stored):
    n = 0
    for k in range(copies):
        sp.dma_start(rows.rearrange("(e k) n -> e k n", k=copies)[0:experts, k, :], shares).then_inc(stored, 16)
        n += 16
    sp.dma_start(rows[experts * copies:experts * copies + shared_rows, :], c.dram["ones"][0:shared_rows, :]).then_inc(stored, 16)
    n += 16
    sp.wait_ge(stored, n)


def stage_route_top2(c, tag, softmax, copies, rows):
    nc = c.nc
    E = 8
    with c.scope() as s:
        w = s.sb(f"{tag}_w", [P, E])
        bias = s.sb(f"{tag}_bias", [P, E])
        lower = s.sb(f"{tag}_lower", [P, E, E])
        logit = s.sb(f"{tag}_logit", [P, TILES, E])
        score = s.sb(f"{tag}_score", [P, TILES, E]) if not softmax else logit
        earlier, equal = s.sb(f"{tag}_earlier", [P, TILES, E, E]), s.sb(f"{tag}_equal", [P, TILES, E, E])
        rank = s.sb(f"{tag}_rank", [P, TILES, E])
        share = s.sb(f"{tag}_share", [P, TILES, E])
        stat = s.sb(f"{tag}_stat", [P, 3, TILES])
        shares = s.sb(f"{tag}_shares", [E, TOK])
        pl = s.ps(f"{tag}_pl", [P, TILES, E])
        pt = [s.ps(f"{tag}_pt{g}", [E, GRP]) for g in range(GROUPS)]
        loaded, logits_ready, step_done = s.sem(f"{tag}_loaded"), s.sem(f"{tag}_logits"), s.sem(f"{tag}_step")
        act_in, act_out, share_ready = s.sem(f"{tag}_actin"), s.sem(f"{tag}_actout"), s.sem(f"{tag}_share_r")
        turned, rows_ready, stored = s.sem(f"{tag}_turned"), s.sem(f"{tag}_rows"), s.sem(f"{tag}_stored")
        block = s.block()

        @block.sync
        def _(sp):
            sp.dma_start(w[:, :], c.dram[f"{tag}_w"]).then_inc(loaded, 16)
            sp.dma_start(bias[:, :], c.dram[f"{tag}_b"].to_broadcast([P, E])).then_inc(loaded, 16)
            sp.dma_start(lower[:, :, :], c.dram["lower"].to_broadcast([P, E, E])).then_inc(loaded, 16)
            sp.wait_ge(rows_ready, GROUPS)
            store_rows(sp, c, rows, shares[:, :], E, copies, 2 * copies if copies == 1 else copies, None, stored)

        @block.tensor
        def _(pe):
            pe.wait_ge(loaded, 48)
            for t in range(TILES):
                ins = nc.tensor.matmul(pl[:, t, :], c.xnT[:, t * P:(t + 1) * P], w[:, :], start=True, stop=True)
            ins.then_inc(logits_ready, 1)
            pe.wait_ge(share_ready, 1)
            for t in range(TILES):
                g, k = divmod(t, GRP // P)
                ins = nc.tensor.transpose(pt[g][:, k * P:(k + 1) * P], share[:, t, :], c.ident[:, :])
                if k == GRP // P - 1:
                    ins.then_inc(turned, 1)

        @block.vector
        def _(dve):
            count = [0]

            def link(ins):
                count[0] += 1
                ins.then_inc(step_done, 1)
                dve.wait_ge(step_done, count[0])

            dve.wait_ge(loaded, 48)
            dve.wait_ge(logits_ready, 1)
            link(nc.vector.tensor_tensor(logit[:, :, :], pl[:, :, :], bias[:, :].unsqueeze(1).to_broadcast([P, TILES, E]), ALU.add))
            if softmax:
                link(nc.vector.tensor_reduce(out=stat[:, 0, :], in_=logit[:, :, :], op=ALU.max, axis=AX.X))
                nc.vector.tensor_tensor(share[:, :, :], logit[:, :, :], over_last(stat[:, 0, :], E), ALU.subtract).then_inc(act_in, 1)
            else:
                nc.vector.memset(stat[:, 0, :], 0.0).then_inc(act_in, 1)
                dve.wait_ge(act_out, 1)
            rank_below(nc, link, score[:, :, :], lower[:, :, :], (earlier[:, :, :, :], equal[:, :, :, :]), rank[:, :, :])
            link(nc.vector.tensor_scalar(rank[:, :, :], rank[:, :, :], 1.5, None, ALU.is_lt))
            dve.wait_ge(act_out, 1)
            src = share if softmax else score
            link(nc.vector.tensor_tensor(share[:, :, :], src[:, :, :], rank[:, :, :], ALU.mult))
            link(nc.vector.tensor_reduce(out=stat[:, 1, :], in_=share[:, :, :], op=ALU.add, axis=AX.X))
            link(nc.vector.reciprocal(stat[:, 2, :], stat[:, 1, :]))
            nc.vector.tensor_tensor(share[:, :, :], share[:, :, :], over_last(stat[:, 2, :], E), ALU.mult).then_inc(share_ready, 1)
            for g in range(GROUPS):
                dve.wait_ge(turned, g + 1)
                nc.vector.tensor_copy(shares[:, g * GRP:(g + 1) * GRP], pt[g][:, :]).then_inc(rows_ready, 1)

        @block.scalar
        def _(act):
            act.wait_ge(act_in, 1)
            if softmax:
                nc.scalar.activation(share[:, :, :], share[:, :, :], ACT.Exp).then_inc(act_out, 1)
            else:
                nc.scalar.activation(score[:, :, :], logit[:, :, :], ACT.Sigmoid).then_inc(act_out, 1)


def stage_route_grouped(c, rows):
    nc = c.nc
    E, G = 64, 8
    M = E // G
    with c.scope() as s:
        w = s.sb("r0_w_sb", [P, E])
        bias = s.sb("r0_bias", [P, E])
        lower = s.sb("r0_lower", [P, G, G])
        score = s.sb("r0_score", [P, TILES, E])
        pick = s.sb("r0_pick", [P, TILES, E])
        left = s.sb("r0_left", [P, TILES, E])
        flag = s.sb("r0_flag", [P, TILES, E])
        top = s.sb("r0_top", [P, TILES, 8])
        group = s.sb("r0_group", [P, 5, TILES * G])
        earlier, equal = s.sb("r0_earlier", [P, TILES, G, G]), s.sb("r0_equal", [P, TILES, G, G])
        rank = s.sb("r0_rank", [P, TILES, G])
        stat = s.sb("r0_stat", [P, 3, TILES])
        shares = s.sb("r0_shares", [E, TOK])
        pl = [s.ps(f"r0_pl{i}", [P, TILES // 2, E]) for i in range(2)]
        pt = [s.ps(f"r0_pt{g}", [E, GRP]) for g in range(GROUPS)]
        loaded, logits_ready, step_done = s.sem("r0_loaded"), s.sem("r0_logits"), s.sem("r0_step")
        scores_ready, share_ready = s.sem("r0_scores"), s.sem("r0_share_r")
        turned, rows_ready, stored = s.sem("r0_turned"), s.sem("r0_rows"), s.sem("r0_stored")
        block = s.block()

        @block.sync
        def _(sp):
            sp.dma_start(w[:, :], c.dram["r0_w"]).then_inc(loaded, 16)
            sp.dma_start(bias[:, :], c.dram["r0_b"].to_broadcast([P, E])).then_inc(loaded, 16)
            sp.dma_start(lower[:, :, :], c.dram["lower"].to_broadcast([P, G, G])).then_inc(loaded, 16)
            sp.wait_ge(rows_ready, GROUPS)
            store_rows(sp, c, rows, shares[:, :], E, 1, 2, None, stored)

        @block.tensor
        def _(pe):
            pe.wait_ge(loaded, 48)
            for t in range(TILES):
                i, k = divmod(t, TILES // 2)
                ins = nc.tensor.matmul(pl[i][:, k, :], c.xnT[:, t * P:(t + 1) * P], w[:, :], start=True, stop=True)
                if k == TILES // 2 - 1:
                    ins.then_inc(logits_ready, 1)
            pe.wait_ge(share_ready, 1)
            for t in range(TILES):
                g, k = divmod(t, GRP // P)
                ins = nc.tensor.transpose(pt[g][:, k * P:(k + 1) * P], pick[:, t, :], c.ident[:, :])
                if k == GRP // P - 1:
                    ins.then_inc(turned, 1)

        @block.scalar
        def _(act):
            for i in range(2):
                act.wait_ge(logits_ready, i + 1)
                half = slice(i * TILES // 2, (i + 1) * TILES // 2)
                nc.scalar.activation(score[:, half, :], pl[i][:, :, :], ACT.Sigmoid).then_inc(scores_ready, 1)

        @block.vector
        def _(dve):
            count = [0]

            def link(ins):
                count[0] += 1
                ins.then_inc(step_done, 1)
                dve.wait_ge(step_done, count[0])

            v = nc.vector
            dve.wait_ge(loaded, 48)
            dve.wait_ge(scores_ready, 2)
            link(v.tensor_tensor(pick[:, :, :], score[:, :, :], bias[:, :].unsqueeze(1).to_broadcast([P, TILES, E]), ALU.add))
            grouped = pick[:, :, :].rearrange("p t (g m) -> p (t g) m", m=M)
            flags = flag[:, :, :].rearrange("p t (g m) -> p (t g) m", m=M)
            best, second, number, best_again, total = (group[:, i, :] for i in range(5))
            link(v.tensor_reduce(out=best, in_=grouped, op=ALU.max, axis=AX.X))
            link(v.tensor_tensor(flags, grouped, over_last(best, M), ALU.is_equal))
            link(v.tensor_reduce(out=number, in_=flags, op=ALU.add, axis=AX.X))
            link(v.scalar_tensor_tensor(out=flag[:, :, :], in0=flag[:, :, :], scalar=MASKED, in1=pick[:, :, :], op0=ALU.mult, op1=ALU.add))
            link(v.tensor_reduce(out=second, in_=flags, op=ALU.max, axis=AX.X))
            link(v.tensor_scalar(number, number, 1.5, None, ALU.is_gt))
            link(v.tensor_scalar(number, number, -MASKED, MASKED, ALU.mult, ALU.add))
            link(v.tensor_tensor(best_again, number, best, ALU.add))
            link(v.tensor_tensor(second, second, best_again, ALU.max))
            link(v.tensor_tensor(total, best, second, ALU.add))
            rank_below(nc, link, total.rearrange("p (t g) -> p t g", g=G), lower[:, :, :],
                       (earlier[:, :, :, :], equal[:, :, :, :]), rank[:, :, :])
            link(v.tensor_scalar(rank[:, :, :], rank[:, :, :], 3.5, None, ALU.is_lt))
            link(v.tensor_tensor(grouped, grouped, over_last(rank[:, :, :].rearrange("p t g -> p (t g)"), M), ALU.mult))
            link(v.tensor_scalar(pick[:, :, :], pick[:, :, :], 0.0, None, ALU.add))
            for t in range(TILES):
                ins = v.max(out=top[:, t, :], in_=pick[:, t, :])
            link(ins)
            for t in range(TILES):
                ins = v.match_replace(out=left[:, t, :], in_to_replace=top[:, t, :], in_values=pick[:, t, :], imm_value=3 * MASKED)
            link(ins)
            link(v.tensor_tensor(flag[:, :, :], pick[:, :, :], left[:, :, :], ALU.not_equal))
            link(v.tensor_tensor(pick[:, :, :], flag[:, :, :], score[:, :, :], ALU.mult))
            link(v.tensor_reduce(out=stat[:, 0, :], in_=pick[:, :, :], op=ALU.add, axis=AX.X))
            link(v.tensor_scalar(stat[:, 1, :], stat[:, 0, :], 1e-20, None, ALU.add))
            link(v.reciprocal(stat[:, 2, :], stat[:, 1, :]))
            link(v.tensor_scalar(stat[:, 2, :], stat[:, 2, :], 2.5, None, ALU.mult))
            v.tensor_tensor(pick[:, :, :], pick[:, :, :], over_last(stat[:, 2, :], E), ALU.mult).then_inc(share_ready, 1)
            for g in range(GROUPS):
                dve.wait_ge(turned, g + 1)
                v.tensor_copy(shares[:, g * GRP:(g + 1) * GRP], pt[g][:, :]).then_inc(rows_ready, 1)



def stage_experts(c, tag, weights, rows, chunks):
    nc = c.nc
    HB = 2
    with c.scope() as s:
        w_gu = [s.sb(f"{tag}_gu{i}", [P, 2 * P]) for i in range(HB)]
        w_dn = [s.sb(f"{tag}_dn{i}", [P, P]) for i in range(HB)]
        share = [s.sb(f"{tag}_share{i}", [P, TOK]) for i in range(HB)]
        hidden = [s.sb(f"{tag}_hidden{i}", [P, TOK]) for i in range(HB)]
        silu = [s.sb(f"{tag}_silu{i}", [P, GRP]) for i in range(2)]
        prod = [s.sb(f"{tag}_prod{i}", [P, GRP]) for i in range(2)]
        zeros = s.sb(f"{tag}_zeros", [P, GRP], BF16)
        gate = [s.ps(f"{tag}_pg{i}", [P, GRP]) for i in range(2)]
        up = [s.ps(f"{tag}_pu{i}", [P, GRP]) for i in range(2)]
        down = [s.ps(f"{tag}_pd{g}", [P, GRP]) for g in range(GROUPS)]
        gu_in, dn_in = [s.sem(f"{tag}_gu_in{i}") for i in range(HB)], [s.sem(f"{tag}_dn_in{i}") for i in range(HB)]
        share_in = [s.sem(f"{tag}_share_in{i}") for i in range(HB)]
        gu_done, silu_done, prod_done = s.sem(f"{tag}_gu_done"), s.sem(f"{tag}_silu_done"), s.sem(f"{tag}_prod_done")
        hidden_done, down_done, zeroed = s.sem(f"{tag}_hidden_done"), s.sem(f"{tag}_down_done"), s.sem(f"{tag}_zeroed")
        block = s.block()
        SET = HB * GROUPS
        half = P // 2

        def unit(k, par, g):
            return (k * HB + par) * GROUPS + g

        @block.sync
        def _(sp):
            def load(chunk, par, k):
                if k is not None:
                    sp.wait_ge(gu_done, unit(k, par, 0) - SET + GROUPS)
                sp.dma_start(w_gu[par][:, :], weights[bass.ds(chunk, 1), :, 0:2 * P].rearrange("c d n -> d (c n)")).then_inc(gu_in[par], 16)
                if k is not None:
                    sp.wait_ge(hidden_done, 2 + unit(k, par, 0) - SET + GROUPS)
                for j in range(2):
                    sp.dma_start(share[par][j * half:(j + 1) * half, :],
                                 rows[bass.ds(chunk * 2 + j, 1), :].to_broadcast([half, TOK])).then_inc(share_in[par], 16)
                if k is not None:
                    sp.wait_ge(down_done, unit(k, par, 0) + GROUPS)
                sp.dma_start(w_dn[par][:, :], weights[bass.ds(chunk, 1), :, 2 * P:3 * P].rearrange("c d n -> d (c n)")).then_inc(dn_in[par], 16)

            load(0, 0, None)
            load(1, 1, None)
            if chunks // HB > 1:
                with sp.Fori(1, chunks // HB) as k:
                    for par in range(HB):
                        load(k * HB + par, par, k)
            if chunks % HB:
                load(chunks - 1, 0, chunks // HB)

        @block.tensor
        def _(pe):
            pe.wait_ge(zeroed, 1)
            for g in range(GROUPS):
                ins = nc.tensor.matmul(down[g][:, :], zeros[:, 0:P], zeros[:, :], start=True, stop=False, skip_group_check=True)
            ins.then_inc(down_done, SET)

            def gate_up(k, par, g):
                n = unit(k, par, g)
                if g == 0:
                    pe.wait_ge(gu_in[par], 16 * (k + 1))
                pe.wait_ge(prod_done, n + 1)
                cols = c.xnT[:, g * GRP:(g + 1) * GRP]
                nc.tensor.matmul(gate[g % 2][:, :], w_gu[par][:, 0:P], cols, start=True, stop=True)
                nc.tensor.matmul(up[g % 2][:, :], w_gu[par][:, P:2 * P], cols, start=True, stop=True).then_inc(gu_done, 1)

            def project(k, par, g, last=False):
                n = unit(k, par, g)
                if g == 0:
                    pe.wait_ge(dn_in[par], 16 * (k + 1))
                pe.wait_ge(hidden_done, n + 3)
                nc.tensor.matmul(down[g][:, :], w_dn[par][:, :], hidden[par][:, g * GRP:(g + 1) * GRP],
                                 start=False, stop=last, skip_group_check=True).then_inc(down_done, 1)

            for g in range(GROUPS):
                gate_up(0, 0, g)
            pairs = (chunks - 1) // HB
            with pe.Fori(0, pairs) as k:
                for par in range(HB):
                    for g in range(GROUPS):
                        gate_up(k + par, 1 - par, g)
                        project(k, par, g)
            if chunks % HB == 0:
                for g in range(GROUPS):
                    gate_up(pairs, 1, g)
                    project(pairs, 0, g)
                for g in range(GROUPS):
                    project(pairs, 1, g, last=True)
            else:
                for g in range(GROUPS):
                    project(pairs, 0, g, last=True)

        def over_units(eng, step):
            with eng.Fori(0, chunks // HB) as k:
                for par in range(HB):
                    for g in range(GROUPS):
                        step(k, par, g)
            if chunks % HB:
                for g in range(GROUPS):
                    step(chunks // HB, 0, g)

        @block.scalar
        def _(act):
            def step(k, par, g):
                act.wait_ge(gu_done, unit(k, par, g) + 1)
                nc.scalar.activation(silu[g % 2][:, :], gate[g % 2][:, :], ACT.Silu).then_inc(silu_done, 1)
            over_units(act, step)
            act.wait_ge(down_done, SET + chunks * GROUPS)
            for g in range(0, GROUPS, 2):
                nc.scalar.activation(hidden[0][:, g * GRP:(g + 1) * GRP], down[g][:, :], ACT.Copy).then_inc(silu_done, 1)

        @block.vector
        def _(dve):
            nc.vector.memset(zeros[:, :], 0.0).then_inc(zeroed, 1)
            nc.vector.memset(prod[0][:, 0:1], 0.0).then_inc(prod_done, 2)
            def step(k, par, g):
                n = unit(k, par, g)
                dve.wait_ge(silu_done, n + 1)
                dve.wait_ge(hidden_done, n + 1)
                nc.vector.tensor_tensor(prod[g % 2][:, :], up[g % 2][:, :], silu[g % 2][:, :], ALU.mult).then_inc(prod_done, 1)
            over_units(dve, step)
            dve.wait_ge(down_done, SET + chunks * GROUPS)
            for g in range(1, GROUPS, 2):
                cols = slice(g * GRP, (g + 1) * GRP)
                nc.vector.tensor_tensor(c.y[:, cols], down[g][:, :], c.y[:, cols], ALU.add)
            for g in range(0, GROUPS, 2):
                cols = slice(g * GRP, (g + 1) * GRP)
                dve.wait_ge(silu_done, chunks * GROUPS + g // 2 + 1)
                nc.vector.tensor_tensor(c.y[:, cols], hidden[0][:, cols], c.y[:, cols], ALU.add)

        @block.gpsimd
        def _(pool):
            nc.gpsimd.memset(hidden[0][:, 0:1], 0.0).then_inc(hidden_done, 2)
            def step(k, par, g):
                n = unit(k, par, g)
                if g == 0:
                    pool.wait_ge(share_in[par], 32 * (k + 1))
                pool.wait_ge(prod_done, n + 3)
                pool.wait_ge(down_done, n + 1)
                cols = slice(g * GRP, (g + 1) * GRP)
                nc.gpsimd.tensor_tensor(hidden[par][:, cols], prod[g % 2][:, :], share[par][:, cols], ALU.mult).then_inc(hidden_done, 1)
            over_units(pool, step)



F32R = mybir.dt.float32r
HI, MID, LO = range(3)
Q_PARTS = (HI, HI, HI, MID, MID, LO)
K_PARTS = (HI, MID, LO, HI, MID, HI)


class Heads:

    def __init__(self, nc, tag, width, null):
        self.tag, self.width, self.null = tag, width, null
        self.small = width == 8
        self.together = 4 if self.small else 1
        self.out_rows = 32 if self.small else width + 1
        self.keys = SEQ + null
        self.part = BF16 if self.small else F32R
        self.rows = 6 * width if self.small else 3 * width
        self.moved = BF16 if self.small else F32
        if self.small:
            self.q = nc.dram_tensor(f"{tag}_q_parts", (HEADS, self.rows, BATCH, SEQ), self.moved, kind="Internal").ap()
            self.k = nc.dram_tensor(f"{tag}_k_parts", (HEADS, self.rows, BATCH, self.keys), self.moved, kind="Internal").ap()
        self.v = nc.dram_tensor(f"{tag}_v_rows", (P, HEADS, TILES, self.out_rows), F32, kind="Internal").ap()
        if not self.small:
            self.v_lo = nc.dram_tensor(f"{tag}_v_low_rows", (P, HEADS, TILES, self.out_rows), F32, kind="Internal").ap()
        self.o = nc.dram_tensor(f"{tag}_sums", (HEADS * self.out_rows, TOK), F32, kind="Internal").ap()
        self.inv = nc.dram_tensor(f"{tag}_inverse", (HEADS, TOK), F32, kind="Internal").ap()


def stage_project_small(c, h):
    nc, tag = c.nc, h.tag
    rope = h.null
    with c.scope() as s:
        names = ["wq", "wk", "wv"] + (["wq_turn", "wk_turn"] if rope else [])
        w = {n: s.sb(f"{tag}_{n}", [P, P]) for n in names}
        if rope:
            cos, sin = s.sb(f"{tag}_cos", [P, SEQ]), s.sb(f"{tag}_sin", [P, SEQ])
            turned = s.sb(f"{tag}_turned", [P, GRP])
        full = {n: s.sb(f"{tag}_{n}_full", [P, BATCH, SEQ if n == "q" else h.keys]) for n in "qk"}
        rest = {n: s.sb(f"{tag}_{n}_rest", list(full[n].shape)) for n in "qk"}
        part = {n: [s.sb(f"{tag}_{n}_part{i}", list(full[n].shape), BF16) for i in range(3)] for n in "qk"}
        v = s.sb(f"{tag}_v", [P, HEADS, TILES, h.out_rows])
        pq = [s.ps(f"{tag}_pq{i}", [P, GRP]) for i in range(2)]
        pt = [s.ps(f"{tag}_pt{i}", [P, GRP]) for i in range(2)]
        pv = [s.ps(f"{tag}_pv{i}", [P, P]) for i in range(4)]
        loaded, projected, copied = s.sem(f"{tag}_loaded"), s.sem(f"{tag}_projected"), s.sem(f"{tag}_copied")
        rotated, step_done = s.sem(f"{tag}_rotated"), s.sem(f"{tag}_step")
        v_done, v_copied, v_filled = s.sem(f"{tag}_v_done"), s.sem(f"{tag}_v_copied"), s.sem(f"{tag}_v_filled")
        hi_done, rest_done, mid_done, lo_done = (s.sem(f"{tag}_{n}") for n in ("hi", "rest", "mid", "lo"))
        stored = s.sem(f"{tag}_stored")
        block = s.block()
        per = SEQ // GRP
        order = [("q", g) for g in range(GROUPS)] + [("k", g) for g in range(GROUPS)]

        @block.sync
        def _(sp):
            for n in names:
                sp.dma_start(w[n][:, :], c.dram[f"{tag}_{n}"]).then_inc(loaded, 16)
            if rope:
                sp.dma_start(cos[:, :], c.dram["cos"]).then_inc(loaded, 16)
                sp.dma_start(sin[:, :], c.dram["sin"]).then_inc(loaded, 16)
                for b in range(BATCH):
                    with nc.allow_non_contiguous_dma(reason="the null key is a column"):
                        sp.dma_start(full["k"][:, b, SEQ:SEQ + 1], c.dram[f"{tag}_k_null"]).then_inc(loaded, 16)
            n = 0
            for i, (name, parts, rows) in enumerate((("q", Q_PARTS, h.q), ("k", K_PARTS, h.k))):
                for sem, p in ((hi_done, HI), (mid_done, MID), (lo_done, LO)):
                    sp.wait_ge(sem, i + 1)
                    for k in range(6):
                        if parts[k] == p:
                            for b in range(BATCH):
                                dst = rows[:, k * h.width:(k + 1) * h.width, b, :]
                                sp.dma_start(dst, part[name][p][:, b, :]).then_inc(stored, 16)
                                n += 16
            sp.wait_ge(v_copied, TILES)
            sp.wait_ge(v_filled, 2)
            sp.dma_start(h.v, v[:, :, :, :]).then_inc(stored, 16)
            sp.wait_ge(stored, n + 16)

        @block.gpsimd
        def _(pool):
            nc.gpsimd.memset(v[:, :, :, h.width + 1:], 0.0).then_inc(v_filled, 1)
            nc.gpsimd.memset(v[:, :, :, h.width:h.width + 1], 1.0).then_inc(v_filled, 1)

        @block.tensor
        def _(pe):
            pe.wait_ge(loaded, 16 * (len(names) + (4 if rope else 0)))
            for i, (name, g) in enumerate(order):
                if i >= 2:
                    pe.wait_ge(copied, i - 1)
                cols = c.xnT[:, g * GRP:(g + 1) * GRP]
                if rope:
                    nc.tensor.matmul(pt[i % 2][:, :], w[f"w{name}_turn"][:, :], cols, start=True, stop=True)
                nc.tensor.matmul(pq[i % 2][:, :], w[f"w{name}"][:, :], cols, start=True, stop=True).then_inc(projected, 1)
            for t in range(TILES):
                if t >= 4:
                    pe.wait_ge(v_copied, t - 3)
                nc.tensor.matmul(pv[t % 4][:, :], c.xnT[:, t * P:(t + 1) * P], w["wv"][:, :], start=True, stop=True).then_inc(v_done, 1)

        @block.vector
        def _(dve):
            count = [0]

            def link(ins):
                count[0] += 1
                ins.then_inc(step_done, 1)
                dve.wait_ge(step_done, count[0])

            if rope:
                dve.wait_ge(loaded, 16 * (len(names) + 4))
            for i, (name, g) in enumerate(order):
                dve.wait_ge(projected, i + 1)
                b, at = g // per, (g % per) * GRP
                dst = full[name][:, b, at:at + GRP]
                if rope:
                    if i:
                        dve.wait_ge(copied, i)
                    link(nc.vector.tensor_tensor(turned[:, :], pt[i % 2][:, :], sin[:, at:at + GRP], ALU.mult))
                    link(nc.vector.tensor_tensor(dst, pq[i % 2][:, :], cos[:, at:at + GRP], ALU.mult))
                    nc.vector.tensor_tensor(dst, dst, turned[:, :], ALU.add).then_inc(copied, 1)
                else:
                    nc.vector.tensor_copy(dst, pq[i % 2][:, :]).then_inc(copied, 1)
            for i, name in enumerate("qk"):
                dve.wait_ge(hi_done, i + 1)
                nc.vector.tensor_tensor(rest[name][:, :, :], full[name][:, :, :], part[name][HI][:, :, :], ALU.subtract).then_inc(rest_done, 1)
            for i, name in enumerate("qk"):
                dve.wait_ge(mid_done, i + 1)
                nc.vector.tensor_tensor(part[name][LO][:, :, :], rest[name][:, :, :], part[name][MID][:, :, :], ALU.subtract).then_inc(lo_done, 1)

        @block.scalar
        def _(act):
            for i, name in enumerate("qk"):
                act.wait_ge(copied, (i + 1) * GROUPS)
                nc.scalar.activation(part[name][HI][:, :, :], full[name][:, :, :], ACT.Copy).then_inc(hi_done, 1)
            for i, name in enumerate("qk"):
                act.wait_ge(rest_done, i + 1)
                nc.scalar.activation(part[name][MID][:, :, :], rest[name][:, :, :], ACT.Copy).then_inc(mid_done, 1)
            for t in range(TILES):
                act.wait_ge(v_done, t + 1)
                nc.scalar.activation(v[:, :, t, 0:h.width], pv[t % 4][:, :].rearrange("p (a d) -> p a d", d=h.width),
                                     ACT.Copy).then_inc(v_copied, 1)


def stage_project_v(c, h, w_v):
    nc, tag, W = c.nc, h.tag, h.width
    with c.scope() as s:
        wv = [s.sb(f"{tag}_wv{i}", [P, GRP]) for i in range(2)]
        v_hi, v_lo = (s.sb(f"{tag}_v_{n}", [P, HEADS, TILES, h.out_rows], F32R) for n in ("hi", "lo"))
        bank = [s.ps(f"{tag}_bank{i}", [P, GRP]) for i in range(4)]
        wv_in = s.sem(f"{tag}_wv_in")
        v_done, v_rounded, v_split, v_filled, v_stored = (s.sem(f"{tag}_{n}") for n in ("v_done", "v_rounded", "v_split", "v_filled", "v_stored"))
        block = s.block()
        half = HEADS // 2

        def place(v, n):
            t, i = divmod(n, 2)
            return v[:, i * half:(i + 1) * half, t, 0:W]

        def heads(ap):
            return ap.rearrange("p (a d) -> p a d", d=W)

        @block.sync
        def _(sp):
            for i in range(2):
                sp.dma_start(wv[i][:, :], w_v[:, i * GRP:(i + 1) * GRP]).then_inc(wv_in, 16)
            sp.wait_ge(v_filled, 2)
            for b in range(BATCH):
                tiles = slice(b * TILES // BATCH, (b + 1) * TILES // BATCH)
                sp.wait_ge(v_split, 2 * tiles.stop)
                sp.dma_start(h.v[:, :, tiles, :], v_hi[:, :, tiles, :].bitcast(F32)).then_inc(v_stored, 16)
                sp.dma_start(h.v_lo[:, :, tiles, :], v_lo[:, :, tiles, :].bitcast(F32)).then_inc(v_stored, 16)
            sp.wait_ge(v_stored, 32 * BATCH)

        @block.tensor
        def _(pe):
            pe.wait_ge(wv_in, 32)
            for n in range(2 * TILES):
                t, i = divmod(n, 2)
                if n >= 4:
                    pe.wait_ge(v_split, n - 3)
                nc.tensor.matmul(bank[n % 4][:, :], c.xnT[:, t * P:(t + 1) * P], wv[i][:, :], start=True, stop=True).then_inc(v_done, 1)

        @block.scalar
        def _(act):
            for n in range(2 * TILES):
                act.wait_ge(v_done, n + 1)
                nc.scalar.activation(place(v_hi, n), heads(bank[n % 4][:, :]), ACT.Copy).then_inc(v_rounded, 1)

        @block.vector
        def _(dve):
            for n in range(2 * TILES):
                dve.wait_ge(v_rounded, n + 1)
                nc.vector.tensor_tensor(place(v_lo, n), heads(bank[n % 4][:, :]), place(v_hi, n).bitcast(F32), ALU.subtract).then_inc(v_split, 1)

        @block.gpsimd
        def _(pool):
            nc.gpsimd.memset(v_hi[:, :, :, W:W + 1].bitcast(F32), 1.0).then_inc(v_filled, 1)
            nc.gpsimd.memset(v_lo[:, :, :, W:W + 1].bitcast(F32), 0.0).then_inc(v_filled, 1)



def stage_attend(c, h, scale, w_qk=None):
    nc, tag, G, W = c.nc, h.tag, h.together, h.width
    units = HEADS // G * BATCH
    KT = SEQ // P
    HT = GRP // P
    NULL = KT
    steps = []
    for half in range(2):
        steps += [(half, NULL)] * h.null + [(half, t) for t in range((half + 1) * HT)]
    NS = len(steps)
    H0 = sum(1 for half, _ in steps if half == 0)
    slots = [(st, g) for st, (_, t) in enumerate(steps) for g in range(1 if t == NULL else G)]
    NSLOT = len(slots)
    slot_end = [max(n for n, (s_, _) in enumerate(slots) if s_ == st) + 1 for st in range(NS)]
    trials = [] if h.small else [("project", x, part) for part in range(2) for x in "qk"]
    NPR = len(trials)
    for half in range(2):
        trials += [("max", g, t, part) for g in range(G) for t in range(half * HT, (half + 1) * HT) for part in range(half + 1)]
        trials += [("null", half)] * h.null + [("turn", half)]
    NT_ALL = len(trials)
    turn_at = [trials.index(("turn", half)) for half in range(2)]
    RING = 3
    LAG, E_RING = (1, 3) if h.small else (3, 6)
    if h.small:
        terms, max_row, max_term, lead = [97], 96, 0, 96
    else:
        terms, max_row, max_term, lead = [P, 96], W, 1, P
    NT = len(terms)
    PADK = 32 * h.null
    with c.scope() as s:
        w = None if h.small else s.sb(f"{tag}_w", [P, 4 * W])
        q = [s.sb(f"{tag}_q{i}", [P, NT, 2, G, GRP], h.part) for i in range(2)]
        k = [s.sb(f"{tag}_k{i}", [P, NT, G, SEQ + PADK], h.part) for i in range(2)]
        v = [s.sb(f"{tag}_vv{i}", [P, G, KT, h.out_rows], F32 if h.small else F32R) for i in range(2)]
        v_null = [s.sb(f"{tag}_vn{i}", [P, G, h.out_rows]) for i in range(2)] if h.null else None
        e = [s.sb(f"{tag}_e{i}", [P, G, GRP]) for i in range(E_RING)]
        if not h.small:
            v_lo = [s.sb(f"{tag}_vlo{i}", [P, G, KT, h.out_rows], F32R) for i in range(2)]
            e_hi, e_lo = ([s.sb(f"{tag}_e_{n}{i}", [P, GRP], F32R) for i in range(E_RING)] for n in ("hi", "lo"))
        neg_max = [s.sb(f"{tag}_neg_max{i}", [P, G * HT]) for i in range(2)]
        neg_max2 = s.sb(f"{tag}_neg_max2", [P, G * HT])
        max_rows = [s.sb(f"{tag}_max_rows{i}", [G * HT, P], h.part) for i in range(2)]
        out_sb = s.sb(f"{tag}_out", [P, 2, GRP])
        mark = s.sb(f"{tag}_mark", [1, 8])
        above = s.sb(f"{tag}_above", [P, P])
        below = s.sb(f"{tag}_below", [P, P])
        above_b, below_b, ident_b = (s.sb(f"{tag}_{n}", [P, P], BF16) for n in ("above_b", "below_b", "ident_b"))
        ps = [s.ps(f"{tag}_ps{i}", [P, GRP]) for i in range(RING)]
        pm = [s.ps(f"{tag}_pm{i}", [P, GRP]) for i in range(RING)]
        po = [s.ps(f"{tag}_po{i}", [P, GRP]) for i in range(2)]
        OUT = slice(0, P if h.small else W + 1)
        consts_in, filled, masks_ready = s.sem(f"{tag}_consts"), [s.sem(f"{tag}_filled{i}") for i in range(2)], s.sem(f"{tag}_masks")
        zero = [s.sb(f"{tag}_zero{i}", [P, 1]) for i in range(2)]
        FILLS = 4 + 2 * h.null
        qk_in = [[s.sem(f"{tag}_qk_in{b}{g}") for g in range(G)] for b in range(2)]
        v_in = [s.sem(f"{tag}_v_in{b}") for b in range(2)]
        w_in, hi_done, k_doubled, e_rounded, e_split = (s.sem(f"{tag}_{n}") for n in (
            "w_in", "hi_done", "k_doubled", "e_rounded", "e_split"))
        scored, exp_done, weighed = s.sem(f"{tag}_scored"), s.sem(f"{tag}_exp"), s.sem(f"{tag}_weighed")
        trial, trial_read = s.sem(f"{tag}_trial"), s.sem(f"{tag}_trial_read")
        max_ready, max_in = s.sem(f"{tag}_max_ready"), [s.sem(f"{tag}_max_in{i}") for i in range(2)]
        out_copied = [s.sem(f"{tag}_out_copied{i}") for i in range(2)]
        out_stored = [s.sem(f"{tag}_out_stored{i}") for i in range(2)]
        block = s.block()
        last = units // 2 - 1
        OVERHEAD = 64

        def freed(u, n, total, ring):
            before = n - ring if n >= ring else max(m for m in range(total) if m % ring == n) - total
            return u * total + before + 1 + ring

        def slot_columns(n):
            half, t = steps[slots[n][0]]
            return GRP if t == NULL else (half + 1) * GRP - max(half * GRP, t * P)

        def trial_columns(n):
            kind, *of = trials[n]
            return {"project": GRP, "null": P, "turn": P}.get(kind) or min((of[2] + 1) * GRP, (of[1] + 1) * P) - of[2] * GRP

        def trials_by(n):
            start, end = (0.22, 1.15) if h.small else (0.0, 0.88)
            passed = n // NSLOT + sum(slot_columns(m) + OVERHEAD for m in range(n % NSLOT + 1)) / sum(slot_columns(m) + OVERHEAD for m in range(NSLOT))
            work = [trial_columns(m) + OVERHEAD for m in range(NT_ALL)]
            due = (passed - start) / (end - start) * sum(work)
            return sum(1 for m in range(NT_ALL) if sum(work[:m]) < due)

        assert trials_by(NSLOT - G) > turn_at[0] and (h.small or trials_by(NSLOT - 1) == NT_ALL) and trials_by(NSLOT + slot_end[H0 - 1] - 1) == NT_ALL

        def slots_with_trials(i, b, before, after, own_from):
            own, done = own_from, 0
            for n in range(NSLOT):
                follow = [(i, b, j) for j in range(own, max(own, trials_by(NSLOT + n)))]
                own = max(own, trials_by(NSLOT + n))
                if after:
                    follow += [(*after, j) for j in range(done, trials_by(n))]
                    done = trials_by(n)
                yield n, follow

        def over_units(eng, unit):
            left = trials_by(NSLOT - 1)
            unit(0, 0, None, (0, 1), NT_ALL)
            with eng.Fori(0, last) as i:
                unit(i, 1, (i, 0), (i + 1, 0), left)
                unit(i + 1, 0, (i, 1), (i + 1, 1), left)
            unit(last, 1, (last, 0), None, left)

        @block.sync
        def _(sp):
            sp.dma_start(above[:, :], c.dram["mask_above"]).then_inc(consts_in, 16)
            sp.dma_start(below[:, :], c.dram["mask_below"]).then_inc(consts_in, 16)

            def load_qk(i, b):
                for g in range(G):
                    head = bass.ds(i * G + g, 1)
                    sp.dma_start(q[b][0:h.rows, 0, :, g, :], h.q[head, :, b, :].rearrange("g r (x n) -> (g r) x n", x=2)).then_inc(qk_in[b][g], 16)
                    sp.dma_start(k[b][0:h.rows, 0, g, 0:h.keys], h.k[head, :, b, :].rearrange("g r n -> (g r) n")).then_inc(qk_in[b][g], 16)

            def load_w(i):
                sp.dma_start(w[:, :], w_qk[bass.ds(i, 1), :, :].rearrange("a d n -> (a d) n")).then_inc(w_in, 16)

            def load_v(i, b):
                for dst, src in ((v, h.v),) if h.small else ((v, h.v), (v_lo, h.v_lo)):
                    dst = dst[b][:, :, :, :] if h.small else dst[b][:, :, :, :].bitcast(F32)
                    sp.dma_start(dst, src[:, bass.ds(i * G, G), b * KT:(b + 1) * KT, :]).then_inc(v_in[b], 16)
                if h.null:
                    for g in range(G):
                        sp.dma_start(v_null[b][32 * g:32 * g + 1, g, :],
                                     c.dram[f"{tag}_v_null"][:, bass.ds(i * G + g, 1), :].rearrange("o g r -> o (g r)")).then_inc(v_in[b], 16)

            def put_max(i, b, half):
                sp.wait_ge(trial_read, RING + NT_ALL * (2 * i + b) + turn_at[half] + 1)
                dst = q[b][max_row:max_row + 1, max_term, half, :, :].rearrange("o g n -> o (g n)")
                sp.dma_start(dst.bitcast(h.moved), max_rows[half][:, :].bitcast(h.moved)).then_inc(max_in[half], 16)

            def store(i, b, half):
                sp.wait_ge(out_copied[half], 2 * i + b + 2)
                at = b * SEQ + half * GRP
                sp.dma_start(h.o[bass.ds((i * G) * h.out_rows, OUT.stop), at:at + GRP], out_sb[OUT, half, :]).then_inc(out_stored[half], 16)

            def unit(i, b, is_last):
                u = 2 * i + b
                if h.small:
                    put_max(i, b, 1)
                if not h.small and b == 0 and not is_last:
                    sp.wait_ge(trial, NT_ALL * (u + 1) + NPR)
                    load_w(i + 1)
                store(i, b, 0)
                if not (is_last and b == 1):
                    for half in range(1 if h.small else 2):
                        put_max(*((i + 1, 0) if b else (i, 1)), half)
                if not is_last:
                    if h.small:
                        sp.wait_ge(scored, NSLOT * (u + 1))
                        load_qk(i + 1, b)
                    sp.wait_ge(weighed, E_RING + NS * (u + 1))
                    load_v(i + 1, b)
                store(i, b, 1)

            if not h.small:
                load_w(0)
            for b in range(2):
                sp.wait_ge(filled[b], FILLS)
                if h.small:
                    load_qk(0, b)
                load_v(0, b)
            for half in range(1 if h.small else 2):
                put_max(0, 0, half)
            with sp.Fori(0, last) as i:
                for b in range(2):
                    unit(i, b, False)
            for b in range(2):
                unit(last, b, True)
            for half in range(2):
                sp.wait_ge(out_stored[half], 16 * (units + 1))

        QK_LOADS, V_LOADS = 32, 16 * (1 + G * h.null if h.small else 2)

        def fill(eng, memset, b):
            def full(ap):
                return ap.bitcast(F32)

            if h.small:
                fills = [(full(q[b][:, 0, :, :, :]), 0.0), (full(k[b][0:96, 0, :, :]), 0.0), (k[b][96:97, 0, :, 0:h.keys], 1.0)]
            else:
                fills = [(full(q[b][W:96, 1, :, :, :]), 0.0), (full(k[b][W:96, 1, :, :]), 0.0), (full(k[b][W:W + 1, 1, :, :]), 1.0)]
            if h.null:
                fills += [(k[b][96:97, 0, :, h.keys:], 0.0), (v_null[b][:, :, :], 0.0)]
            fills += [(zero[b][:, :], 0.0)]
            for n, (rows, value) in enumerate(fills):
                memset(rows, value).then_inc(filled[b], 1)
                eng.wait_ge(filled[b], n + 1)

        @block.gpsimd
        def _(pool):
            fill(pool, nc.gpsimd.memset, 1)

            def double_k(i, b):
                pool.wait_ge(hi_done, (2 * i + b + 1) * NPR)
                hi = k[b][0:W, 0, 0, :].bitcast(F32)
                nc.gpsimd.tensor_tensor(k[b][0:W, 1, 0, :], hi, zero[b][0:W, :].to_broadcast([W, SEQ]), ALU.add).then_inc(k_doubled, 1)

            def split_e(i, b, n):
                half, t = steps[n]
                lo = max(0, t * P - half * GRP)
                pool.wait_ge(e_rounded, (2 * i + b) * NSLOT + n + 1)
                nc.gpsimd.tensor_tensor(e_lo[n % E_RING][:, lo:], e[n % E_RING][:, 0, lo:], e_hi[n % E_RING][:, lo:].bitcast(F32), ALU.subtract).then_inc(e_split, 1)

            def unit(i, b, before, after, own_from):
                for n in range(NSLOT):
                    if n:
                        split_e(i, b, n - 1)
                    elif before:
                        split_e(*before, NSLOT - 1)
                    if after and trials_by(n) >= NPR > (trials_by(n - 1) if n else 0):
                        double_k(*after)

            if not h.small:
                pool.wait_ge(filled[0], FILLS)
                double_k(0, 0)
                over_units(pool, unit)
                split_e(last, 1, NSLOT - 1)

        @block.tensor
        def _(pe):
            def try_max(i, b, n):
                u = 2 * i + b
                bank = pm[n % RING]
                kind, *of = trials[n]
                if h.small and kind == "max" and of[1:] == [0, 0]:
                    pe.wait_ge(qk_in[b][of[0]], QK_LOADS * (i + 1))
                if n == 0 and NPR and b == 0:
                    pe.wait_ge(w_in, 16 * (i + 1))
                if n == NPR > 0:
                    pe.wait_ge(trial_read, RING + u * NT_ALL + NPR)
                pe.wait_ge(trial_read, freed(u, n, NT_ALL, RING))
                if kind == "project":
                    x, part = of
                    at = 0 if x == "q" else 2 * W
                    first = b * SEQ + part * GRP
                    ins = nc.tensor.matmul(bank[:, :], w[:, at:at + 2 * W], c.xnT[:, first:first + GRP], start=True, stop=True)
                elif kind == "max":
                    g, t, part = of
                    lhs = q[b][0:lead, 0, t // HT, g, t % HT * P:(t % HT + 1) * P]
                    lo, hi = part * GRP, min((part + 1) * GRP, (t + 1) * P)
                    diag = hi == (t + 1) * P
                    ins = nc.tensor.matmul(bank[:, 0:hi - lo], lhs, k[b][0:lead, 0, g, lo:hi], start=True, stop=not diag)
                    if diag:
                        ins = nc.tensor.matmul(bank[:, t * P - lo:hi - lo], ident_b[:, :], above_b[:, :], start=False, stop=True)
                elif kind == "null":
                    for at in range(G * HT):
                        g, t = divmod(at, HT)
                        ins = nc.tensor.matmul(bank[:, at:at + 1], q[b][0:lead, 0, of[0], g, t * P:(t + 1) * P],
                                               k[b][0:lead, 0, g, SEQ:SEQ + 1], start=True, stop=True)
                else:
                    half, = of
                    if half:
                        pe.wait_ge(max_ready, u + 1)
                    else:
                        pe.wait_ge(trial_read, RING + u * NT_ALL + n)
                    ins = nc.tensor.transpose(bank[0:G * HT, 0:P], neg_max[half][:, :], c.ident[:, :])
                ins.then_inc(trial, 1)

            def score(i, b, n):
                u = 2 * i + b
                st, g = slots[n]
                half, t = steps[st]
                bank = ps[n % RING]
                if g == 0 and st in (0, H0):
                    pe.wait_ge(max_in[st == H0], 16 * (u + 1))
                if n == 0:
                    if not h.small:
                        pe.wait_ge(k_doubled, u + 1)
                pe.wait_ge(exp_done, freed(u, n, NSLOT, RING))
                first = half * GRP
                if t == NULL:
                    for a in range(G):
                        ins = nc.tensor.matmul(bank[32 * a:32 * a + 32, :], k[b][0:terms[0], 0, a, SEQ:SEQ + PADK],
                                               q[b][0:terms[0], 0, half, a, :], start=True, stop=True)
                else:
                    lo = max(first, t * P)
                    diag = lo == t * P
                    for m in range(NT):
                        ins = nc.tensor.matmul(bank[:, lo - first:], k[b][0:terms[m], m, g, t * P:(t + 1) * P],
                                               q[b][0:terms[m], m, half, g, lo - first:], start=m == 0, stop=m == NT - 1 and not diag)
                    if diag:
                        ins = nc.tensor.matmul(bank[:, lo - first:lo - first + P], ident_b[:, :], below_b[:, :], start=False, stop=True)
                ins.then_inc(scored, 1)

            def weigh(i, b, st):
                u = 2 * i + b
                half, t = steps[st]
                if st == 0:
                    pe.wait_ge(v_in[b], V_LOADS * (i + 1))
                if st in (0, H0):
                    pe.wait_ge(out_copied[half], u + 1)
                if not h.small:
                    pe.wait_ge(e_split, u * NSLOT + st + 1)
                elif st + LAG >= NS or slot_end[st + LAG] - RING < slot_end[st]:
                    pe.wait_ge(exp_done, RING + u * NSLOT + slot_end[st])
                lo = 0 if t == NULL else max(0, t * P - half * GRP)
                if not h.small:
                    for lhs, rhs in ((v, e_hi), (v_lo, e_hi), (v, e_lo)):
                        ins = nc.tensor.matmul(po[half][0:h.out_rows, lo:], lhs[b][:, 0, t, :], rhs[st % E_RING][:, lo:],
                                               start=st in (0, H0) and lhs is v and rhs is e_hi,
                                               stop=st in (H0 - 1, NS - 1) and rhs is e_lo, skip_group_check=True)
                    ins.then_inc(weighed, 1)
                    return
                for g in range(G):
                    lhs = v_null[b][:, g, :] if t == NULL else v[b][:, g, t, :]
                    ins = nc.tensor.matmul(po[half][g * h.out_rows:(g + 1) * h.out_rows, lo:], lhs,
                                           e[st % E_RING][:, 0 if t == NULL else g, lo:], start=st in (0, H0),
                                           stop=st in (H0 - 1, NS - 1), skip_group_check=True)
                ins.then_inc(weighed, 1)

            def unit(i, b, before, after, own_from):
                for n, follow in slots_with_trials(i, b, before, after, own_from):
                    st = slots[n][0]
                    score(i, b, n)
                    for item in follow:
                        try_max(*item)
                    if n + 1 == slot_end[st]:
                        if st >= LAG:
                            weigh(i, b, st - LAG)
                        elif before:
                            weigh(*before, NS - LAG + st)

            for b in range(2):
                pe.wait_ge(filled[b], FILLS)
            pe.wait_ge(masks_ready, 3)
            for n in range(NT_ALL):
                try_max(0, 0, n)
            over_units(pe, unit)
            for st in range(NS - LAG, NS):
                weigh(last, 1, st)

        @block.scalar
        def _(act):
            for n, (sem, free) in enumerate(((exp_done, RING), (weighed, E_RING), (trial_read, RING), (out_copied[0], 1),
                                             (out_stored[0], 16), (out_stored[1], 16))):
                nc.scalar.activation(mark[:, n:n + 1], c.ident[0:1, 0:1], ACT.Copy).then_inc(sem, free)

            def split(i, b, n):
                _, x, part = trials[n]
                act.wait_ge(trial, (2 * i + b) * NT_ALL + n + 1)
                dst = q[b][:, 0, part, 0, :] if x == "q" else k[b][:, 0, 0, part * GRP:(part + 1) * GRP]
                nc.scalar.activation(dst, pm[n % RING][:, :], ACT.Copy).then_inc(hi_done, 1)

            def copy_out(i, b, half):
                u = 2 * i + b
                act.wait_ge(weighed, E_RING + u * NS + (NS if half else H0))
                act.wait_ge(out_stored[half], 16 * (u + 1))
                nc.scalar.activation(out_sb[OUT, half, :], po[half][OUT, :], ACT.Copy).then_inc(out_copied[half], 1)

            def round_e(i, b, n):
                half, t = steps[n]
                lo = max(0, t * P - half * GRP)
                act.wait_ge(exp_done, RING + (2 * i + b) * NSLOT + n + 1)
                nc.scalar.activation(e_hi[n % E_RING][:, lo:], e[n % E_RING][:, 0, lo:], ACT.Copy).then_inc(e_rounded, 1)

            def unit(i, b, before, after, own_from):
                u = 2 * i + b
                for n, follow in slots_with_trials(i, b, before, after, own_from):
                    st, g = slots[n]
                    half, t = steps[st]
                    if n == 0 or slots[n - 1][0] != st:
                        act.wait_ge(weighed, freed(u, st, NS, E_RING))
                    act.wait_ge(scored, u * NSLOT + n + 1)
                    lo = 0 if t == NULL else max(0, t * P - half * GRP)
                    nc.scalar.activation(e[st % E_RING][:, g, lo:], ps[n % RING][:, lo:], ACT.Exp, scale=scale).then_inc(exp_done, 1)
                    if not h.small and n:
                        round_e(i, b, n - 1)
                    elif not h.small and before:
                        round_e(*before, NSLOT - 1)
                    for item in follow:
                        if item[2] < NPR:
                            split(*item)
                    if n + 1 == slot_end[H0 + LAG]:
                        copy_out(i, b, 0)
                    if before and n + 1 == slot_end[LAG]:
                        copy_out(*before, 1)

            for n in range(NPR):
                split(0, 0, n)
            over_units(act, unit)
            if not h.small:
                round_e(last, 1, NSLOT - 1)
            copy_out(last, 1, 1)

        @block.vector
        def _(dve):
            fill(dve, nc.vector.memset, 0)
            dve.wait_ge(consts_in, 32)
            nc.vector.tensor_copy(above_b[:, :], above[:, :]).then_inc(masks_ready, 1)
            nc.vector.tensor_copy(below_b[:, :], below[:, :]).then_inc(masks_ready, 1)
            nc.vector.tensor_copy(ident_b[:, :], c.ident[:, :]).then_inc(masks_ready, 1)
            nc.vector.memset(mark[:, 6:7], 0.0).then_inc(out_copied[1], 1)

            def read_trial(i, b, n):
                u = 2 * i + b
                kind, *of = trials[n]
                bank = pm[n % RING]
                if kind == "project":
                    x, part = of
                    cols = slice(part * GRP, (part + 1) * GRP)
                    dve.wait_ge(hi_done, u * NPR + n + 1)
                    if x == "q":
                        nc.vector.tensor_tensor(q[b][0:W, 1, part, 0, :], bank[0:W, :], q[b][0:W, 0, part, 0, :].bitcast(F32), ALU.subtract).then_inc(trial_read, 1)
                    else:
                        nc.vector.tensor_tensor(k[b][W:P, 0, 0, cols], bank[W:P, :], k[b][W:P, 0, 0, cols].bitcast(F32), ALU.subtract).then_inc(trial_read, 1)
                elif kind == "max":
                    g, t, part = of
                    hi = min((part + 1) * GRP, (t + 1) * P) - part * GRP
                    at = g * HT + t % HT
                    dst = (neg_max2 if part else neg_max[t // HT])[:, at:at + 1]
                    dve.wait_ge(trial, u * NT_ALL + n + 1)
                    nc.vector.tensor_reduce(out=dst, in_=bank[:, 0:hi], op=ALU.max, axis=AX.X, negate=True).then_inc(trial_read, 1)
                elif kind == "null":
                    most = neg_max[of[0]]
                    dve.wait_ge(trial, u * NT_ALL + n + 1)
                    dve.wait_ge(trial_read, RING + u * NT_ALL + n)
                    nc.vector.scalar_tensor_tensor(out=most[:, :], in0=bank[:, 0:G * HT], scalar=-1.0, in1=most[:, :],
                                                   op0=ALU.mult, op1=ALU.min).then_inc(trial_read, 1)
                else:
                    half, = of
                    if half:
                        dve.wait_ge(trial_read, RING + u * NT_ALL + n)
                        nc.vector.tensor_tensor(neg_max[1][:, :], neg_max[1][:, :], neg_max2[:, :], ALU.min).then_inc(max_ready, 1)
                    dve.wait_ge(trial, u * NT_ALL + n + 1)
                    if not (isinstance(u, int) and u == 0):
                        dve.wait_ge(max_in[half], 16 * u)
                    nc.vector.tensor_copy(max_rows[half][:, :], bank[0:G * HT, 0:P]).then_inc(trial_read, 1)

            def unit(i, b, before, after, own_from):
                for n, follow in slots_with_trials(i, b, before, after, own_from):
                    for item in follow:
                        read_trial(*item)

            for n in range(NT_ALL):
                read_trial(0, 0, n)
            over_units(dve, unit)


def stage_attention_out(c, h, w_out):
    nc, tag = c.nc, h.tag
    chunks = HEADS * h.width // P
    per = HEADS // chunks
    with c.scope() as s:
        den = s.sb(f"{tag}_den", [P, HEADS * TOK // P])
        w = s.sb(f"{tag}_wo", [P, chunks, P])
        num = [s.sb(f"{tag}_num{i}", [P, TOK]) for i in range(chunks)]
        ring = min(chunks, 4)
        inv = [s.sb(f"{tag}_inv{i}", [P, TOK]) for i in range(ring)]
        po = [s.ps(f"{tag}_pout{g}", [P, GRP]) for g in range(GROUPS)]
        den_in, den_done, den_stored = s.sem(f"{tag}_den_in"), s.sem(f"{tag}_den_done"), s.sem(f"{tag}_den_st")
        w_in, num_in = s.sem(f"{tag}_wo_in"), [s.sem(f"{tag}_num_in{i}") for i in range(chunks)]
        inv_in, divided, used = [s.sem(f"{tag}_inv_in{i}") for i in range(ring)], s.sem(f"{tag}_divided"), s.sem(f"{tag}_used")
        block = s.block()
        parts = P // HEADS
        width = TOK // parts

        @block.sync
        def _(sp):
            src = dram_view(h.o, h.width * TOK, [[h.out_rows * TOK, HEADS], [width, parts], [1, width]])
            sp.dma_start(den[:, :], src).then_inc(den_in, 16)
            sp.dma_start(w[:, :, :], w_out.rearrange("(k p) d -> p k d", p=P)).then_inc(w_in, 16)
            for k in range(chunks):
                src = dram_view(h.o, k * per * h.out_rows * TOK, [[h.out_rows * TOK, per], [TOK, h.width], [1, TOK]])
                sp.dma_start(num[k][:, :], src).then_inc(num_in[k], 16)
                if k == min(1, chunks - 1):
                    sp.wait_ge(den_done, 1)
                    sp.dma_start(h.inv.rearrange("a (k n) -> a k n", k=parts), den[:, :]).then_inc(den_stored, 16)
            sp.wait_ge(den_stored, 16)
            for k in range(chunks):
                if k >= ring:
                    sp.wait_ge(divided, k - ring + 1)
                src = dram_view(h.inv, k * per * TOK, [[TOK, per], [0, h.width], [1, TOK]])
                sp.dma_start(inv[k % ring][:, :], src).then_inc(inv_in[k % ring], 16)

        @block.vector
        def _(dve):
            dve.wait_ge(den_in, 16)
            nc.vector.reciprocal(den[:, :], den[:, :]).then_inc(den_done, 1)
            for k in range(chunks):
                dve.wait_ge(num_in[k], 16)
                dve.wait_ge(inv_in[k % ring], 16 * (k // ring + 1))
                nc.vector.tensor_tensor(num[k][:, :], num[k][:, :], inv[k % ring][:, :], ALU.mult).then_inc(divided, 1)
            dve.wait_ge(used, chunks)
            for g in range(1, GROUPS, 2):
                nc.vector.tensor_copy(c.y[:, g * GRP:(g + 1) * GRP], po[g][:, :])

        @block.scalar
        def _(act):
            act.wait_ge(used, chunks)
            for g in range(0, GROUPS, 2):
                nc.scalar.activation(c.y[:, g * GRP:(g + 1) * GRP], po[g][:, :], ACT.Copy)

        @block.tensor
        def _(pe):
            pe.wait_ge(w_in, 16)
            for k in range(chunks):
                pe.wait_ge(divided, k + 1)
                for g in range(GROUPS):
                    ins = nc.tensor.matmul(po[g][:, :], w[:, k, :], num[k][:, g * GRP:(g + 1) * GRP],
                                           start=k == 0, stop=k == chunks - 1)
                ins.then_inc(used, 1)



BLOCK = 16
HIDDEN = 352


def fp4_round(nc, link, src, sign, wait_sign, mag, level, above, stat, dst):
    v = nc.vector
    largest, inverse, half = (stat[:, i, :] for i in range(3))
    link(v.scalar_tensor_tensor(out=mag, in0=src, scalar=-1.0, in1=src, op0=ALU.mult, op1=ALU.max))
    link(v.tensor_reduce(out=largest, in_=mag, op=ALU.max, axis=AX.X))
    link(v.tensor_scalar(largest, largest, 1.0 / 6.0, 1e-12, ALU.mult, ALU.max))
    link(v.reciprocal(inverse, largest))
    link(v.tensor_scalar(half, largest, 0.5, None, ALU.mult))
    link(v.tensor_tensor(mag, mag, over_last(inverse, BLOCK), ALU.mult))
    link(v.tensor_scalar(level, mag, 5.0, 2.0, ALU.is_gt, ALU.mult))
    for step in (3.5, 2.5):
        link(v.scalar_tensor_tensor(out=level, in0=mag, scalar=step, in1=level, op0=ALU.is_gt, op1=ALU.add))
    link(v.tensor_scalar(above, mag, 1.75, None, ALU.is_gt))
    link(v.scalar_tensor_tensor(out=level, in0=level, scalar=2.0, in1=above, op0=ALU.mult, op1=ALU.add))
    for step in (1.25, 0.75, 0.25):
        link(v.scalar_tensor_tensor(out=level, in0=mag, scalar=step, in1=level, op0=ALU.is_gt, op1=ALU.add))
    link(v.tensor_tensor(level, level, over_last(half, BLOCK), ALU.mult))
    wait_sign()
    return v.tensor_tensor(dst, level, sign, ALU.mult)


def stage_fp4_ffn(c, w_gate_up, w_down):
    nc = c.nc
    with c.scope() as s:
        BT = GRP // P
        rows = 3 * P
        xq = s.sb("f4_xq", [P, TILES, P])
        xqT = s.sb("f4_xqT", [P, TOK])
        w_rows = s.sb("f4_w_rows", [P, 6, P])
        wd_rows = s.sb("f4_wd_rows", [P, HIDDEN])
        wT = s.sb("f4_wT", [P, 2, rows])
        wdT = s.sb("f4_wdT", [P, 3, P])
        hid = [s.sb(f"f4_hid{i}", [P, BT, HIDDEN]) for i in range(2)]
        hq = [s.sb(f"f4_hq{i}", [P, BT, HIDDEN]) for i in range(2)]
        hqT = s.sb("f4_hqT", [P, 3, GRP])
        silu = [s.sb(f"f4_silu{i}", [P, HIDDEN]) for i in range(2)]
        size = TILES * P
        sign, mag, level, above = (s.sb(f"f4_{n}", [P, size]) for n in ("sign", "mag", "level", "above"))
        stat = s.sb("f4_stat", [P, 3, size // BLOCK])
        gate = [s.ps(f"f4_pg{i}", [P, HIDDEN]) for i in range(2)]
        up = [s.ps(f"f4_pu{i}", [P, HIDDEN]) for i in range(2)]
        pt = [s.ps(f"f4_pt{i}", [P, GRP]) for i in range(3)]
        po = s.ps("f4_po", [P, GRP])
        loaded, step_done, signed = s.sem("f4_loaded"), s.sem("f4_step"), s.sem("f4_signed")
        rounded, turned, placed = s.sem("f4_rounded"), s.sem("f4_turned"), s.sem("f4_placed")
        gu_done, silu_done, prod_done = s.sem("f4_gu_done"), s.sem("f4_silu_done"), s.sem("f4_prod_done")
        h_turned, h_placed, down_done, added = s.sem("f4_h_turned"), s.sem("f4_h_placed"), s.sem("f4_down"), s.sem("f4_added")
        block = s.block()
        chunk = [(0, P), (P, P), (2 * P, HIDDEN - 2 * P)]

        def blocks(ap):
            return ap.rearrange("p (k m) -> p k m", m=BLOCK)

        jobs = [(c.xn[:, :, :].rearrange("p t d -> p (t d)"), xq[:, :, :].rearrange("p t d -> p (t d)")),
                (w_rows[:, :, :].rearrange("p t d -> p (t d)"), w_rows[:, :, :].rearrange("p t d -> p (t d)")),
                (wd_rows[:, :], wd_rows[:, :])]
        jobs += [(hid[g % 2][:, :, :].rearrange("p t d -> p (t d)"), hq[g % 2][:, :, :].rearrange("p t d -> p (t d)"))
                 for g in range(GROUPS)]

        @block.sync
        def _(sp):
            sp.dma_start(w_rows[:, :, :], w_gate_up.rearrange("(t p) d -> p t d", p=P)).then_inc(loaded, 16)
            sp.dma_start(wd_rows[:, :], w_down).then_inc(loaded, 16)

        @block.vector
        def _(dve):
            count = [0]

            def link(ins):
                count[0] += 1
                ins.then_inc(step_done, 1)
                dve.wait_ge(step_done, count[0])

            def job(j):
                src, dst = jobs[j]
                n = src.shape[1]
                fp4_round(nc, link, blocks(src), blocks(sign[:, 0:n]), lambda: dve.wait_ge(signed, j + 1),
                          blocks(mag[:, 0:n]), blocks(level[:, 0:n]), blocks(above[:, 0:n]),
                          stat[:, :, 0:n // BLOCK], blocks(dst)).then_inc(rounded, 1)

            def gated(g):
                if g >= 2:
                    dve.wait_ge(rounded, 3 + g - 1)
                for t in range(g * BT, (g + 1) * BT):
                    dve.wait_ge(silu_done, t + 1)
                    nc.vector.tensor_tensor(hid[g % 2][:, t % BT, :], up[t % 2][:, :], silu[t % 2][:, :], ALU.mult).then_inc(prod_done, 1)

            job(0)
            dve.wait_ge(loaded, 32)
            job(1)
            job(2)
            gated(0)
            for g in range(GROUPS):
                dve.wait_ge(prod_done, (g + 1) * BT)
                if g >= 2:
                    dve.wait_ge(h_turned, 3 * (g - 1))
                job(3 + g)
                if g + 1 < GROUPS:
                    gated(g + 1)
                dve.wait_ge(down_done, g + 1)
                cols = slice(g * GRP, (g + 1) * GRP)
                nc.vector.tensor_tensor(c.y[:, cols], po[:, :], c.y[:, cols], ALU.add).then_inc(added, 1)

        @block.scalar
        def _(act):
            def signs(j):
                if j >= 1:
                    act.wait_ge(rounded, j)
                src, _ = jobs[j]
                if j >= 3:
                    act.wait_ge(prod_done, (j - 2) * BT)
                nc.scalar.activation(sign[:, 0:src.shape[1]], src, ACT.Sign).then_inc(signed, 1)

            signs(0)
            act.wait_ge(loaded, 32)
            signs(1)
            signs(2)
            for n in range(GROUPS):
                act.wait_ge(turned, n + 1)
                nc.scalar.activation(xqT[:, n * GRP:(n + 1) * GRP], (pt + [po])[n][:, :], ACT.Copy).then_inc(placed, 1)
            for i in range(2):
                act.wait_ge(turned, GROUPS + i + 1)
                nc.scalar.activation(wT[:, i, :], pt[i][:, 0:rows], ACT.Copy).then_inc(placed, 1)
            act.wait_ge(turned, GROUPS + 3)
            nc.scalar.activation(wdT[:, 0:2, :], pt[2][:, 0:2 * P].rearrange("p (a n) -> p a n", n=P), ACT.Copy).then_inc(placed, 1)
            nc.scalar.activation(wdT[0:HIDDEN - 2 * P, 2, :], pt[2][0:HIDDEN - 2 * P, 2 * P:rows], ACT.Copy).then_inc(placed, 1)

            def silus(g):
                for t in range(g * BT, (g + 1) * BT):
                    act.wait_ge(gu_done, t + 1)
                    nc.scalar.activation(silu[t % 2][:, :], gate[t % 2][:, :], ACT.Silu).then_inc(silu_done, 1)

            silus(0)
            for g in range(GROUPS):
                signs(3 + g)
                if g + 1 < GROUPS:
                    silus(g + 1)
                for k, (_, n) in enumerate(chunk):
                    act.wait_ge(h_turned, 3 * g + k + 1)
                    if g:
                        act.wait_ge(down_done, g)
                    nc.scalar.activation(hqT[0:n, k, :], pt[k][0:n, :], ACT.Copy).then_inc(h_placed, 1)

        @block.tensor
        def _(pe):
            pe.wait_ge(rounded, 1)
            for t in range(TILES):
                g, k = divmod(t, BT)
                ins = nc.tensor.transpose((pt + [po])[g][:, k * P:(k + 1) * P], xq[:, t, :], c.ident[:, :])
                if k == BT - 1:
                    ins.then_inc(turned, 1)
            pe.wait_ge(rounded, 2)
            for i in range(2):
                pe.wait_ge(placed, i + 1)
                for k in range(3):
                    ins = nc.tensor.transpose(pt[i][:, k * P:(k + 1) * P], w_rows[:, 3 * i + k, :], c.ident[:, :])
                ins.then_inc(turned, 1)
            pe.wait_ge(rounded, 3)
            pe.wait_ge(placed, 3)
            for k, (at, n) in enumerate(chunk):
                ins = nc.tensor.transpose(pt[2][0:n, k * P:(k + 1) * P], wd_rows[:, at:at + n], c.ident[:, :])
            ins.then_inc(turned, 1)
            pe.wait_ge(placed, GROUPS + 4)

            def gate_ups(g):
                for t in range(g * BT, (g + 1) * BT):
                    if t >= 2:
                        pe.wait_ge(prod_done, t - 1)
                    tile = xqT[:, t * P:(t + 1) * P]
                    nc.tensor.matmul(gate[t % 2][:, :], tile, wT[:, 0, 0:HIDDEN], start=True, stop=True)
                    nc.tensor.matmul(up[t % 2][:, :], tile, wT[:, 1, 0:HIDDEN], start=True, stop=True).then_inc(gu_done, 1)

            gate_ups(0)
            for g in range(GROUPS):
                if g + 1 < GROUPS:
                    gate_ups(g + 1)
                pe.wait_ge(rounded, 3 + g + 1)
                for k, (at, n) in enumerate(chunk):
                    if g:
                        pe.wait_ge(h_placed, 3 * (g - 1) + k + 1)
                    for t in range(BT):
                        ins = nc.tensor.transpose(pt[k][0:n, t * P:(t + 1) * P], hq[g % 2][:, t, at:at + n], c.ident[:, :])
                    ins.then_inc(h_turned, 1)
                pe.wait_ge(h_placed, 3 * (g + 1))
                if g:
                    pe.wait_ge(added, g)
                for k, (at, n) in enumerate(chunk):
                    ins = nc.tensor.matmul(po[:, :], wdT[0:n, k, :], hqT[0:n, k, :], start=k == 0, stop=k == 2)
                ins.then_inc(down_done, 1)



def build(nc, dram):
    with ExitStack() as ctx:
        c = Chip(nc, ctx, dram)

        def share_rows(tag, chunks):
            return nc.dram_tensor(f"{tag}_shares", (2 * chunks, TOK), F32, kind="Internal").ap()

        def experts(layer, rows):
            stage_experts(c, f"e{layer}", dram[f"e{layer}_w"], rows, dram[f"e{layer}_w"].shape[0])

        stage_load(c)

        stage_norm(c, "n0")
        rows = share_rows("e0", dram["e0_w"].shape[0])
        stage_conv_branch(c)
        stage_route_grouped(c, rows)
        experts(0, rows)
        stage_add(c, "s0", also_xn=True)
        c.clear_semaphores()

        stage_norm(c, "n1")
        h = Heads(nc, "a1", 64, 0)
        stage_project_v(c, h, dram["a1_w_v"])
        stage_attend(c, h, 64 ** -0.5, dram["a1_w_qk"])
        stage_attention_out(c, h, dram["a1_w_out"])
        stage_fp4_ffn(c, dram["f1_w_gate_up"], dram["f1_w_down"])
        stage_add(c, "s1", also_xn=False)
        c.clear_semaphores()

        stage_norm(c, "n2")
        h = Heads(nc, "a2", 8, 1)
        stage_project_small(c, h)
        stage_attend(c, h, 4 ** -0.5)
        stage_attention_out(c, h, dram["a2_w_out"])
        rows = share_rows("e2", dram["e2_w"].shape[0])
        stage_route_top2(c, "r2", True, 1, rows)
        experts(2, rows)
        stage_add(c, "s2", also_xn=False)
        c.clear_semaphores()

        stage_norm(c, "n3")
        h = Heads(nc, "a3", 8, 0)
        stage_project_small(c, h)
        stage_attend(c, h, 8 ** -0.5)
        stage_attention_out(c, h, dram["a3_w_out"])
        rows = share_rows("e3", dram["e3_w"].shape[0])
        stage_route_top2(c, "r3", False, 4, rows)
        experts(3, rows)
        stage_add(c, "s3", also_xn=False)

        stage_store(c)


def laid_out(i):
    f = np.float32
    a = {"x": i["L0_attn_x"].reshape(TOK, P)}

    a["ident"] = np.eye(P, dtype=f)
    a["ones"] = np.ones((4, TOK), f)
    a["lower"] = np.tril(np.ones((8, 8), f), -1)[None]
    a["mask_above"] = np.triu(np.full((P, P), MASKED, f), 1)
    a["mask_below"] = np.tril(np.full((P, P), MASKED, f), -1)
    pos = np.arange(SEQ, dtype=f)
    freq = (1.0 / 10000.0 ** (np.arange(0, 4, 2, dtype=f) / 4)).astype(f)
    angle = pos[None, :] * freq[:, None]
    cos, sin = np.ones((HEADS, 8, SEQ), f), np.zeros((HEADS, 8, SEQ), f)
    cos[:, 4:6] = cos[:, 6:8] = np.cos(angle)
    sin[:, 4:6], sin[:, 6:8] = -np.sin(angle), np.sin(angle)
    a["cos"], a["sin"] = cos.reshape(P, SEQ), sin.reshape(P, SEQ)

    for n in range(2):
        taps = i[f"L0_attn_k{n}"][0].T[::-1]
        a[f"k{n}T"] = np.concatenate([np.zeros((CBLK, P), f), taps, np.zeros((CBLK - 1, P), f)])
    a["L0_W_in"], a["L0_W_out"] = i["L0_attn_W_in"], i["L0_attn_W_out"]
    a["L0_b_in"] = i["L0_attn_b_in"][None]
    a["L0_cols"] = np.stack([i["L0_attn_gamma"], i["L0_attn_beta"], i["L0_attn_b_out"]], 1)
    a["r0_w"], a["r0_b"] = i["L0_ffn_router_w"].T, i["L0_ffn_e_bias"][None]

    def pairs(w):
        return w.reshape(-1, 2, P, P // 2).transpose(0, 2, 1, 3).reshape(-1, P, P)

    def joined(gate, up, down):
        return np.concatenate([gate, up, down], 2)

    a["e0_w"] = np.concatenate([
        joined(pairs(i["L0_ffn_Wg"]), pairs(i["L0_ffn_Wu"]), i["L0_ffn_Wd"].reshape(-1, P, P)),
        joined(i["L0_ffn_SWg"][None], i["L0_ffn_SWu"][None], i["L0_ffn_SWd"][None])])

    def twice(w):
        w = w.reshape(P, HEADS, -1).transpose(1, 0, 2)
        return [w, w]

    a["a1_w_qk"] = np.concatenate(twice(i["L1_attn_Wq"]) + twice(i["L1_attn_Wk"]), 2)
    a["a1_w_v"], a["a1_w_out"] = i["L1_attn_Wv"], i["L1_attn_Wo"]
    pad = np.zeros((3 * P - HIDDEN, P), f)
    a["f1_w_gate_up"] = np.concatenate([i["L1_ffn_w_gate"], pad, i["L1_ffn_w_up"], pad])
    a["f1_w_down"] = i["L1_ffn_w_down"]

    def heads(sem, geo):
        return np.concatenate([sem.reshape(-1, HEADS, 4), geo.reshape(-1, HEADS, 4)], 2).reshape(-1, P)

    def partner(geo):
        return geo.reshape(-1, HEADS, 2, 2)[:, :, ::-1].reshape(-1, HEADS * 4)

    g = {n: i[f"L2_attn_{n}"] for n in ("wq_sem", "wk_sem", "wq_geo", "wk_geo", "k_sem_null", "k_geo_null")}
    for n in ("wq", "wk"):
        a[f"a2_{n}"] = heads(g[f"{n}_sem"], g[f"{n}_geo"])
        a[f"a2_{n}_turn"] = heads(g[f"{n}_sem"], partner(g[f"{n}_geo"]))
    a["a2_wv"], a["a2_w_out"] = i["L2_attn_wv"], i["L2_attn_wo"]
    a["a2_k_null"] = heads(g["k_sem_null"][None], g["k_geo_null"][None]).T
    v_null = np.zeros((1, HEADS, 32), f)
    v_null[0, :, 0:8] = i["L2_attn_v_null"].reshape(HEADS, 8)
    v_null[0, :, 8] = 1.0
    a["a2_v_null"] = v_null
    a["r2_w"], a["r2_b"] = i["L2_ffn_router_w"], i["L2_ffn_router_b"][None]
    a["e2_w"] = np.concatenate([
        joined(pairs(i[f"L2_ffn_{n}_w1"]), pairs(i[f"L2_ffn_{n}_w3"]), i[f"L2_ffn_{n}_w2"].reshape(-1, P, P))
        for n in ("routed", "shared")])

    for n in "qkv":
        a[f"a3_w{n}"] = i[f"L3_attn_W_{n.upper()}"]
    a["a3_w_out"] = i["L3_attn_W_o"]
    a["r3_w"], a["r3_b"] = i["L3_ffn_router_w"].T, i["L3_ffn_routing_bias"][None]

    def hidden_rows(w):
        return w.reshape(-1, P, P).transpose(0, 2, 1)

    def down_columns(w):
        return w.reshape(-1, P, 2, P).transpose(0, 2, 3, 1).reshape(-1, P, P)

    a["e3_w"] = np.concatenate([
        joined(hidden_rows(i["L3_ffn_wg"]), hidden_rows(i["L3_ffn_wu"]), down_columns(i["L3_ffn_wd"])),
        joined(hidden_rows(i["L3_ffn_sg_w"]), hidden_rows(i["L3_ffn_su_w"]), down_columns(i["L3_ffn_sd_w"]))])
    return {n: np.ascontiguousarray(v) for n, v in a.items()}


def kernel(**inputs):
    import concourse.bacc as bacc
    from concourse.bass_utils import run_bass_kernel_spmd

    nc = bacc.Bacc("TRN2", target_bir_lowering=False, num_devices=1)
    arrays = laid_out({n: np.asarray(v) for n, v in inputs.items()})
    dram = {n: nc.dram_tensor(f"in_{n}", v.shape, mybir.dt.from_np(v.dtype), kind="ExternalInput").ap()
            for n, v in arrays.items()}
    dram["out"] = nc.dram_tensor("out", (TOK, P), F32, kind="ExternalOutput").ap()
    build(nc, dram)
    result = run_bass_kernel_spmd(nc, [{f"in_{n}": v for n, v in arrays.items()}], core_ids=[0])
    return result.results[0]["out"].reshape(BATCH, SEQ, P)
```
